# Optimizing a Trainium2 kernel written in Bass

```python
import numpy as np
import jax
import jax.numpy as jnp

def _softmax(x, axis=-1):
    return jax.nn.softmax(x, axis=axis)

def _gelu(x):
    return jax.nn.gelu(x, approximate=True)

def _silu(x):
    return jax.nn.silu(x)

def _sigmoid(x):
    return jax.nn.sigmoid(x)

def _layernorm(x, axis=-1, eps=1e-05):
    m = jnp.mean(x, axis=axis, keepdims=True)
    v = jnp.var(x, axis=axis, keepdims=True)
    return (x - m) / jnp.sqrt(v + eps)

def _scatter_add(tgt, idx, src, axis=0):
    return tgt.at[idx].add(src)

def _segment_sum(src, seg, n):
    return jax.ops.segment_sum(src, seg, n)
kernel_name = 'mk_decoder_preln_d1_seqx_r4_dd1555'

def setup_inputs(seed: int=0):
    np.random.seed(seed)
    _w = jnp.asarray

    def _rec_inputs():
        import jax
        import jax.numpy as jnp
        _rk = jax.random.key(seed)
        x = -0.0002928 + 1 * jax.random.normal(jax.random.fold_in(_rk, 1), (16, 256, 256), jnp.float32)
        _lenS = 256 - jax.random.randint(jax.random.fold_in(_rk, 7), (16,), 0, max(1, 256 // 4) + 1, jnp.int32)
        _lenS2 = 120 - jax.random.randint(jax.random.fold_in(_rk, 8), (16,), 0, max(1, 120 // 4) + 1, jnp.int32)
        _ctx_1024P = jax.random.normal(jax.random.fold_in(_rk, 11), (16, 16, 256), jnp.float32)
        _ctx_1024c = jax.random.dirichlet(jax.random.fold_in(_rk, 511), 0.3 * jnp.ones((16,), jnp.float32), (16, 120))
        _ctx_1024t = jnp.einsum('bsk,bkd->bsd', _ctx_1024c, _ctx_1024P)
        _ctx_1024t = _ctx_1024t * jax.lax.rsqrt(jnp.mean(jnp.square(_ctx_1024t)) + 1e-12) * 0.953939
        ctx_1024 = -1.39393e-06 + 0.999914 * (_ctx_1024t + 0.3 * jax.random.normal(jax.random.fold_in(_rk, 611), (16, 120, 256), jnp.float32))
        _validS = jnp.arange(256)[None, :] < _lenS[:, None]
        _validS2 = jnp.arange(120)[None, :] < _lenS2[:, None]
        _causal = jnp.tril(jnp.ones((256, 256), dtype=bool))
        mask_Bx1xSxS2_ik1 = jnp.where(jnp.broadcast_to(_validS2[:, None, None, :], (16, 1, 256, 120)), 1, 0).astype(jnp.int32)
        return (x, ctx_1024, mask_Bx1xSxS2_ik1)
    x, ctx_1024, mask_Bx1xSxS2_ik1 = _rec_inputs()

    def _L0_attn_setup():
        import jax, jax.numpy as jnp
        import numpy as np
        H = 16
        WIN = 128
        G = 64
        MAXPOS = 2048
        key = jax.random.key(seed)
        ks = jax.random.split(key, 9)
        B, S, D = (4, 1024, 256)
        s = 1.0 / np.sqrt(D)
        return {'x': jax.random.normal(ks[0], (B, S, D), jnp.float32), 'pos_emb': jax.random.normal(ks[1], (MAXPOS, D), jnp.float32) * 0.02, 'global_memory': jax.random.normal(ks[2], (1, G, D), jnp.float32), 'conv_w': jax.random.normal(ks[3], (D, D, 4), jnp.float32) * s, 'conv_b': jax.random.normal(ks[4], (D,), jnp.float32) * 0.01, 'gate_w': jax.random.normal(ks[5], (2 * D, D), jnp.float32) * s, 'gate_b': jnp.zeros((D,), jnp.float32), 'out_w': jax.random.normal(ks[6], (D, D), jnp.float32) * s, 'out_b': jnp.zeros((D,), jnp.float32)}
    _L0_attn_all = _L0_attn_setup()
    _L0_attn_in = {k: v for k, v in _L0_attn_all.items() if k in ('pos_emb', 'global_memory', 'conv_w', 'conv_b', 'gate_w', 'gate_b', 'out_w', 'out_b')}
    del _L0_attn_all

    def _L0_xattn_setup():
        import jax, jax.numpy as jnp
        import numpy as np
        B, S, D, H = (2, 512, 256, 16)
        DK = D // H
        key = jax.random.key(seed)
        ks = jax.random.split(key, 8)
        inp = {'Q': jax.random.normal(ks[0], (B, S, D), dtype=jnp.float32), 'K': jax.random.normal(ks[1], (B, S, D), dtype=jnp.float32), 'V': jax.random.normal(ks[2], (B, S, D), dtype=jnp.float32), 'mask': jax.random.randint(ks[3], (B, 1, S, S), 0, 2, dtype=jnp.int32), 'Wq': jax.random.normal(ks[4], (D, D), dtype=jnp.float32) / np.sqrt(D), 'Wk': jax.random.normal(ks[5], (D, D), dtype=jnp.float32) / np.sqrt(D), 'Wv': jax.random.normal(ks[6], (D, D), dtype=jnp.float32) / np.sqrt(D), 'Wo': jax.random.normal(ks[7], (D, D), dtype=jnp.float32) / np.sqrt(D)}
        return inp
    _L0_xattn_all = _L0_xattn_setup()
    _L0_xattn_in = {k: v for k, v in _L0_xattn_all.items() if k in ('Wq', 'Wk', 'Wv', 'Wo')}
    del _L0_xattn_all

    def _L0_ffn_setup():
        import jax, jax.numpy as jnp
        import numpy as np
        NUM_EXPERTS = 8
        TOP_K = 2
        DIM = 256
        HIDDEN = 512
        BATCH, SEQ = (4, 512)
        key = jax.random.key(seed)
        k_x, k_r, k1, k2, k3 = jax.random.split(key, 5)
        scale = 0.02
        return {'x': jax.random.normal(k_x, (BATCH, SEQ, DIM), dtype=jnp.float32), 'router_w': jax.random.normal(k_r, (NUM_EXPERTS, DIM), dtype=jnp.float32) * scale, 'w1': jax.random.normal(k1, (NUM_EXPERTS, HIDDEN, DIM), dtype=jnp.float32) * scale, 'w2': jax.random.normal(k2, (NUM_EXPERTS, DIM, HIDDEN), dtype=jnp.float32) * scale, 'w3': jax.random.normal(k3, (NUM_EXPERTS, HIDDEN, DIM), dtype=jnp.float32) * scale}
    _L0_ffn_all = _L0_ffn_setup()
    _L0_ffn_in = {k: v for k, v in _L0_ffn_all.items() if k in ('router_w', 'w1', 'w2', 'w3')}
    del _L0_ffn_all
    return {'x': x, 'ctx_1024': ctx_1024, 'mask_Bx1xSxS2_ik1': mask_Bx1xSxS2_ik1, 'L0_attn_pos_emb': _L0_attn_in['pos_emb'], 'L0_attn_global_memory': _L0_attn_in['global_memory'], 'L0_attn_conv_w': _L0_attn_in['conv_w'], 'L0_attn_conv_b': _L0_attn_in['conv_b'], 'L0_attn_gate_w': _L0_attn_in['gate_w'], 'L0_attn_gate_b': _L0_attn_in['gate_b'], 'L0_attn_out_w': _L0_attn_in['out_w'], 'L0_attn_out_b': _L0_attn_in['out_b'], 'L0_xattn_Wq': _L0_xattn_in['Wq'], 'L0_xattn_Wk': _L0_xattn_in['Wk'], 'L0_xattn_Wv': _L0_xattn_in['Wv'], 'L0_xattn_Wo': _L0_xattn_in['Wo'], 'L0_ffn_router_w': _L0_ffn_in['router_w'], 'L0_ffn_w1': _L0_ffn_in['w1'], 'L0_ffn_w2': _L0_ffn_in['w2'], 'L0_ffn_w3': _L0_ffn_in['w3']}

def reference(x, ctx_1024, mask_Bx1xSxS2_ik1, L0_attn_pos_emb, L0_attn_global_memory, L0_attn_conv_w, L0_attn_conv_b, L0_attn_gate_w, L0_attn_gate_b, L0_attn_out_w, L0_attn_out_b, L0_xattn_Wq, L0_xattn_Wk, L0_xattn_Wv, L0_xattn_Wo, L0_ffn_router_w, L0_ffn_w1, L0_ffn_w2, L0_ffn_w3):
    import jax
    import jax.numpy as jnp

    def _L0_attn_ref(x, pos_emb, global_memory, conv_w, conv_b, gate_w, gate_b, out_w, out_b):
        import jax, jax.numpy as jnp
        import numpy as np
        H = 16
        WIN = 128
        G = 64
        MAXPOS = 2048
        B, S, D = x.shape
        hd = D // H
        scale = 1.0 / np.sqrt(hd)
        x = x + pos_emb[:S][None]
        pad = -S % WIN
        xp = jnp.pad(x, ((0, 0), (0, pad), (0, 0))) if pad else x
        nW = xp.shape[1] // WIN
        w = xp.reshape(B, nW, WIN, H, hd)
        attn = jnp.einsum('bnqhd,bnkhd->bnhqk', w, w) * scale
        attn = jax.nn.softmax(attn, axis=-1)
        local = jnp.einsum('bnhqk,bnkhd->bnqhd', attn, w)
        local = local.reshape(B, nW * WIN, D)[:, :S]
        comp = jax.lax.conv_general_dilated(x.transpose(0, 2, 1), conv_w, window_strides=(4,), padding='VALID', dimension_numbers=('NCH', 'OIH', 'NCH')) + conv_b[None, :, None]
        comp = comp.transpose(0, 2, 1)[:, :G]
        gt = jnp.concatenate([comp, jnp.broadcast_to(global_memory, (B, G, D))], axis=1)
        gt = gt.reshape(B, 2 * G, H, hd)
        xm = x.reshape(B, S, H, hd)
        ga = jax.nn.softmax(jnp.einsum('bshd,bghd->bhsg', xm, gt) * scale, axis=-1)
        glob = jnp.einsum('bhsg,bghd->bshd', ga, gt).reshape(B, S, D)
        mix = jax.nn.sigmoid(jnp.concatenate([local, glob], axis=-1) @ gate_w + gate_b)
        out = mix * local + (1.0 - mix) * glob
        return out @ out_w + out_b

    def _L0_xattn_ref(Q, K, V, mask, Wq, Wk, Wv, Wo):
        import jax, jax.numpy as jnp
        import numpy as np
        B, S, D, H = (2, 512, 256, 16)
        DK = D // H
        b, s, d = Q.shape
        q = (Q @ Wq.T).reshape(b, s, H, DK).transpose(0, 2, 1, 3)
        k = (K @ Wk.T).reshape(b, -1, H, DK).transpose(0, 2, 1, 3)
        v = (V @ Wv.T).reshape(b, -1, H, DK).transpose(0, 2, 1, 3)
        score = jnp.einsum('bhqd,bhkd->bhqk', q, k) / jnp.sqrt(jnp.float32(DK))
        score = jnp.where(mask == 0, jnp.float32(1e-09), score)
        attn = jax.nn.softmax(score, axis=-1)
        out = jnp.einsum('bhqk,bhkd->bhqd', attn, v)
        out = out.transpose(0, 2, 1, 3).reshape(b, s, d)
        return out @ Wo.T

    def _L0_ffn_ref(x, router_w, w1, w2, w3):
        import jax, jax.numpy as jnp
        import numpy as np
        NUM_EXPERTS = 8
        TOP_K = 2
        DIM = 256
        HIDDEN = 512
        BATCH, SEQ = (4, 512)
        B, S, D = x.shape
        E = router_w.shape[0]
        xf = x.reshape(-1, D)
        logits = xf @ router_w.T
        probs = jax.nn.softmax(logits, axis=-1)
        top_p, top_i = jax.lax.top_k(probs, TOP_K)
        top_p = top_p / jnp.sum(top_p, axis=-1, keepdims=True)
        cw = jnp.sum(top_p[..., None] * jax.nn.one_hot(top_i, E, dtype=xf.dtype), axis=1)
        out = jnp.zeros_like(xf)
        for e in range(E):
            h = jax.nn.silu(xf @ w1[e].T) * (xf @ w3[e].T)
            out = out + cw[:, e:e + 1] * (h @ w2[e].T)
        return out.reshape(B, S, D)
    x = x + _L0_attn_ref(_layernorm(x, axis=-1), L0_attn_pos_emb, L0_attn_global_memory, L0_attn_conv_w, L0_attn_conv_b, L0_attn_gate_w, L0_attn_gate_b, L0_attn_out_w, L0_attn_out_b)
    x = x + _L0_xattn_ref(_layernorm(x, axis=-1), ctx_1024, ctx_1024, mask_Bx1xSxS2_ik1, L0_xattn_Wq, L0_xattn_Wk, L0_xattn_Wv, L0_xattn_Wo)
    x = x + _L0_ffn_ref(_layernorm(x, axis=-1), L0_ffn_router_w, L0_ffn_w1, L0_ffn_w2, L0_ffn_w3)
    return x

_drawn_inputs = setup_inputs


def setup_inputs(seed=0):
    import zlib

    import numpy as np

    out = dict(_drawn_inputs(seed))
    spreads = {'L0_attn_gate_b': (0.0, 0.667), 'L0_attn_out_b': (0.0, 0.1)}
    factors = {'L0_attn_pos_emb': 3.201,
     'L0_attn_conv_b': 8.0,
     'L0_ffn_router_w': 5.203,
     'L0_ffn_w1': 4.505,
     'L0_ffn_w2': 4.458,
     'L0_ffn_w3': 4.463}
    for name, (base, spread) in spreads.items():
        noise = np.random.default_rng([zlib.crc32(name.encode()), seed]).standard_normal(out[name].shape)
        drawn = base * np.exp(spread * noise) if base else spread * noise
        out[name] = jnp.asarray(drawn.astype(out[name].dtype))
    for name, factor in factors.items():
        out[name] = (out[name] * factor).astype(out[name].dtype)
    return out
```

```python
from contextlib import ExitStack

import numpy as np

import concourse.bass as bass
from concourse import mybir

F32 = mybir.dt.float32
BF16 = mybir.dt.bfloat16
I32 = mybir.dt.int32
U32 = mybir.dt.uint32
ALU = mybir.AluOpType
ACT = mybir.ActivationFunctionType
AX_X = mybir.AxisListType.X

P = 128
D = 256
DT = D // P
H = 16
HD = D // H
HU = H // DT
NB = 16
S = 256
NT = S // P
TILES = NB * NT
G = 64
CK = 4
KX = 120
E = 8
HID = 512
HT = HID // P
TOKENS = NB * S
TOP = 2
N_ST = (TOP * TOKENS + E * (P - 1)) // P
N_ST += N_ST % 2
ZERO_P = 96
ZERO_N = N_ST * P // (NB * ZERO_P)
EPS = 1e-5
SCALE = 1.0 / float(np.sqrt(HD))
Q_SLOTS = ((0, 3, 0), (1, 2, 0), (2, 1, 0))
K_SLOTS = ((0, 3, 1), (0, 2, 1), (0, 1, 0))
SLOTS = 6
KS = SLOTS * HD




class Row:

    def __init__(self, reg, off, par=None):
        self.reg, self.off = reg, off
        self.par = off % 2 if reg is None else par

    def plus(self, n):
        return Row(self.reg, self.off + n, (self.par + n) % 2)

    def lin(self, k, c=0):
        if self.reg is None:
            return k * self.off + c
        return self.reg * k + (k * self.off + c)


class Started:
    sem = None


def wait(eng, sem, value, apart=False):
    if isinstance(value, int):
        if value > 0:
            eng.wait_ge(sem, value)
        return
    if apart or eng.engine in (mybir.EngineType.Pool, mybir.EngineType.SP):
        value = eng.to_reg(value)
        eng.wait_ge(Started.sem, 1)
    eng.wait_ge(sem, value)


def build(nc, a):
    with ExitStack() as ctx:
        Program(nc, a, ctx).emit()


class Program:
    def __init__(self, nc, a, ctx):
        self.nc, self.a, self.ctx = nc, a, ctx
        self.sems = {}

    def sem(self, name):
        if name not in self.sems:
            self.sems[name] = self.ctx.enter_context(self.nc.semaphore(name))
        return self.sems[name]

    def sb(self, name, shape, dt=F32, ctx=None):
        return (ctx or self.ctx).enter_context(self.nc.sbuf_tensor(name, shape, dt))

    def emit(self):
        nc, a, ctx = self.nc, self.a, self.ctx
        self.xres = self.sb("xres", [P, TILES, D])
        self.w1s = self.sb("w1s", [P, E * DT, HID])
        self.ident = self.sb("ident", [P, P])
        self.neg_ident = self.sb("neg_ident", [P, P], BF16)
        self.eps = self.sb("eps", [P, 4])
        Started.sem = self.sem("started")
        self.rows_dram = nc.dram_tensor("x_rows", [N_ST * P, D], F32, kind="Internal").ap()
        self.S = [ctx.enter_context(nc.psum_tensor(f"ps_scores{i}", [P, HU, P], F32)) for i in range(2)]
        self.T = [ctx.enter_context(nc.psum_tensor(f"ps_turn{i}", [P, 4, P], F32)) for i in range(2)]
        self.O = ctx.enter_context(nc.psum_tensor("ps_out", [P, 4, P], F32))
        self.M = ctx.enter_context(nc.psum_tensor("ps_misc", [P, 512], F32))
        with ExitStack() as c1:
            self_attention(self, c1)
        self.w3s = self.sb("w3s", [P, E * DT, HID])
        with ExitStack() as c2:
            cross_attention(self, c2)
        with ExitStack() as c3:
            experts(self, c3)


class Units:

    def __init__(self, p, ctx, tag):
        self.p, self.nc = p, p.nc
        sem = lambda n: p.sem(f"{tag}_{n}")
        self.s_scores = sem("scores")
        self.s_masked = sem("masked")
        self.s_max = sem("max")
        self.s_negm = sem("negm")
        self.s_exp = sem("exp")
        self.s_turn = sem("turn")
        self.s_ev = [sem("ev0"), sem("ev1")]
        self.s_pv = sem("pv")
        self.s_out = sem("oev")
        self.probs = [p.sb(f"{tag}_probs{i}", [P, HU, P], ctx=ctx) for i in range(2)]
        self.probsT = [p.sb(f"{tag}_probsT{i}", [P, HU, P], ctx=ctx) for i in range(2)]
        self.rowmax = [p.sb(f"{tag}_rowmax{i}", [P, HU], BF16, ctx=ctx) for i in range(2)]
        self.outT = [p.sb(f"{tag}_outT{i}", [P, 4, P], ctx=ctx) for i in range(2)]

    def scores(self, pe, U, up, q, k, nk):
        wait(pe, self.s_exp, U - 1)
        for h in range(HU):
            mm = pe.matmul(self.p.S[up][:, h, 0:nk], q(h), k(h), start=(h % 4 == 0), stop=False,
                           skip_group_check=True)
        mm.then_inc(self.s_scores, 1)

    def maxima(self, dve, U, up, nk, masked=None):
        sc = self.p.S[up][:, :, 0:nk]
        wait(dve, self.s_scores, U + 1, apart=masked is not None)
        if masked is not None:
            mask, value = masked
            dve.copy_predicated(sc, mask.unsqueeze(1).broadcast_to((P, HU, nk)),
                                value.unsqueeze(2).broadcast_to((P, HU, nk))).then_inc(self.s_masked, 1)
            wait(dve, self.s_masked, U + 1)
        dve.tensor_reduce(self.rowmax[up][:], sc, AX_X, ALU.max).then_inc(self.s_max, 1)

    def subtract_max(self, pe, U, up, nk):
        wait(pe, self.s_max, U + 1)
        for g in range(2):
            mm = pe.matmul(self.p.S[up][:, 4 * g:4 * g + 4, 0:nk], self.p.neg_ident[:],
                           self.rowmax[up][:, 4 * g:4 * g + 4].unsqueeze(2).broadcast_to((P, 4, nk)),
                           start=False, stop=True, skip_group_check=True)
        mm.then_inc(self.s_negm, 1)

    def exponentials(self, act, U, up, nk):
        wait(act, self.s_negm, U + 1)
        wait(act, self.s_turn, 2 * (U - 1))
        act.activation(self.probs[up][:, :, 0:nk], self.p.S[up][:, :, 0:nk], ACT.Exp,
                       scale=SCALE).then_inc(self.s_exp, 1)

    def turn(self, pe, U, up, nk):
        wait(pe, self.s_exp, U + 1)
        for g in range(2):
            wait(pe, self.s_ev[g], U)
            for h in range(4):
                mm = pe.transpose(self.p.T[g][0:nk, h, :], self.probs[up][:, 4 * g + h, 0:nk], self.p.ident[:])
            mm.then_inc(self.s_turn, 1)

    def evacuate(self, eng, g, U, up, nk):
        wait(eng, self.s_turn, 2 * U + 1 + g)
        wait(eng, self.s_pv, U - 1)
        dst, src = self.probsT[up][0:nk, 4 * g:4 * g + 4, :], self.p.T[g][0:nk, :, :]
        ins = eng.copy(dst, src) if g == 0 else eng.tensor_copy(dst, src)
        ins.then_inc(self.s_ev[g], 1)

    def values(self, pe, U, up, Oi, ft, v, nk):
        wait(pe, self.s_ev[0], U + 1)
        wait(pe, self.s_ev[1], U + 1)
        if Oi is not None:
            wait(pe, self.s_out, Oi)
        for h in range(HU):
            j = h % 4
            mm = pe.matmul(self.p.O[32 * j:32 * j + 32, 2 * ft + h // 4, :], v(h),
                           self.probsT[up][0:nk, h, :], start=True, stop=True,
                           tile_position=(0, 32 * j), skip_group_check=True)
        mm.then_inc(self.s_pv, 1)

    def out_copy(self, act, U, Oi, op, s_back):
        wait(act, self.s_pv, U + 1)
        wait(act, s_back, Oi - 1)
        act.copy(self.outT[op][:], self.p.O[:]).then_inc(self.s_out, 1)


def rows_of(e, n_rows, prologue, row, epilogue):
    prologue(e)
    row(e, Row(None, 0), True, False)
    with e.eng.Fori(1, n_rows - 3, 2) as r:
        row(e, Row(r, 0, 1), False, False)
        row(e, Row(r, 1, 0), False, False)
    for n in range(n_rows - 3, n_rows):
        row(e, Row(None, n), False, n == n_rows - 1)
    epilogue(e, Row(None, n_rows))


class Walker:

    def __init__(self, kind, eng):
        self.kind, self.eng, self.free = kind, eng, []


class Stages:

    def __init__(self, p, tag):
        self.p, self.tag = p, tag

    def written(self, name):
        return self.p.sem(f"{self.tag}_{name}_mm")

    def read(self, name):
        return self.p.sem(f"{self.tag}_{name}_rd")

    def run(self, e, name, index, needs, produce, reader, consume):
        if e.kind == "pe":
            for sem, value in e.free:
                wait(e.eng, sem, value, apart=True)
            for sem, value in needs:
                wait(e.eng, sem, value, apart=True)
            produce(e.eng).then_inc(self.written(name), 1)
        if e.kind == reader:
            wait(e.eng, self.written(name), index + 1)
            consume(e.eng).then_inc(self.read(name), 1)
        e.free = [(self.read(name), index + 1)]


def on_engines(nc, walk, before=None):
    with nc.Block() as block:
        @block.tensor
        def _(eng):
            walk(Walker("pe", eng))

        @block.scalar
        def _(eng):
            walk(Walker("act", eng))

        @block.vector
        def _(eng):
            walk(Walker("dve", eng))

        @block.gpsimd
        def _(eng):
            walk(Walker("pool", eng))

        @block.sync
        def _(eng):
            walk(Walker("sp", eng))


def split_rest(pool, first, whole, rest, second, third, sem, count):
    pool.tensor_tensor(rest, whole, first, ALU.subtract).then_inc(sem, 1)
    wait(pool, sem, count + 1)
    pool.tensor_copy(second, rest).then_inc(sem, 1)
    wait(pool, sem, count + 2)
    pool.tensor_tensor(third, rest, second, ALU.subtract).then_inc(sem, 1)


def load_stack(sp, stack, scratch, slots, sem):
    row = 0
    for part, n, step in slots:
        n_rows = n * HD
        for s in range(n):
            src = scratch[part + s * step].rearrange("(h d) t -> d h t", d=HD)
            sp.dma_start(stack[row + s * HD:row + (s + 1) * HD, :, :], src).then_inc(sem, 16)
        row += n_rows


def self_attention(p, ctx):
    nc, a = p.nc, p.a
    sb = lambda n, s, dt=F32: p.sb(n, s, dt, ctx)
    u = Units(p, ctx, "sa")
    st = Stages(p, "sa")
    sem = p.sem
    UPR = 2 * DT * NT

    pos = sb("pos", [P, NT, D])
    conv_w = sb("conv_w", [P, DT, CK, D])
    conv_b = sb("conv_b", [G, D])
    gate_w = sb("gate_w", [P, 2 * DT, D])
    gate_b = sb("gate_b", [P, D])
    out_w = sb("out_w", [P, DT, D])
    out_b = sb("out_b", [P, NT, D])
    memory = sb("memory", [P, D])
    w = [sb(f"w{i}", [P, NT, D]) for i in range(2)]
    wT = [sb(f"wT{i}", [P, DT, S]) for i in range(2)]
    wp = [sb(f"wp{i}", [P, 3, DT, S], BF16) for i in range(2)]
    rest = sb("rest", [P, DT, S])
    gT = sb("gT", [P, DT, P])
    gp = sb("gp", [P, 3, DT, P], BF16)
    grest = sb("grest", [P, DT, P])
    qs = [sb(f"qs{i}", [KS, H, S], BF16) for i in range(2)]
    ks = [sb(f"ks{i}", [KS, H, S], BF16) for i in range(2)]
    gs = [sb(f"gs{i}", [KS, H, P], BF16) for i in range(2)]
    gn = sb("gn", [G, D])
    vl = [sb(f"vl{i}", [P, NT, H, 2 * HD]) for i in range(2)]
    vg = [sb(f"vg{i}", [P, H, 2 * HD]) for i in range(2)]
    stats = sb("stats", [P, NT, 6])
    mv = sb("mv", [P, NT, 2])
    rstd = sb("rstd", [P, NT, 1])
    rec = sb("rec", [P, H, 1])
    att = [[sb(f"att{i}{j}", [P, D]) for j in range(2)] for i in range(NT)]
    attT = sb("attT", [P, 2 * DT, P])
    z = sb("z", [P, D])
    ez = sb("ez", [P, D])
    diff = sb("diff", [P, D])
    mix = sb("mix", [P, D])
    mixT = sb("mixT", [P, DT, P])
    w_scr = [nc.dram_tensor(f"w_scr{i}", [3, D, S], BF16, kind="Internal").ap() for i in range(2)]
    g_scr = [nc.dram_tensor(f"g_scr{i}", [3, D, P], BF16, kind="Internal").ap() for i in range(2)]
    x_t = a["x"].rearrange("b (n p) d -> p (b n) d", p=P)
    w1_t = a["w1T"].rearrange("e (k p) h -> p (e k) h", p=P)

    def consts(e):
        if e.kind == "sp":
            loads = [(p.ident[:], a["ident"]), (pos[:], a["pos_emb"][0:S].rearrange("(n p) d -> p n d", p=P)),
                     (conv_w[:], a["conv_w"].rearrange("(k p) t o -> p k t o", p=P)),
                     (conv_b[:], a["conv_b"].unsqueeze(0).broadcast_to((G, D))),
                     (gate_w[:], a["gate_w"].rearrange("(k p) o -> p k o", p=P)),
                     (gate_b[:], a["gate_b"].unsqueeze(0).broadcast_to((P, D))),
                     (out_w[:], a["out_w"].rearrange("(k p) o -> p k o", p=P)),
                     (out_b[:, 0, :], a["out_b"].unsqueeze(0).broadcast_to((P, D))),
                     (out_b[:, 1, :], a["out_b"].unsqueeze(0).broadcast_to((P, D))),
                     (memory[G:P, :], a["global_memory"][0])]
            for dst, src in loads:
                e.eng.dma_start(dst, src).then_inc(sem("const"), 16)
            e.n_const = len(loads)
        N_CONST = 16 * 10
        if e.kind == "pool":
            e.eng.memset(p.eps[:, 1:2], 0.0).then_inc(Started.sem, 1)
            e.eng.memset(p.eps[:, 0:1], -0.5).then_inc(sem("set"), 1)
            e.eng.memset(memory[0:G, :], 0.0).then_inc(sem("set"), 1)
            for i in range(2):
                e.eng.memset(vl[i][:], 1.0).then_inc(sem("set"), 1)
                e.eng.memset(vg[i][:], 1.0).then_inc(sem("set"), 1)
            wait(e.eng, sem("const"), N_CONST)
            wait(e.eng, sem("set"), 6)
            for i in range(2):
                e.eng.tensor_copy(vg[i][G:P, :, 0:HD], memory[G:P, :].rearrange("p (h d) -> p h d", d=HD))\
                    .then_inc(sem("set"), 1)
        if e.kind == "dve":
            wait(e.eng, sem("const"), N_CONST)
            e.eng.tensor_scalar(p.neg_ident[:], p.ident[:], -1.0, None, ALU.mult).then_inc(sem("set_dve"), 1)
        if e.kind == "pe":
            wait(e.eng, sem("const"), N_CONST)
            wait(e.eng, sem("set_dve"), 1)
        if e.kind in ("act", "pe", "pool"):
            wait(e.eng, sem("set"), 8)
        if e.kind == "act":
            wait(e.eng, sem("const"), N_CONST)


        def turn(pe):
            for k in range(DT):
                mm = pe.transpose(p.M[:, k * P:(k + 1) * P], memory[:, k * P:(k + 1) * P], p.ident[:])
            return mm

        def copy(act):
            return act.copy(gT[:, :, G:P], p.M[:, 0:DT * P].rearrange("p (k g) -> p k g", k=DT)[:, :, G:P])
        st.run(e, "mem", 0, [], turn, "act", copy)


    def load_x(e, r):
        if e.kind == "sp":
            t = r.lin(NT)
            wait(e.eng, sem("x"), r.lin(32))
            e.eng.dma_start(p.xres[:, bass.ds(t, NT), :], x_t[:, bass.ds(t, NT), :]).then_inc(sem("x"), 16)
            e.eng.dma_start(p.w1s[:, bass.ds(r.lin(1), 1), :], w1_t[:, bass.ds(r.lin(1), 1), :])\
                .then_inc(sem("x"), 16)

    def normalise(e, r):
        if e.kind == "dve":
            wait(e.eng, sem("x"), r.lin(32, 32))
            for n in range(NT):
                e.eng.bn_stats(stats[:, n, :], p.xres[:, bass.ds(r.lin(NT, n), 1), :]).then_inc(sem("stats"), 1)
            wait(e.eng, sem("stats"), r.lin(NT, NT), apart=True)
            for n in range(NT):
                e.eng.bn_aggr(mv[:, n, :], stats[:, n, :]).then_inc(sem("mv"), 1)

    def apply_norm(e, r):
        i = r.par
        if e.kind == "dve":
            wait(e.eng, sem("rstd"), r.lin(2, 2))
            wait(e.eng, sem("wp1"), r.lin(1, -1))
            wait(e.eng, sem("vl"), r.lin(1, -1))
            for n in range(NT):
                e.eng.tensor_scalar(w[i][:, n, :].unsqueeze(1), p.xres[:, bass.ds(r.lin(NT, n), 1), :],
                                    mv[:, n, 0:1], rstd[:, n, :], ALU.subtract, ALU.mult)\
                    .then_inc(sem("norm"), 1)
        if e.kind == "pool":
            wait(e.eng, sem("mv"), r.lin(NT, NT))
            wait(e.eng, sem("norm"), r.lin(NT))
            e.eng.tensor_scalar(rstd[:], mv[:, :, 1:2], EPS, None, ALU.add).then_inc(sem("rstd"), 1)
            wait(e.eng, sem("rstd"), r.lin(2, 1))
            e.eng.tensor_tensor(rstd[:], rstd[:], p.eps[:, 0:1].unsqueeze(1).broadcast_to((P, NT, 1)),
                                ALU.pow).then_inc(sem("rstd"), 1)
            wait(e.eng, sem("norm"), r.lin(NT, NT))
            e.eng.tensor_tensor(w[i][:], w[i][:], pos[:], ALU.add).then_inc(sem("w"), 1)

    def turn_w(e, r):
        i = r.par

        def turn(pe):
            for k in range(DT):
                for n in range(NT):
                    mm = pe.transpose(p.M[:, k * S + n * P:k * S + (n + 1) * P], w[i][:, n, k * P:(k + 1) * P],
                                      p.ident[:])
            return mm

        def copy(act):
            wait(act, sem("ws"), r.lin(3, -3))
            return act.copy(wT[i][:], p.M[:].rearrange("p (k t) -> p k t", k=DT))
        st.run(e, "turn_w", r.lin(1), [(sem("w"), r.lin(1, 1))], turn, "act", copy)
        if e.kind == "act":
            wait(e.eng, st.read("turn_w"), r.lin(1, 1))
            wait(e.eng, sem("w_scr"), r.lin(16, -16))
            e.eng.copy(wp[i][:, 0, :, :], wT[i][:]).then_inc(sem("wp1"), 1)

    def parts_w(e, r):
        i = r.par
        if e.kind == "pool":
            wait(e.eng, sem("wp1"), r.lin(1, 1))
            split_rest(e.eng, wp[i][:, 0, :, :], wT[i][:], rest[:], wp[i][:, 1, :, :], wp[i][:, 2, :, :],
                       sem("ws"), r.lin(3))
            wait(e.eng, u.s_pv, r.lin(UPR, -UPR))
            e.eng.tensor_copy(vl[i][:, :, :, 0:HD], w[i][:].rearrange("p n (h d) -> p n h d", d=HD))\
                .then_inc(sem("vl"), 1)
            xr = p.xres[:, bass.ds(r.lin(NT), NT), :]
            e.eng.tensor_tensor(xr, xr, out_b[:], ALU.add).then_inc(sem("xb"), 1)
        if e.kind == "sp":
            wait(e.eng, sem("ws"), r.lin(3, 3))
            wait(e.eng, sem("stacks"), r.lin(192))
            e.eng.dma_start(w_scr[i].rearrange("c (k p) t -> p c k t", p=P), wp[i][:]).then_inc(sem("w_scr"), 16)
            wait(e.eng, sem("w_scr"), r.lin(16, 16))
            wait(e.eng, u.s_scores, r.lin(UPR, -UPR))
            load_stack(e.eng, qs[i], w_scr[i], Q_SLOTS, sem("stacks"))
            load_stack(e.eng, ks[i], w_scr[i], K_SLOTS, sem("stacks"))

    def compress(e, r):
        i = r.par

        def products(pe):
            taps = [(k, t) for k in range(DT) for t in range(CK)]
            for n, (k, t) in enumerate(taps):
                mm = pe.matmul(p.M[0:G, 0:D], wT[i][:, k, :].rearrange("p (g t) -> p t g", t=CK)[:, t, :],
                               conv_w[:, k, t, :], start=(n == 0), stop=(n == len(taps) - 1))
            return mm

        def add_bias(dve):
            wait(dve, st.written("turn_g"), r.lin(1))
            wait(dve, sem("vg"), r.lin(1))
            return dve.tensor_tensor(gn[:], p.M[0:G, 0:D], conv_b[:], ALU.add)
        st.run(e, "conv", r.lin(1), [(st.read("turn_w"), r.lin(1, 1))], products, "dve", add_bias)
        if e.kind == "pool":
            wait(e.eng, st.read("conv"), r.lin(1, 1))
            wait(e.eng, u.s_pv, r.lin(UPR, -UPR))
            e.eng.tensor_copy(vg[i][0:G, :, 0:HD], gn[:].rearrange("p (h d) -> p h d", d=HD))\
                .then_inc(sem("vg"), 1)

    def turn_g(e, r):
        i = r.par

        def turn(pe):
            for k in range(DT):
                mm = pe.transpose(p.M[:, k * G:(k + 1) * G], gn[:, k * P:(k + 1) * P],
                                  p.ident[0:G, 0:G])
            return mm

        def copy(act):
            wait(act, sem("gs"), r.lin(3))
            return act.copy(gT[:, :, 0:G], p.M[:, 0:DT * G].rearrange("p (k g) -> p k g", k=DT))
        st.run(e, "turn_g", r.lin(1), [(st.read("conv"), r.lin(1, 1))], turn, "act", copy)
        if e.kind == "act":
            wait(e.eng, st.read("turn_g"), r.lin(1, 1))
            wait(e.eng, sem("g_scr"), r.lin(16))
            e.eng.copy(gp[:, 0, :, :], gT[:]).then_inc(sem("gp1"), 1)

    def parts_g(e, r):
        i = r.par
        if e.kind == "pool":
            wait(e.eng, sem("gp1"), r.lin(1, 1))
            split_rest(e.eng, gp[:, 0, :, :], gT[:], grest[:], gp[:, 1, :, :], gp[:, 2, :, :],
                       sem("gs"), r.lin(3))
        if e.kind == "sp":
            wait(e.eng, sem("gs"), r.lin(3, 3))
            wait(e.eng, sem("g_stack"), r.lin(96))
            e.eng.dma_start(g_scr[i].rearrange("c (k p) t -> p c k t", p=P), gp[:]).then_inc(sem("g_scr"), 16)
            wait(e.eng, sem("g_scr"), r.lin(16, 16))
            load_stack(e.eng, gs[i], g_scr[i], K_SLOTS, sem("g_stack"))


    def unit(s):
        return s // 4, s // 2 % 2, s % 2

    def scores(e, r, s):
        n, kind, f = unit(s)
        i = r.par
        if e.kind == "pe":
            if s == 0:
                wait(e.eng, sem("stacks"), r.lin(192, 192))
            if s == 2:
                wait(e.eng, sem("g_stack"), r.lin(96, 96))
            q = lambda h: qs[i][:, f * HU + h, n * P:(n + 1) * P]
            k = (lambda h: gs[i][:, f * HU + h, :]) if kind else (lambda h: ks[i][:, f * HU + h, n * P:(n + 1) * P])
            u.scores(e.eng, r.lin(UPR, s), s % 2, q, k, P)
        if e.kind == "dve":
            u.maxima(e.eng, r.lin(UPR, s), s % 2, P)

    def values(e, r, s):
        n, kind, f = unit(s)
        i = r.par
        if s == 0:
            wait(e.eng, sem("vl"), r.lin(1, 1))
            wait(e.eng, sem("vg"), r.lin(1, 1))
        v = (lambda h: vg[i][:, f * HU + h, :]) if kind else (lambda h: vl[i][:, n, f * HU + h, :])
        u.values(e.eng, r.lin(UPR, s), s % 2, r.lin(UPR // 2, s // 2) if f == 0 else None, f, v, P)


    def turn_back(e, r, n, kind):
        o = r.lin(UPR // 2, 2 * n + kind)

        def turn(pe):
            for g in range(4):
                mm = pe.transpose(p.M[:, g * P:(g + 1) * P], u.outT[kind][:, g, :], p.ident[:])
            return mm

        def divide(dve):
            m = p.M[:].rearrange("p (h d) -> p h d", h=H)
            dve.reciprocal(rec[:], m[:, :, HD:HD + 1]).then_inc(sem("rec"), 1)
            wait(dve, sem("rec"), o + 1)
            if kind == 0:
                wait(dve, sem("mixed"), r.lin(NT, n - 1))
            return dve.tensor_tensor(att[n][kind][:].rearrange("p (h d) -> p h d", d=HD), m[:, :, 0:HD],
                                     rec[:].broadcast_to((P, H, HD)), ALU.mult)
        st.run(e, "back", o, [(u.s_out, o + 1)], turn, "dve", divide)

    def turn_att(e, r, n):
        t = r.lin(NT, n)

        def turn(pe):
            for kind in range(2):
                for k in range(DT):
                    c = (kind * DT + k) * P
                    mm = pe.transpose(p.M[:, c:c + P], att[n][kind][:, k * P:(k + 1) * P], p.ident[:])
            return mm

        def copy(act):
            return act.copy(attT[:], p.M[:].rearrange("p (k t) -> p k t", k=2 * DT))
        st.run(e, "att", t, [(st.read("back"), r.lin(UPR // 2, 2 * n + 2))], turn, "act", copy)

    def gate(e, r, n):
        t = r.lin(NT, n)

        def products(pe):
            for k in range(2 * DT):
                mm = pe.matmul(p.M[:, 0:D], attT[:, k, :], gate_w[:, k, :], start=(k == 0), stop=(k == 2 * DT - 1))
            return mm

        def add_bias(dve):
            wait(dve, sem("ez"), t)
            return dve.tensor_tensor(z[:], p.M[:, 0:D], gate_b[:], ALU.add)
        st.run(e, "gate", t, [(st.read("att"), t + 1)], products, "dve", add_bias)
        if e.kind == "act":
            wait(e.eng, st.read("gate"), t + 1)
            wait(e.eng, sem("e1"), 3 * t)
            e.eng.activation(ez[:], z[:], ACT.Exp, scale=-1.0).then_inc(sem("ez"), 1)
        if e.kind == "pool":
            wait(e.eng, st.read("back"), r.lin(UPR // 2, 2 * n + 2))
            wait(e.eng, sem("e1"), 3 * t)
            e.eng.tensor_tensor(diff[:], att[n][0][:], att[n][1][:], ALU.subtract).then_inc(sem("df"), 1)

    def mix_tile(e, r, n):
        t = r.lin(NT, n)
        if e.kind == "dve":
            wait(e.eng, sem("ez"), t + 1)
            e.eng.tensor_scalar(ez[:], ez[:], 1.0, None, ALU.add).then_inc(sem("e1"), 1)
            wait(e.eng, sem("e1"), 3 * t + 1)
            e.eng.reciprocal(ez[:], ez[:]).then_inc(sem("e1"), 1)
            wait(e.eng, sem("e1"), 3 * t + 2)
            wait(e.eng, sem("df"), t + 1)
            wait(e.eng, st.written("mixT"), t)
            e.eng.tensor_tensor(mix[:], diff[:], ez[:], ALU.mult).then_inc(sem("e1"), 1)
            wait(e.eng, sem("e1"), 3 * t + 3)
            e.eng.tensor_tensor(mix[:], mix[:], att[n][1][:], ALU.add).then_inc(sem("mixed"), 1)

    def turn_mix(e, r, n):
        t = r.lin(NT, n)

        def turn(pe):
            for k in range(DT):
                mm = pe.transpose(p.M[:, k * P:(k + 1) * P], mix[:, k * P:(k + 1) * P], p.ident[:])
            return mm

        def copy(act):
            return act.copy(mixT[:], p.M[:, 0:D].rearrange("p (k t) -> p k t", k=DT))
        st.run(e, "mixT", t, [(sem("mixed"), t + 1)], turn, "act", copy)

    def project(e, r, n):
        t = r.lin(NT, n)

        def products(pe):
            for k in range(DT):
                mm = pe.matmul(p.M[:, 0:D], mixT[:, k, :], out_w[:, k, :], start=(k == 0), stop=(k == DT - 1))
            return mm

        def residual(dve):
            wait(dve, sem("xb"), r.lin(1, 1))
            x = p.xres[:, bass.ds(t, 1), :]
            return dve.tensor_tensor(x, p.M[:, 0:D].unsqueeze(1), x, ALU.add)
        st.run(e, "proj", t, [(st.read("mixT"), t + 1)], products, "dve", residual)


    def prologue(e):
        consts(e)
        r0 = Row(None, 0)
        load_x(e, r0)
        load_x(e, r0.plus(1))
        normalise(e, r0)
        apply_norm(e, r0)
        turn_w(e, r0)
        parts_w(e, r0)
        compress(e, r0)
        turn_g(e, r0)
        parts_g(e, r0)
        scores(e, r0, 0)

    def slot(e, r, s, first, last, drain=False):
        U, nxt, prev = r.lin(UPR, s), r.plus(1), r.plus(-1)
        lag = lambda d: (r, s - d) if s >= d else (prev, s - d + UPR)
        exists = lambda d: s >= d or not first
        stages = {
            0: [lambda: None if first else turn_back(e, prev, 1, 0), lambda: None if first else gate(e, prev, 0)],
            1: [lambda: None if first else turn_mix(e, prev, 0), lambda: None if last or drain else turn_w(e, nxt)],
            2: [lambda: None if first else turn_back(e, prev, 1, 1), lambda: None if last or drain else compress(e, nxt)],
            3: [lambda: None if first else project(e, prev, 0), lambda: None if first else turn_att(e, prev, 1)],
            4: [lambda: None if last or drain else turn_g(e, nxt), lambda: None if first else gate(e, prev, 1),
                lambda: None if drain else turn_back(e, r, 0, 0)],
            5: [],
            6: [lambda: None if first else turn_mix(e, prev, 1), lambda: None if drain else turn_back(e, r, 0, 1)],
            7: [lambda: None if first else project(e, prev, 1), lambda: None if drain else turn_att(e, r, 0)],
        }[s] + [lambda: None] * 3
        more = not drain and not (last and s == UPR - 1)
        if s == 0 and not (last or drain):
            normalise(e, nxt)
        k = e.kind
        if more:
            scores(e, *((r, s + 1) if s + 1 < UPR else (nxt, 0)))
        if s == 1 and not first:
            mix_tile(e, prev, 0)
        if s == 6 and not first:
            mix_tile(e, prev, 1)
        if k == "pe":
            stages[0]()
            if not drain:
                u.subtract_max(e.eng, U, s % 2, P)
            if exists(1) and not (drain and s >= 1):
                u.turn(e.eng, *at_unit(lag(1)), P)
            stages[1]()
            if exists(2) and not (drain and s >= 2):
                values(e, *lag(2))
            stages[2]()
            return
        if s == 0 and not (last or drain):
            apply_norm(e, nxt)
        if k == "act" and not drain:
            u.exponentials(e.eng, U, s % 2, P)
        stages[0]()
        if exists(1) and not (drain and s >= 1) and k in ("act", "dve"):
            u.evacuate(e.eng, 0 if k == "act" else 1, *at_unit(lag(1)), P)
        stages[1]()
        if k == "act" and s % 2 == 1 and exists(2) and not (drain and s >= 2):
            rr, ss = lag(2)
            u.out_copy(e.eng, rr.lin(UPR, ss), rr.lin(UPR // 2, ss // 2), ss // 2 % 2, st.written("back"))
        stages[2]()
        if s == 2 and not (last or drain):
            parts_w(e, nxt)
        if s == 5 and not (last or drain):
            parts_g(e, nxt)

    def at_unit(x):
        r, s = x
        return r.lin(UPR, s), s % 2

    def row(e, r, first, last):
        if e.kind == "sp":
            if not last:
                if not (r.reg is None and r.off >= NB - 2):
                    load_x(e, r.plus(2))
                parts_w(e, r.plus(1))
                parts_g(e, r.plus(1))
            return
        e.free = [(st.read("turn_g"), 1) if first else (st.read("att"), r.lin(NT, -1))]
        for s in range(UPR):
            slot(e, r, s, first, last)

    def epilogue(e, r):
        if e.kind == "sp":
            return
        e.free = [(st.read("att"), r.lin(NT, -1))]
        for s in range(UPR):
            slot(e, r, s, False, True, drain=True)

    on_engines(nc, lambda e: rows_of(e, NB, prologue, row, epilogue))



def cross_attention(p, ctx):
    nc, a = p.nc, p.a
    sb = lambda n, s, dt=F32: p.sb(n, s, dt, ctx)
    u = Units(p, ctx, "xa")
    st = Stages(p, "xa")
    sem = lambda n: p.sem("xa_" + n)
    UPR = DT * NT

    wt = {n: sb(n + "_sb", [P, DT, D]) for n in ("WqT", "WkT", "WvT", "WoT")}
    masked_score = sb("masked_score", [P, 1])
    zeros = sb("zeros", [P, D])
    zero_t = p.rows_dram.rearrange("(r p n) d -> r p n d", r=NB, p=ZERO_P)
    xn = sb("xn", [P, NT, D])
    nT = sb("nT", [P, DT, S])
    ctx_n = [sb(f"ctx_n{i}", [KX, D]) for i in range(2)]
    cT = [sb(f"cT{i}", [P, DT, KX]) for i in range(2)]
    qT = sb("qT", [P, DT, S])
    qp = sb("qp", [P, 3, DT, S], BF16)
    kT = sb("kT", [P, DT, KX])
    kp = sb("kp", [P, 3, DT, KX], BF16)
    rest = sb("xrest", [P, DT, S])
    qs = [sb(f"xqs{i}", [KS, H, S], BF16) for i in range(2)]
    ks = [sb(f"xks{i}", [KS, H, KX], BF16) for i in range(2)]
    vx = [sb(f"vx{i}", [KX, H, 2 * HD]) for i in range(2)]
    mask = [sb(f"mask{i}", [P, NT, KX], I32) for i in range(2)]
    zero = [sb(f"zero{i}", [P, NT, KX], I32) for i in range(2)]
    stats = sb("xstats", [P, NT, 6])
    mv = sb("xmv", [P, NT, 2])
    rstd = sb("xrstd", [P, NT, 1])
    rec = sb("xrec", [P, H, 1])
    att = sb("xatt", [P, D])
    attT = sb("xattT", [P, DT, P])
    q_scr = [nc.dram_tensor(f"q_scr{i}", [3, D, S], BF16, kind="Internal").ap() for i in range(2)]
    k_scr = [nc.dram_tensor(f"k_scr{i}", [3, D, KX], BF16, kind="Internal").ap() for i in range(2)]
    ctx_t = a["ctx"].rearrange("b k d -> k b d")
    mask_t = a["mask"].rearrange("b (n p) k -> p (b n) k", p=P)
    w3_t = a["w3T"].rearrange("e (k p) h -> p (e k) h", p=P)

    def consts(e):
        N_CONST = 16 * 4
        if e.kind == "sp":
            for n in ("WqT", "WkT", "WvT", "WoT"):
                e.eng.dma_start(wt[n][:], a[n].rearrange("(k p) o -> p k o", p=P)).then_inc(sem("const"), 16)
            wait(e.eng, sem("set"), 4)
        if e.kind == "pool":
            e.eng.memset(masked_score[:], 1e-9 / SCALE).then_inc(sem("set"), 1)
            e.eng.memset(zeros[:], 0.0).then_inc(sem("set"), 1)
            for i in range(2):
                e.eng.memset(vx[i][:], 1.0).then_inc(sem("set"), 1)
            wait(e.eng, sem("set"), 4)
        if e.kind in ("dve", "act"):
            wait(e.eng, sem("set"), 4)
        if e.kind == "pe":
            wait(e.eng, sem("const"), N_CONST)
            wait(e.eng, sem("set"), 4)

    def load(e, r):
        if e.kind == "sp":
            i = r.par
            wait(e.eng, sem("in"), r.lin(64))
            wait(e.eng, st.written("turn_c"), r.lin(1, -1))
            wait(e.eng, sem("zero"), r.lin(1, -1))
            e.eng.dma_start(ctx_n[i][:].unsqueeze(1), ctx_t[:, bass.ds(r.lin(1), 1), :]).then_inc(sem("in"), 16)
            e.eng.dma_start(mask[i][:], mask_t[:, bass.ds(r.lin(NT), NT), :]).then_inc(sem("in"), 16)
            e.eng.dma_start(p.w3s[:, bass.ds(r.lin(1), 1), :], w3_t[:, bass.ds(r.lin(1), 1), :])\
                .then_inc(sem("in"), 16)
            e.eng.dma_start(zero_t[bass.ds(r.lin(1), 1), :, :, :].rearrange("r p n d -> (r p) n d"),
                            zeros[0:ZERO_P, :].unsqueeze(1).broadcast_to((ZERO_P, ZERO_N, D)))\
                .then_inc(sem("in"), 16)

    def normalise(e, r):
        if e.kind == "dve":
            for n in range(NT):
                e.eng.bn_stats(stats[:, n, :], p.xres[:, bass.ds(r.lin(NT, n), 1), :]).then_inc(sem("stats"), 1)
            wait(e.eng, sem("stats"), r.lin(NT, NT), apart=True)
            for n in range(NT):
                e.eng.bn_aggr(mv[:, n, :], stats[:, n, :]).then_inc(sem("mv"), 1)
        if e.kind == "pool":
            wait(e.eng, sem("mv"), r.lin(NT, NT))
            wait(e.eng, sem("norm"), r.lin(NT))
            e.eng.tensor_scalar(rstd[:], mv[:, :, 1:2], EPS, None, ALU.add).then_inc(sem("rstd"), 1)
            wait(e.eng, sem("rstd"), r.lin(2, 1))
            e.eng.tensor_tensor(rstd[:], rstd[:], p.eps[:, 0:1].unsqueeze(1).broadcast_to((P, NT, 1)),
                                ALU.pow).then_inc(sem("rstd"), 1)
            wait(e.eng, sem("in"), r.lin(64, 64))
            wait(e.eng, u.s_masked, r.lin(UPR, -UPR))
            e.eng.tensor_scalar(zero[r.par][:], mask[r.par][:], 0.0, None, ALU.is_equal).then_inc(sem("zero"), 1)

    def apply_norm(e, r):
        if e.kind == "dve":
            wait(e.eng, sem("rstd"), r.lin(2, 2))
            wait(e.eng, st.written("turn_n"), r.lin(1))
            for n in range(NT):
                e.eng.tensor_scalar(xn[:, n, :].unsqueeze(1), p.xres[:, bass.ds(r.lin(NT, n), 1), :],
                                    mv[:, n, 0:1], rstd[:, n, :], ALU.subtract, ALU.mult)\
                    .then_inc(sem("norm"), 1)

    def turn_n(e, r):
        def turn(pe):
            for k in range(DT):
                for n in range(NT):
                    mm = pe.transpose(p.M[:, k * S + n * P:k * S + (n + 1) * P], xn[:, n, k * P:(k + 1) * P],
                                      p.ident[:])
            return mm

        def copy(act):
            return act.copy(nT[:], p.M[:].rearrange("p (k t) -> p k t", k=DT))
        st.run(e, "turn_n", r.lin(1), [(sem("norm"), r.lin(NT, NT))], turn, "act", copy)

    def turn_c(e, r):
        i = r.par

        def turn(pe):
            for k in range(DT):
                mm = pe.transpose(p.M[:, k * KX:(k + 1) * KX], ctx_n[i][:, k * P:(k + 1) * P],
                                  p.ident[0:KX, 0:KX])
            return mm

        def copy(act):
            return act.copy(cT[i][:], p.M[:, 0:DT * KX].rearrange("p (k t) -> p k t", k=DT))
        st.run(e, "turn_c", r.lin(1), [(sem("in"), r.lin(64, 64))], turn, "act", copy)

    def features(pe, weights, xT, n):
        for o in range(DT):
            for k in range(DT):
                mm = pe.matmul(p.M[:, o * n:(o + 1) * n], weights[:, k, o * P:(o + 1) * P], xT[:, k, :],
                               start=(k == 0), stop=(k == DT - 1))
        return mm

    def queries(e, r):
        def copy(act):
            wait(act, sem("qp"), r.lin(3))
            return act.copy(qT[:], p.M[:].rearrange("p (k t) -> p k t", k=DT))
        st.run(e, "q", r.lin(1), [(st.read("turn_n"), r.lin(1, 1))],
               lambda pe: features(pe, wt["WqT"], nT, S), "act", copy)
        if e.kind == "act":
            wait(e.eng, st.read("q"), r.lin(1, 1))
            wait(e.eng, sem("q_scr"), r.lin(16))
            e.eng.copy(qp[:, 0, :, :], qT[:]).then_inc(sem("qp1"), 1)

    def keys(e, r):
        i = r.par

        def copy(act):
            wait(act, sem("kp"), r.lin(3))
            return act.copy(kT[:], p.M[:, 0:DT * KX].rearrange("p (k t) -> p k t", k=DT))
        st.run(e, "k", r.lin(1), [(st.read("turn_c"), r.lin(1, 1))],
               lambda pe: features(pe, wt["WkT"], cT[i], KX), "act", copy)
        if e.kind == "act":
            wait(e.eng, st.read("k"), r.lin(1, 1))
            wait(e.eng, sem("k_scr"), r.lin(16))
            e.eng.copy(kp[:, 0, :, :], kT[:]).then_inc(sem("kp1"), 1)

    def parts(e, r):
        i = r.par
        if e.kind == "pool":
            wait(e.eng, sem("qp1"), r.lin(1, 1))
            wait(e.eng, sem("kp"), r.lin(3))
            split_rest(e.eng, qp[:, 0, :, :], qT[:], rest[:], qp[:, 1, :, :], qp[:, 2, :, :], sem("qp"), r.lin(3))
            wait(e.eng, sem("kp1"), r.lin(1, 1))
            wait(e.eng, sem("qp"), r.lin(3, 3))
            split_rest(e.eng, kp[:, 0, :, :], kT[:], rest[:, :, 0:KX], kp[:, 1, :, :], kp[:, 2, :, :],
                       sem("kp"), r.lin(3))
        if e.kind == "sp":
            wait(e.eng, sem("qp"), r.lin(3, 3))
            wait(e.eng, sem("stacks"), r.lin(192))
            e.eng.dma_start(q_scr[i].rearrange("c (k p) t -> p c k t", p=P), qp[:]).then_inc(sem("q_scr"), 16)
            wait(e.eng, sem("kp"), r.lin(3, 3))
            e.eng.dma_start(k_scr[i].rearrange("c (k p) t -> p c k t", p=P), kp[:]).then_inc(sem("k_scr"), 16)
            wait(e.eng, u.s_scores, r.lin(UPR, -UPR))
            wait(e.eng, sem("q_scr"), r.lin(16, 16))
            load_stack(e.eng, qs[i], q_scr[i], Q_SLOTS, sem("stacks"))
            wait(e.eng, sem("k_scr"), r.lin(16, 16))
            load_stack(e.eng, ks[i], k_scr[i], K_SLOTS, sem("stacks"))

    def make_values(e, r):
        i = r.par

        def products(pe):
            for k in range(DT):
                mm = pe.matmul(p.M[0:KX, 0:D], cT[i][:, k, :], wt["WvT"][:, k, :], start=(k == 0),
                               stop=(k == DT - 1))
            return mm

        def copy(act):
            wait(act, u.s_pv, r.lin(UPR, -UPR))
            return act.copy(vx[i][:, :, 0:HD], p.M[0:KX, 0:D].rearrange("p (h d) -> p h d", d=HD))
        st.run(e, "v", r.lin(1), [(st.read("turn_c"), r.lin(1, 1))], products, "act", copy)

    def scores(e, r, s):
        n, f = s // DT, s % DT
        i = r.par
        if e.kind == "pe":
            if s == 0:
                wait(e.eng, sem("stacks"), r.lin(192, 192))
            u.scores(e.eng, r.lin(UPR, s), s % 2, lambda h: qs[i][:, f * HU + h, n * P:(n + 1) * P],
                     lambda h: ks[i][:, f * HU + h, :], KX)
        if e.kind == "dve":
            if s == 0:
                wait(e.eng, sem("zero"), r.lin(1, 1), apart=True)
            u.maxima(e.eng, r.lin(UPR, s), s % 2, KX, (zero[i][:, n, :], masked_score[:]))

    def values(e, r, s):
        f = s % DT
        if s == 0:
            wait(e.eng, st.read("v"), r.lin(1, 1))
        u.values(e.eng, r.lin(UPR, s), s % 2, r.lin(UPR // 2, s // 2) if f == 0 else None, f,
                 lambda h: vx[r.par][:, f * HU + h, :], KX)

    def turn_back(e, r, n):
        t = r.lin(NT, n)

        def turn(pe):
            for g in range(4):
                mm = pe.transpose(p.M[:, g * P:(g + 1) * P], u.outT[n][:, g, :], p.ident[:])
            return mm

        def divide(dve):
            m = p.M[:].rearrange("p (h d) -> p h d", h=H)
            dve.reciprocal(rec[:], m[:, :, HD:HD + 1]).then_inc(sem("rec"), 1)
            wait(dve, sem("rec"), t + 1)
            wait(dve, st.written("att"), t)
            return dve.tensor_tensor(att[:].rearrange("p (h d) -> p h d", d=HD), m[:, :, 0:HD],
                                     rec[:].broadcast_to((P, H, HD)), ALU.mult)
        st.run(e, "back", t, [(u.s_out, t + 1)], turn, "dve", divide)

    def turn_att(e, r, n):
        t = r.lin(NT, n)

        def turn(pe):
            for k in range(DT):
                mm = pe.transpose(p.M[:, k * P:(k + 1) * P], att[:, k * P:(k + 1) * P], p.ident[:])
            return mm

        def copy(act):
            return act.copy(attT[:], p.M[:, 0:D].rearrange("p (k t) -> p k t", k=DT))
        st.run(e, "att", t, [(st.read("back"), t + 1)], turn, "act", copy)

    def project(e, r, n):
        t = r.lin(NT, n)

        def products(pe):
            for k in range(DT):
                mm = pe.matmul(p.M[:, 0:D], attT[:, k, :], wt["WoT"][:, k, :], start=(k == 0), stop=(k == DT - 1))
            return mm

        def residual(dve):
            x = p.xres[:, bass.ds(t, 1), :]
            return dve.tensor_tensor(x, p.M[:, 0:D].unsqueeze(1), x, ALU.add)
        st.run(e, "proj", t, [(st.read("att"), t + 1)], products, "dve", residual)

    def prepare(e, r):
        load(e, r)
        normalise(e, r)
        apply_norm(e, r)
        turn_n(e, r)
        turn_c(e, r)
        queries(e, r)
        keys(e, r)
        parts(e, r)

    def prologue(e):
        consts(e)
        prepare(e, Row(None, 0))
        make_values(e, Row(None, 0))
        prepare(e, Row(None, 1))
        scores(e, Row(None, 0), 0)

    def lag(r, s, d):
        return (r, s - d) if s >= d else (r.plus(-1), s - d + UPR)

    def at_unit(x):
        return x[0].lin(UPR, x[1]), x[1] % 2

    def slot(e, r, s, first, ahead, last, drain=False):
        U, nxt, nxt2, prev = r.lin(UPR, s), r.plus(1), r.plus(2), r.plus(-1)
        exists = lambda d: s >= d or not first
        done = lambda f, *x: (lambda: None if first else f(e, prev, *x))
        then = lambda f, row, ok: (lambda: f(e, row) if ok else None)
        stages = {
            0: [done(turn_back, 0), then(turn_n, nxt2, ahead), then(turn_c, nxt2, ahead)],
            1: [done(turn_att, 0), then(queries, nxt2, ahead), then(keys, nxt2, ahead)],
            2: [done(project, 0), done(turn_back, 1), then(make_values, nxt, not (last or drain))],
            3: [done(turn_att, 1), lambda: None, done(project, 1)],
        }[s]
        k = e.kind
        if s == 0 and ahead:
            normalise(e, nxt2)
        if not drain and not (last and s == UPR - 1):
            scores(e, *((r, s + 1) if s + 1 < UPR else (nxt, 0)))
        if s == 0 and ahead:
            apply_norm(e, nxt2)
        if k == "act" and not drain:
            u.exponentials(e.eng, U, s % 2, KX)
        stages[0]()
        if k == "pe" and not drain:
            u.subtract_max(e.eng, U, s % 2, KX)
        if exists(1) and not (drain and s >= 1):
            if k == "pe":
                u.turn(e.eng, *at_unit(lag(r, s, 1)), KX)
            if k in ("act", "dve"):
                u.evacuate(e.eng, 0 if k == "act" else 1, *at_unit(lag(r, s, 1)), KX)
        stages[1]()
        if exists(2) and not (drain and s >= 2):
            rr, ss = lag(r, s, 2)
            if k == "pe":
                values(e, rr, ss)
            if k == "act" and s % 2 == 1:
                u.out_copy(e.eng, rr.lin(UPR, ss), rr.lin(UPR // 2, ss // 2), ss // 2 % 2, st.written("back"))
        stages[2]()
        if s == 1 and ahead:
            parts(e, nxt2)

    def row(e, r, first, last):
        ahead = not (r.reg is None and r.off >= NB - 2)
        if e.kind == "sp":
            if ahead:
                load(e, r.plus(2))
                parts(e, r.plus(2))
            return
        if not first:
            e.free = [(st.read("v"), r.lin(1, 1)), (st.read("proj"), r.lin(NT, -NT))]
        for s in range(UPR):
            slot(e, r, s, first, ahead, last)

    def epilogue(e, r):
        if e.kind != "sp":
            for s in range(UPR):
                slot(e, r, s, False, False, True, drain=True)

    on_engines(nc, lambda e: rows_of(e, NB, prologue, row, epilogue))



RING = 8


def experts(p, ctx):
    w2s = p.sb("w2s", [P, E * HT, D], ctx=ctx)
    slot_id = p.sb("slot_id", [P, TOP, TILES], I32, ctx)
    share = p.sb("share", [P, TOP, TILES], ctx=ctx)
    tile_expert = p.sb("tile_expert", [1, N_ST], I32, ctx)
    y_dram = p.nc.dram_tensor("y_rows", [N_ST * P, D], F32, kind="Internal").ap()
    with ExitStack() as c:
        route(p, c, w2s, slot_id, share, tile_expert)
    with ExitStack() as c:
        expert_tiles(p, c, w2s, tile_expert, y_dram)
    with ExitStack() as c:
        combine(p, c, slot_id, share, y_dram)


def route(p, ctx, w2s, slot_id, share, tile_expert):
    nc, a = p.nc, p.a
    sb = lambda n, s, dt=F32: p.sb(n, s, dt, ctx)
    sem = lambda n: p.sem("rt_" + n)
    xn_all = sb("xn_all", [P, TILES, D])
    xb = [sb(f"xb{i}", [P, NT, D]) for i in range(2)]
    nT = [sb(f"rnT{i}", [P, DT, S]) for i in range(2)]
    routerT = sb("routerT_sb", [P, DT, E])
    before = sb("before_sb", [P, P])
    ones = sb("ones", [P, P])
    iota_e = sb("iota_e_sb", [P, E])
    iota_t = sb("iota_t_sb", [1, N_ST])
    stats = sb("rstats", [P, NT, 6])
    mv = sb("rmv", [P, NT, 2])
    rstd = sb("rrstd", [P, NT, 1])
    t8 = lambda n, dt=F32: sb(n, [P, TILES, E], dt)
    prob, top, sel, posn, tmp = (t8(n) for n in ("prob", "top", "sel", "posn", "tmp"))
    hot = [t8("hot0"), t8("hot1")]
    scan = [t8("scan0"), t8("scan1")]
    top_id = t8("top_id", U32)
    tile1 = sb("tile1", [P, TILES, 1])
    idf = sb("idf", [P, TILES, TOP])
    slotf = sb("slotf", [P, TOP, TILES, 1])
    count_i = sb("count_i", [P, E], I32)
    tiles_i = sb("tiles_i", [P, E], I32)
    tiles_e, starts = sb("tiles_e", [P, E]), sb("starts", [P, E])
    cum = [sb("cum0", [P, E]), sb("cum1", [P, E])]
    passed = sb("passed", [1, N_ST, E])
    expert_f = sb("expert_f", [1, N_ST, 1])

    def walk(e):
        if e.kind == "sp":
            for dst, src in ((routerT[:], a["routerT"].rearrange("(k p) e -> p k e", p=P)),
                             (before[:], a["before"]), (iota_e[:], a["iota_e"].unsqueeze(0).broadcast_to((P, E))),
                             (iota_t[:], a["iota_t"].unsqueeze(0))):
                e.eng.dma_start(dst, src).then_inc(sem("const"), 16)
            e.eng.dma_start(w2s[:], a["w2T"].rearrange("e (k p) d -> p (e k) d", p=P)).then_inc(p.sem("w2"), 16)
        if e.kind == "pool":
            e.eng.memset(ones[:], 1.0).then_inc(sem("set"), 1)
        if e.kind in ("pe", "dve"):
            wait(e.eng, sem("const"), 64)
            wait(e.eng, sem("set"), 1)
        row(e, Row(None, 0))
        with e.eng.Fori(1, NB - 1, 2) as r:
            row(e, Row(r, 0, 1))
            row(e, Row(r, 1, 0))
        row(e, Row(None, NB - 1))
        assign(e)

    def row(e, r):
        i = r.par
        if e.kind == "dve":
            for n in range(NT):
                e.eng.bn_stats(stats[:, n, :], p.xres[:, bass.ds(r.lin(NT, n), 1), :]).then_inc(sem("stats"), 1)
            wait(e.eng, sem("stats"), r.lin(NT, NT), apart=True)
            for n in range(NT):
                e.eng.bn_aggr(mv[:, n, :], stats[:, n, :]).then_inc(sem("mv"), 1)
            wait(e.eng, sem("rstd"), r.lin(2, 2))
            wait(e.eng, sem("turn"), r.lin(1, -1))
            for n in range(NT):
                t = bass.ds(r.lin(NT, n), 1)
                for dst in (xb[i][:, n:n + 1, :], xn_all[:, t, :]):
                    e.eng.tensor_scalar(dst, p.xres[:, t, :], mv[:, n, 0:1], rstd[:, n, :],
                                        ALU.subtract, ALU.mult).then_inc(sem("norm"), 1)
        if e.kind == "pool":
            wait(e.eng, sem("mv"), r.lin(NT, NT))
            wait(e.eng, sem("norm"), r.lin(2 * NT))
            e.eng.tensor_scalar(rstd[:], mv[:, :, 1:2], EPS, None, ALU.add).then_inc(sem("rstd"), 1)
            wait(e.eng, sem("rstd"), r.lin(2, 1))
            e.eng.tensor_tensor(rstd[:], rstd[:], p.eps[:, 0:1].unsqueeze(1).broadcast_to((P, NT, 1)),
                                ALU.pow).then_inc(sem("rstd"), 1)
        if e.kind == "pe":
            wait(e.eng, sem("norm"), r.lin(2 * NT, 2 * NT))
            wait(e.eng, sem("nT"), r.lin(1, -1))
            for k in range(DT):
                for n in range(NT):
                    mm = e.eng.transpose(p.T[i][:, k * NT + n, :], xb[i][:, n, k * P:(k + 1) * P], p.ident[:])
            mm.then_inc(sem("turn"), 1)
            wait(e.eng, sem("nT"), r.lin(1, 1))
            out = p.O[:].rearrange("p a b -> p (a b)")
            for n in range(NT):
                for k in range(DT):
                    mm = e.eng.matmul(out[:, bass.ds(r.lin(NT * E, n * E), E)], nT[i][:, k, n * P:(n + 1) * P],
                                      routerT[:, k, :], start=(k == 0), stop=(k == DT - 1), skip_group_check=True)
            mm.then_inc(sem("logits"), 1)
        if e.kind == "act":
            wait(e.eng, sem("turn"), r.lin(1, 1))
            wait(e.eng, sem("logits"), r.lin(1, -1))
            e.eng.copy(nT[i][:], p.T[i][:].rearrange("p (k n) t -> p k (n t)", k=DT)).then_inc(sem("nT"), 1)

    def assign(e):
        flat = lambda x: x[:].rearrange("p t e -> p (t e)")
        wide = lambda x: x.unsqueeze(1).broadcast_to((P, TILES, E))
        counts = lambda x: x[:, 0:TILES * E].rearrange("p (t e) -> p t e", e=E)
        bank = lambda x: x[:].rearrange("p a b -> p (a b)")
        v = e.eng
        steps = 0

        def step(ins):
            nonlocal steps
            steps += 1
            ins.then_inc(sem("step"), 1)
            wait(v, sem("step"), steps)

        if e.kind == "dve":
            wait(v, sem("logits"), NB)
            logits = counts(bank(p.O))
            step(v.tensor_reduce(tile1[:], logits, AX_X, ALU.max))
            step(v.tensor_tensor(tmp[:], logits, tile1[:].broadcast_to((P, TILES, E)), ALU.subtract))
        if e.kind == "act":
            wait(e.eng, sem("step"), 2)
            e.eng.activation(prob[:], tmp[:], ACT.Exp).then_inc(sem("exp"), 1)
        if e.kind == "dve":
            wait(v, sem("exp"), 1)
            step(v.tensor_reduce(tile1[:], prob[:], AX_X, ALU.add))
            step(v.reciprocal(tile1[:], tile1[:]))
            step(v.tensor_tensor(prob[:], prob[:], tile1[:].broadcast_to((P, TILES, E)), ALU.mult))
            for t in range(TILES):
                ins = v.max(top[:, t, :], prob[:, t, :])
            step(ins)
            for t in range(TILES):
                ins = v.max_index(top_id[:, t, :], top[:, t, :], prob[:, t, :])
            step(ins)
            step(v.tensor_tensor(tile1[:], top[:, :, 0:1], top[:, :, 1:2], ALU.add))
            step(v.reciprocal(tile1[:], tile1[:]))
            for j in range(TOP):
                step(v.tensor_tensor(share[:, j, :].unsqueeze(2), top[:, :, j:j + 1], tile1[:], ALU.mult))
            step(v.tensor_copy(idf[:], top_id[:, :, 0:TOP]))
            for j in range(TOP):
                step(v.tensor_tensor(hot[j][:], wide(iota_e[:]), idf[:, :, j:j + 1].broadcast_to((P, TILES, E)),
                                     ALU.is_equal))
            v.tensor_tensor(sel[:], hot[0][:], hot[1][:], ALU.add).then_inc(sem("sel"), 1)
        if e.kind == "pe":
            wait(e.eng, sem("sel"), 1)
            e.eng.matmul(p.M[:, 0:TILES * E], before[:], flat(sel), start=True, stop=True)
            e.eng.matmul(bank(p.T[0])[:, 0:TILES * E], ones[:], flat(sel), start=True,
                         stop=True).then_inc(sem("count"), 1)
        if e.kind == "dve":
            total, prefix = counts(bank(p.T[0])), counts(p.M)
            wait(v, sem("count"), 1)
            step(v.tensor_copy(scan[0][:], total))
            cur, d = 0, 1
            while d < TILES:
                step(v.tensor_copy(scan[1 - cur][:, 0:d, :], scan[cur][:, 0:d, :]))
                step(v.tensor_tensor(scan[1 - cur][:, d:, :], scan[cur][:, d:, :], scan[cur][:, 0:TILES - d, :],
                                     ALU.add))
                cur, d = 1 - cur, 2 * d
            step(v.tensor_scalar(count_i[:], scan[cur][:, TILES - 1, :], float(P - 1), None, ALU.add))
            step(v.tensor_scalar(tiles_i[:], count_i[:], P.bit_length() - 1, None, ALU.logical_shift_right))
            step(v.tensor_copy(tiles_e[:], tiles_i[:]))
            step(v.tensor_copy(cum[0][:], tiles_e[:]))
            c, d = 0, 1
            while d < E:
                step(v.tensor_copy(cum[1 - c][:, 0:d], cum[c][:, 0:d]))
                step(v.tensor_tensor(cum[1 - c][:, d:], cum[c][:, d:], cum[c][:, 0:E - d], ALU.add))
                c, d = 1 - c, 2 * d
            step(v.tensor_tensor(starts[:], cum[c][:], tiles_e[:], ALU.subtract))
            step(v.tensor_scalar(starts[:], starts[:], float(P), None, ALU.mult))
            step(v.tensor_tensor(posn[:], scan[cur][:], total, ALU.subtract))
            step(v.tensor_tensor(posn[:], posn[:], prefix, ALU.add))
            step(v.tensor_tensor(posn[:], posn[:], wide(starts[:]), ALU.add))
            for j in range(TOP):
                step(v.tensor_tensor(tmp[:], posn[:], hot[j][:], ALU.mult))
                step(v.tensor_reduce(slotf[:, j, :, :], tmp[:], AX_X, ALU.add))
            v.tensor_copy(slot_id[:], slotf[:].rearrange("p j t o -> p j (t o)")).then_inc(sem("slots"), 1)
            step(v.tensor_tensor(passed[:], iota_t[:].unsqueeze(2).broadcast_to((1, N_ST, E)),
                                 cum[c][0:1, :].unsqueeze(1).broadcast_to((1, N_ST, E)), ALU.is_ge))
            step(v.tensor_reduce(expert_f[:], passed[:], AX_X, ALU.add))
            step(v.tensor_scalar(tile_expert[:].unsqueeze(2), expert_f[:], float(E - 1), None, ALU.min))
        if e.kind == "pool":
            wait(e.eng, sem("slots"), 1)
            wait(e.eng, sem("norm"), 2 * NT * NB)
            pairs = [(t, j) for t in range(TILES) for j in range(TOP)]
            for n, (t, j) in enumerate(pairs):
                s = sem(f"scatter{n % RING}")
                wait(e.eng, s, 16 * (n // RING))
                e.eng.indirect_dma_start(p.rows_dram, bass.IndirectOffsetOnAxis(ap=slot_id[:, j, t:t + 1], axis=0),
                                         xn_all[:, t, :], None).then_inc(s, 16)
            for k in range(RING):
                wait(e.eng, sem(f"scatter{k}"), 16 * (len(pairs) // RING))

    on_engines(nc, walk)


def expert_tiles(p, ctx, w2s, tile_expert, y_dram):
    nc = p.nc
    sb = lambda n, s, dt=F32: p.sb(n, s, dt, ctx)
    sem = lambda n: p.sem("et_" + n)
    xg = [sb(f"xg{i}", [P, D]) for i in range(2)]
    xgT = [sb(f"xgT{i}", [P, DT, P]) for i in range(2)]
    ex = [sb(f"ex{i}", [P, HID]) for i in range(2)]
    gate = [sb(f"gate{i}", [P, HID]) for i in range(2)]
    gT = [sb(f"ggT{i}", [P, HT, P]) for i in range(2)]
    y = [sb(f"y{i}", [P, D]) for i in range(2)]
    h_ps = [p.S[i][:].rearrange("p (w a) b -> p w (a b)", w=2) for i in range(2)]
    x_ps, g_ps = p.T[0], p.T[1]
    y_ps = p.O[:].rearrange("p a b -> p (a b)")[:, 0:D]
    rows_t = p.rows_dram.rearrange("(t p) d -> p t d", p=P)
    y_t = y_dram.rearrange("(t p) d -> p t d", p=P)

    def load(e, r):
        if e.kind == "sp":
            wait(e.eng, sem("x_in"), r.lin(16))
            wait(e.eng, sem("x_turn"), r.lin(1, -1))
            e.eng.dma_start(xg[r.par][:].unsqueeze(1), rows_t[:, bass.ds(r.lin(1), 1), :]).then_inc(sem("x_in"), 16)

    def turn_x(e, r):
        if e.kind == "pe":
            wait(e.eng, sem("x_in"), r.lin(16, 16))
            wait(e.eng, sem("xT"), r.lin(1))
            for k in range(DT):
                mm = e.eng.transpose(x_ps[:, k, :], xg[r.par][:, k * P:(k + 1) * P], p.ident[:])
            mm.then_inc(sem("x_turn"), 1)
        if e.kind == "act":
            wait(e.eng, sem("x_turn"), r.lin(1, 1))
            wait(e.eng, sem("h"), r.lin(1, -1))
            e.eng.copy(xgT[r.par][:], x_ps[:, 0:DT, :]).then_inc(sem("xT"), 1)

    def expert_of(e, r):
        return e.eng.value_load(tile_expert[0:1, bass.ds(r.lin(1), 1)], min_val=0, max_val=E - 1)

    def hidden(e, r):
        i = r.par
        if e.kind == "pe":
            expert = expert_of(e, r)
            wait(e.eng, sem("xT"), r.lin(1, 1))
            wait(e.eng, sem("gate"), r.lin(4, -4))
            for j, w in enumerate((p.w1s, p.w3s)):
                for k in range(DT):
                    mm = e.eng.matmul(h_ps[i][:, j:j + 1, :], xgT[i][:, k, :], w[:, bass.ds(expert * DT + k, 1), :],
                                      start=(k == 0), stop=(k == DT - 1))
            mm.then_inc(sem("h"), 1)
        if e.kind == "act":
            wait(e.eng, sem("h"), r.lin(1, 1))
            wait(e.eng, sem("gate"), r.lin(4, -4))
            e.eng.activation(ex[i][:], h_ps[i][:, 0, :], ACT.Exp, scale=-1.0).then_inc(sem("exp"), 1)
        if e.kind == "dve":
            wait(e.eng, sem("exp"), r.lin(1, 1))
            wait(e.eng, sem("g_turn"), r.lin(1, -1))
            e.eng.tensor_scalar(ex[i][:], ex[i][:], 1.0, None, ALU.add).then_inc(sem("gate"), 1)
            wait(e.eng, sem("gate"), r.lin(4, 1))
            e.eng.reciprocal(ex[i][:], ex[i][:]).then_inc(sem("gate"), 1)
            wait(e.eng, sem("gate"), r.lin(4, 2))
            e.eng.tensor_tensor(gate[i][:], h_ps[i][:, 0, :], ex[i][:], ALU.mult).then_inc(sem("gate"), 1)
            wait(e.eng, sem("gate"), r.lin(4, 3))
            e.eng.tensor_tensor(gate[i][:], h_ps[i][:, 1, :], gate[i][:], ALU.mult).then_inc(sem("gate"), 1)

    def turn_gate(e, r):
        i = r.par
        if e.kind == "pe":
            wait(e.eng, sem("gate"), r.lin(4, 4))
            wait(e.eng, sem("gT"), r.lin(1))
            for k in range(HT):
                mm = e.eng.transpose(g_ps[:, k, :], gate[i][:, k * P:(k + 1) * P], p.ident[:])
            mm.then_inc(sem("g_turn"), 1)
        if e.kind == "act":
            wait(e.eng, sem("g_turn"), r.lin(1, 1))
            wait(e.eng, sem("y"), r.lin(1, -1))
            e.eng.copy(gT[i][:], g_ps[:]).then_inc(sem("gT"), 1)

    def outputs(e, r):
        i = r.par
        if e.kind == "pe":
            expert = expert_of(e, r)
            wait(e.eng, sem("gT"), r.lin(1, 1))
            wait(e.eng, sem("y_sb"), r.lin(1))
            for k in range(HT):
                mm = e.eng.matmul(y_ps.unsqueeze(1), gT[i][:, k, :], w2s[:, bass.ds(expert * HT + k, 1), :],
                                  start=(k == 0), stop=(k == HT - 1))
            mm.then_inc(sem("y"), 1)
        if e.kind == "act":
            wait(e.eng, sem("y"), r.lin(1, 1))
            wait(e.eng, sem("y_out"), r.lin(16, -16))
            e.eng.copy(y[i][:], y_ps).then_inc(sem("y_sb"), 1)
        if e.kind == "sp":
            wait(e.eng, sem("y_sb"), r.lin(1, 1))
            wait(e.eng, sem("y_out"), r.lin(16))
            e.eng.dma_start(y_t[:, bass.ds(r.lin(1), 1), :], y[i][:].unsqueeze(1)).then_inc(sem("y_out"), 16)

    def tile(e, r):
        n = r.off if r.reg is None else None
        has = lambda d: n is None or 0 <= n + d < N_ST
        if has(2):
            load(e, r.plus(2))
        if has(0):
            hidden(e, r)
        if has(-1):
            turn_gate(e, r.plus(-1))
        if has(1):
            turn_x(e, r.plus(1))
        if has(-2):
            outputs(e, r.plus(-2))

    def walk(e):
        if e.kind == "pe":
            wait(e.eng, p.sem("w2"), 16)
        load(e, Row(None, 0))
        load(e, Row(None, 1))
        turn_x(e, Row(None, 0))
        for n in range(4):
            tile(e, Row(None, n))
        with e.eng.Fori(4, N_ST - 3, 2) as r:
            tile(e, Row(r, 0, 0))
            tile(e, Row(r, 1, 1))
        for n in range(N_ST - 2, N_ST + 2):
            tile(e, Row(None, n))
        if e.kind == "sp":
            wait(e.eng, sem("y_out"), 16 * N_ST)

    on_engines(nc, walk)


def combine(p, ctx, slot_id, share, y_dram):
    nc = p.nc
    sem = lambda n: p.sem("cb_" + n)
    got = [p.sb(f"got{i}", [P, D], ctx=ctx) for i in range(RING)]
    out_t = p.a["out"].rearrange("b (n p) d -> p (b n) d", p=P)
    GROUP = 4
    pairs = [(t, j) for t in range(TILES) for j in range(TOP)]

    def walk(e):
        if e.kind == "pool":
            for n, (t, j) in enumerate(pairs):
                k = n % RING
                wait(e.eng, sem("used"), n - RING + 1)
                wait(e.eng, sem(f"got{k}"), 16 * (n // RING))
                e.eng.indirect_dma_start(got[k][:], None, y_dram,
                                         bass.IndirectOffsetOnAxis(ap=slot_id[:, j, t:t + 1], axis=0))\
                    .then_inc(sem(f"got{k}"), 16)
        if e.kind == "dve":
            for n, (t, j) in enumerate(pairs):
                k = n % RING
                wait(e.eng, sem(f"got{k}"), 16 * (n // RING + 1))
                wait(e.eng, sem("used"), n)
                e.eng.scalar_tensor_tensor(p.xres[:, t, :], got[k][:], share[:, j, t:t + 1], p.xres[:, t, :],
                                           ALU.mult, ALU.add).then_inc(sem("used"), 1)
        if e.kind == "sp":
            for g in range(TILES // GROUP):
                ts = slice(g * GROUP, (g + 1) * GROUP)
                wait(e.eng, sem("used"), TOP * GROUP * (g + 1))
                e.eng.dma_start(out_t[:, ts, :], p.xres[:, ts, :]).then_inc(sem("out"), 16)
            wait(e.eng, sem("out"), 16 * (TILES // GROUP))

    on_engines(nc, walk)


def layout(x, ctx_1024, mask_Bx1xSxS2_ik1, L0_attn_pos_emb, L0_attn_global_memory, L0_attn_conv_w,
           L0_attn_conv_b, L0_attn_gate_w, L0_attn_gate_b, L0_attn_out_w, L0_attn_out_b,
           L0_xattn_Wq, L0_xattn_Wk, L0_xattn_Wv, L0_xattn_Wo, L0_ffn_router_w, L0_ffn_w1,
           L0_ffn_w2, L0_ffn_w3):
    c = np.ascontiguousarray
    return {
        "x": c(x), "ctx": c(ctx_1024), "mask": c(np.reshape(mask_Bx1xSxS2_ik1, (NB, S, KX))),
        "pos_emb": c(L0_attn_pos_emb), "global_memory": c(L0_attn_global_memory),
        "conv_w": c(np.transpose(L0_attn_conv_w, (1, 2, 0))), "conv_b": c(L0_attn_conv_b),
        "gate_w": c(L0_attn_gate_w), "gate_b": c(L0_attn_gate_b),
        "out_w": c(L0_attn_out_w), "out_b": c(L0_attn_out_b),
        "WqT": c(np.transpose(L0_xattn_Wq)), "WkT": c(np.transpose(L0_xattn_Wk)),
        "WvT": c(np.transpose(L0_xattn_Wv)), "WoT": c(np.transpose(L0_xattn_Wo)),
        "routerT": c(np.transpose(L0_ffn_router_w)),
        "w1T": c(np.transpose(L0_ffn_w1, (0, 2, 1))), "w3T": c(np.transpose(L0_ffn_w3, (0, 2, 1))),
        "w2T": c(np.transpose(L0_ffn_w2, (0, 2, 1))),
        "ident": np.eye(P, dtype=np.float32), "before": np.triu(np.ones((P, P), np.float32), 1),
        "iota_e": np.arange(E, dtype=np.float32), "iota_t": np.arange(N_ST, dtype=np.float32),
    }


def kernel(**inputs):
    import concourse.bacc as bacc
    from concourse.bass_utils import run_bass_kernel_spmd

    nc = bacc.Bacc("TRN2", target_bir_lowering=False, num_devices=1)
    arrays = {f"in_{name}": array for name, array in layout(**inputs).items()}
    aps = {name[3:]: nc.dram_tensor(name, array.shape, mybir.dt.from_np(array.dtype), kind="ExternalInput").ap()
           for name, array in arrays.items()}
    aps["out"] = nc.dram_tensor("out", (NB, S, D), F32, kind="ExternalOutput").ap()
    build(nc, aps)
    return run_bass_kernel_spmd(nc, [arrays], core_ids=[0]).results[0]["out"]
```

```python
from contextlib import ExitStack

import numpy as np

import concourse.bass as bass
from concourse import mybir

F32 = mybir.dt.float32
BF16 = mybir.dt.bfloat16
I32 = mybir.dt.int32
U32 = mybir.dt.uint32
ALU = mybir.AluOpType
ACT = mybir.ActivationFunctionType
AX_X = mybir.AxisListType.X

P = 128
D = 256
DT = D // P
H = 16
HD = D // H
HU = H // DT
NB = 16
S = 256
NT = S // P
TILES = NB * NT
G = 64
CK = 4
KX = 120
E = 8
HID = 512
HT = HID // P
TOKENS = NB * S
TOP = 2
N_ST = (TOP * TOKENS + E * (P - 1)) // P
N_ST += N_ST % 2
EPS = 1e-5
SCALE = 1.0 / float(np.sqrt(HD))
Q_SLOTS = ((0, 3, 0), (1, 2, 0), (2, 1, 0))
K_SLOTS = ((0, 3, 1), (0, 2, 1), (0, 1, 0))
SLOTS = 6
KS = SLOTS * HD




class Row:

    def __init__(self, reg, off, par=None):
        self.reg, self.off = reg, off
        self.par = off % 2 if reg is None else par

    def plus(self, n):
        return Row(self.reg, self.off + n, (self.par + n) % 2)

    def lin(self, k, c=0):
        if self.reg is None:
            return k * self.off + c
        return self.reg * k + (k * self.off + c)


class Started:
    sem = None


def wait(eng, sem, value, apart=False):
    if isinstance(value, int):
        if value > 0:
            eng.wait_ge(sem, value)
        return
    if apart or eng.engine in (mybir.EngineType.Pool, mybir.EngineType.SP):
        value = eng.to_reg(value)
        eng.wait_ge(Started.sem, 1)
    eng.wait_ge(sem, value)


def build(nc, a):
    with ExitStack() as ctx:
        Program(nc, a, ctx).emit()


class Program:
    def __init__(self, nc, a, ctx):
        self.nc, self.a, self.ctx = nc, a, ctx
        self.sems = {}

    def sem(self, name):
        if name not in self.sems:
            self.sems[name] = self.ctx.enter_context(self.nc.semaphore(name))
        return self.sems[name]

    def sb(self, name, shape, dt=F32, ctx=None):
        return (ctx or self.ctx).enter_context(self.nc.sbuf_tensor(name, shape, dt))

    def emit(self):
        nc, a, ctx = self.nc, self.a, self.ctx
        self.xres = self.sb("xres", [P, TILES, D])
        self.w1s = self.sb("w1s", [P, E * DT, HID])
        self.ident = self.sb("ident", [P, P])
        self.neg_ident = self.sb("neg_ident", [P, P], BF16)
        self.eps = self.sb("eps", [P, 4])
        Started.sem = self.sem("started")
        self.S = [ctx.enter_context(nc.psum_tensor(f"ps_scores{i}", [P, HU, P], F32)) for i in range(2)]
        self.T = [ctx.enter_context(nc.psum_tensor(f"ps_turn{i}", [P, 4, P], F32)) for i in range(2)]
        self.O = ctx.enter_context(nc.psum_tensor("ps_out", [P, 4, P], F32))
        self.M = ctx.enter_context(nc.psum_tensor("ps_misc", [P, 512], F32))
        with ExitStack() as c1:
            self_attention(self, c1)
        self.w3s = self.sb("w3s", [P, E * DT, HID])
        self.w2s = self.sb("w2s", [P, E * HT, D])
        with ExitStack() as c2:
            cross_attention(self, c2)
        with ExitStack() as c3:
            experts(self, c3)


class Units:

    def __init__(self, p, ctx, tag):
        self.p, self.nc = p, p.nc
        sem = lambda n: p.sem(f"{tag}_{n}")
        self.s_scores = sem("scores")
        self.s_masked = sem("masked")
        self.s_max = sem("max")
        self.s_negm = sem("negm")
        self.s_exp = sem("exp")
        self.s_turn = sem("turn")
        self.s_ev = [sem("ev0"), sem("ev1")]
        self.s_pv = sem("pv")
        self.s_out = sem("oev")
        self.probs = [p.sb(f"{tag}_probs{i}", [P, HU, P], ctx=ctx) for i in range(2)]
        self.probsT = [p.sb(f"{tag}_probsT{i}", [P, HU, P], ctx=ctx) for i in range(2)]
        self.rowmax = [p.sb(f"{tag}_rowmax{i}", [P, HU], BF16, ctx=ctx) for i in range(2)]
        self.outT = [p.sb(f"{tag}_outT{i}", [P, 4, P], ctx=ctx) for i in range(2)]

    def scores(self, pe, U, up, q, k, nk):
        wait(pe, self.s_exp, U - 1)
        for h in range(HU):
            mm = pe.matmul(self.p.S[up][:, h, 0:nk], q(h), k(h), start=(h % 4 == 0), stop=False,
                           skip_group_check=True)
        mm.then_inc(self.s_scores, 1)

    def maxima(self, dve, U, up, nk, masked=None):
        sc = self.p.S[up][:, :, 0:nk]
        wait(dve, self.s_scores, U + 1, apart=masked is not None)
        if masked is not None:
            mask, value = masked
            dve.copy_predicated(sc, mask.unsqueeze(1).broadcast_to((P, HU, nk)),
                                value.unsqueeze(2).broadcast_to((P, HU, nk))).then_inc(self.s_masked, 1)
            wait(dve, self.s_masked, U + 1)
        dve.tensor_reduce(self.rowmax[up][:], sc, AX_X, ALU.max).then_inc(self.s_max, 1)

    def subtract_max(self, pe, U, up, nk):
        wait(pe, self.s_max, U + 1)
        for g in range(2):
            mm = pe.matmul(self.p.S[up][:, 4 * g:4 * g + 4, 0:nk], self.p.neg_ident[:],
                           self.rowmax[up][:, 4 * g:4 * g + 4].unsqueeze(2).broadcast_to((P, 4, nk)),
                           start=False, stop=True, skip_group_check=True)
        mm.then_inc(self.s_negm, 1)

    def exponentials(self, act, U, up, nk):
        wait(act, self.s_negm, U + 1)
        wait(act, self.s_turn, 2 * (U - 1))
        act.activation(self.probs[up][:, :, 0:nk], self.p.S[up][:, :, 0:nk], ACT.Exp,
                       scale=SCALE).then_inc(self.s_exp, 1)

    def turn(self, pe, U, up, nk):
        wait(pe, self.s_exp, U + 1)
        for g in range(2):
            wait(pe, self.s_ev[g], U)
            for h in range(4):
                mm = pe.transpose(self.p.T[g][0:nk, h, :], self.probs[up][:, 4 * g + h, 0:nk], self.p.ident[:])
            mm.then_inc(self.s_turn, 1)

    def evacuate(self, eng, g, U, up, nk):
        wait(eng, self.s_turn, 2 * U + 1 + g)
        wait(eng, self.s_pv, U - 1)
        dst, src = self.probsT[up][0:nk, 4 * g:4 * g + 4, :], self.p.T[g][0:nk, :, :]
        ins = eng.copy(dst, src) if g == 0 else eng.tensor_copy(dst, src)
        ins.then_inc(self.s_ev[g], 1)

    def values(self, pe, U, up, Oi, ft, v, nk):
        wait(pe, self.s_ev[0], U + 1)
        wait(pe, self.s_ev[1], U + 1)
        if Oi is not None:
            wait(pe, self.s_out, Oi)
        for h in range(HU):
            j = h % 4
            mm = pe.matmul(self.p.O[32 * j:32 * j + 32, 2 * ft + h // 4, :], v(h),
                           self.probsT[up][0:nk, h, :], start=True, stop=True,
                           tile_position=(0, 32 * j), skip_group_check=True)
        mm.then_inc(self.s_pv, 1)

    def out_copy(self, act, U, Oi, op, s_back):
        wait(act, self.s_pv, U + 1)
        wait(act, s_back, Oi - 1)
        act.copy(self.outT[op][:], self.p.O[:]).then_inc(self.s_out, 1)


FIRST = 3
LAST = 3


def rows_of(e, n_rows, prologue, row, epilogue):
    prologue(e)
    for n in range(FIRST):
        row(e, Row(None, n), n == 0, False)
    with e.eng.Fori(FIRST, n_rows - LAST - 1, 2) as r:
        row(e, Row(r, 0, FIRST % 2), False, False)
        row(e, Row(r, 1, 1 - FIRST % 2), False, False)
    for n in range(n_rows - LAST, n_rows):
        row(e, Row(None, n), False, n == n_rows - 1)
    epilogue(e, Row(None, n_rows))


class Walker:

    def __init__(self, kind, eng):
        self.kind, self.eng, self.free = kind, eng, []


class Stages:

    def __init__(self, p, tag):
        self.p, self.tag = p, tag

    def written(self, name):
        return self.p.sem(f"{self.tag}_{name}_mm")

    def read(self, name):
        return self.p.sem(f"{self.tag}_{name}_rd")

    def run(self, e, name, index, needs, produce, reader, consume):
        if e.kind == "pe":
            for sem, value in e.free:
                wait(e.eng, sem, value, apart=True)
            for sem, value in needs:
                wait(e.eng, sem, value, apart=True)
            produce(e.eng).then_inc(self.written(name), 1)
        if e.kind == reader:
            wait(e.eng, self.written(name), index + 1)
            consume(e.eng).then_inc(self.read(name), 1)
        e.free = [(self.read(name), index + 1)]


def on_engines(nc, walk, before=None):
    with nc.Block() as block:
        @block.tensor
        def _(eng):
            walk(Walker("pe", eng))

        @block.scalar
        def _(eng):
            walk(Walker("act", eng))

        @block.vector
        def _(eng):
            walk(Walker("dve", eng))

        @block.gpsimd
        def _(eng):
            walk(Walker("pool", eng))

        @block.sync
        def _(eng):
            walk(Walker("sp", eng))


def split_rest(pool, first, whole, rest, second, third, sem, count):
    pool.tensor_tensor(rest, whole, first, ALU.subtract).then_inc(sem, 1)
    wait(pool, sem, count + 1)
    pool.tensor_copy(second, rest).then_inc(sem, 1)
    wait(pool, sem, count + 2)
    pool.tensor_tensor(third, rest, second, ALU.subtract).then_inc(sem, 1)


def load_stack(sp, stack, scratch, slots, sem):
    row = 0
    for part, n, step in slots:
        n_rows = n * HD
        for s in range(n):
            src = scratch[part + s * step].rearrange("(h d) t -> d h t", d=HD)
            sp.dma_start(stack[row + s * HD:row + (s + 1) * HD, :, :], src).then_inc(sem, 16)
        row += n_rows


def self_attention(p, ctx):
    nc, a = p.nc, p.a
    sb = lambda n, s, dt=F32: p.sb(n, s, dt, ctx)
    u = Units(p, ctx, "sa")
    st = Stages(p, "sa")
    sem = p.sem
    UPR = 2 * DT * NT

    pos = sb("pos", [P, NT, D])
    conv_w = sb("conv_w", [P, DT, CK, D])
    conv_b = sb("conv_b", [G, D])
    gate_w = sb("gate_w", [P, 2 * DT, D])
    gate_b = sb("gate_b", [P, D])
    out_w = sb("out_w", [P, DT, D])
    out_b = sb("out_b", [P, NT, D])
    memory = sb("memory", [P, D])
    w = [sb(f"w{i}", [P, NT, D]) for i in range(2)]
    wT = [sb(f"wT{i}", [P, DT, S]) for i in range(2)]
    wp = [sb(f"wp{i}", [P, 3, DT, S], BF16) for i in range(2)]
    rest = sb("rest", [P, DT, S])
    gT = sb("gT", [P, DT, P])
    gp = sb("gp", [P, 3, DT, P], BF16)
    grest = sb("grest", [P, DT, P])
    qs = [sb(f"qs{i}", [KS, H, S], BF16) for i in range(2)]
    ks = [sb(f"ks{i}", [KS, H, S], BF16) for i in range(2)]
    gs = [sb(f"gs{i}", [KS, H, P], BF16) for i in range(2)]
    gn = sb("gn", [G, D])
    vl = [sb(f"vl{i}", [P, NT, H, 2 * HD]) for i in range(2)]
    vg = [sb(f"vg{i}", [P, H, 2 * HD]) for i in range(2)]
    stats = sb("stats", [P, NT, 6])
    mv = sb("mv", [P, NT, 2])
    rstd = sb("rstd", [P, NT, 1])
    rec = sb("rec", [P, H, 1])
    att = [[sb(f"att{i}{j}", [P, D]) for j in range(2)] for i in range(NT)]
    attT = sb("attT", [P, 2 * DT, P])
    z = sb("z", [P, D])
    tanh = sb("tanh", [P, D])
    diff = sb("diff", [P, D])
    mix = sb("mix", [P, D])
    mixT = sb("mixT", [P, DT, P])
    w_scr = [nc.dram_tensor(f"w_scr{i}", [3, D, S], BF16, kind="Internal").ap() for i in range(2)]
    g_scr = [nc.dram_tensor(f"g_scr{i}", [3, D, P], BF16, kind="Internal").ap() for i in range(2)]
    x_t = a["x"].rearrange("b (n p) d -> p (b n) d", p=P)
    w1_t = a["w1T"].rearrange("e (k p) h -> p (e k) h", p=P)

    def consts(e):
        if e.kind == "sp":
            loads = [(p.ident[:], a["ident"]), (pos[:], a["pos_emb"][0:S].rearrange("(n p) d -> p n d", p=P)),
                     (conv_w[:], a["conv_w"].rearrange("(k p) t o -> p k t o", p=P)),
                     (conv_b[:], a["conv_b"].unsqueeze(0).broadcast_to((G, D))),
                     (gate_w[:], a["gate_w"].rearrange("(k p) o -> p k o", p=P)),
                     (gate_b[:], a["gate_b"].unsqueeze(0).broadcast_to((P, D))),
                     (out_w[:], a["out_w"].rearrange("(k p) o -> p k o", p=P)),
                     (out_b[:, 0, :], a["out_b"].unsqueeze(0).broadcast_to((P, D))),
                     (out_b[:, 1, :], a["out_b"].unsqueeze(0).broadcast_to((P, D))),
                     (memory[G:P, :], a["global_memory"][0])]
            for dst, src in loads:
                e.eng.dma_start(dst, src).then_inc(sem("const"), 16)
            e.n_const = len(loads)
        N_CONST = 16 * 10
        if e.kind == "pool":
            e.eng.memset(p.eps[:, 1:2], 0.0).then_inc(Started.sem, 1)
            e.eng.memset(p.eps[:, 0:1], -0.5).then_inc(sem("set"), 1)
            e.eng.memset(memory[0:G, :], 0.0).then_inc(sem("set"), 1)
            for i in range(2):
                e.eng.memset(vl[i][:], 1.0).then_inc(sem("set"), 1)
                e.eng.memset(vg[i][:], 1.0).then_inc(sem("set"), 1)
            wait(e.eng, sem("const"), N_CONST)
            wait(e.eng, sem("set"), 6)
            for i in range(2):
                e.eng.tensor_copy(vg[i][G:P, :, 0:HD], memory[G:P, :].rearrange("p (h d) -> p h d", d=HD))\
                    .then_inc(sem("set"), 1)
        if e.kind == "dve":
            wait(e.eng, sem("const"), N_CONST)
            e.eng.tensor_scalar(p.neg_ident[:], p.ident[:], -1.0, None, ALU.mult).then_inc(sem("set_dve"), 1)
        if e.kind == "pe":
            wait(e.eng, sem("const"), N_CONST)
            wait(e.eng, sem("set_dve"), 1)
        if e.kind in ("act", "pe", "pool"):
            wait(e.eng, sem("set"), 8)
        if e.kind == "act":
            wait(e.eng, sem("const"), N_CONST)


        def turn(pe):
            for k in range(DT):
                mm = pe.transpose(p.M[:, k * P:(k + 1) * P], memory[:, k * P:(k + 1) * P], p.ident[:])
            return mm

        def copy(act):
            return act.copy(gT[:, :, G:P], p.M[:, 0:DT * P].rearrange("p (k g) -> p k g", k=DT)[:, :, G:P])
        st.run(e, "mem", 0, [], turn, "act", copy)


    def load_x(e, r):
        if e.kind == "sp":
            t = r.lin(NT)
            wait(e.eng, sem("x"), r.lin(32))
            e.eng.dma_start(p.xres[:, bass.ds(t, NT), :], x_t[:, bass.ds(t, NT), :]).then_inc(sem("x"), 16)
            e.eng.dma_start(p.w1s[:, bass.ds(r.lin(1), 1), :], w1_t[:, bass.ds(r.lin(1), 1), :])\
                .then_inc(sem("x"), 16)

    def normalise(e, r):
        if e.kind == "dve":
            wait(e.eng, sem("x"), r.lin(32, 32))
            for n in range(NT):
                e.eng.bn_stats(stats[:, n, :], p.xres[:, bass.ds(r.lin(NT, n), 1), :]).then_inc(sem("stats"), 1)
            wait(e.eng, sem("stats"), r.lin(NT, NT), apart=True)
            for n in range(NT):
                e.eng.bn_aggr(mv[:, n, :], stats[:, n, :]).then_inc(sem("mv"), 1)

    def apply_norm(e, r):
        i = r.par
        if e.kind == "dve":
            wait(e.eng, sem("rstd"), r.lin(2, 2))
            wait(e.eng, sem("wp1"), r.lin(1, -1))
            wait(e.eng, sem("vl"), r.lin(1, -1))
            for n in range(NT):
                e.eng.tensor_scalar(w[i][:, n, :].unsqueeze(1), p.xres[:, bass.ds(r.lin(NT, n), 1), :],
                                    mv[:, n, 0:1], rstd[:, n, :], ALU.subtract, ALU.mult)\
                    .then_inc(sem("norm"), 1)
        if e.kind == "pool":
            wait(e.eng, sem("mv"), r.lin(NT, NT))
            wait(e.eng, sem("norm"), r.lin(NT))
            e.eng.tensor_scalar(rstd[:], mv[:, :, 1:2], EPS, None, ALU.add).then_inc(sem("rstd"), 1)
            wait(e.eng, sem("rstd"), r.lin(2, 1))
            e.eng.tensor_tensor(rstd[:], rstd[:], p.eps[:, 0:1].unsqueeze(1).broadcast_to((P, NT, 1)),
                                ALU.pow).then_inc(sem("rstd"), 1)
            wait(e.eng, sem("norm"), r.lin(NT, NT))
            e.eng.tensor_tensor(w[i][:], w[i][:], pos[:], ALU.add).then_inc(sem("w"), 1)

    def turn_w(e, r):
        i = r.par

        def turn(pe):
            for k in range(DT):
                for n in range(NT):
                    mm = pe.transpose(p.M[:, k * S + n * P:k * S + (n + 1) * P], w[i][:, n, k * P:(k + 1) * P],
                                      p.ident[:])
            return mm

        def copy(act):
            wait(act, sem("ws"), r.lin(3, -3))
            return act.copy(wT[i][:], p.M[:].rearrange("p (k t) -> p k t", k=DT))
        st.run(e, "turn_w", r.lin(1), [(sem("w"), r.lin(1, 1))], turn, "act", copy)
        if e.kind == "act":
            wait(e.eng, st.read("turn_w"), r.lin(1, 1))
            wait(e.eng, sem("w_scr"), r.lin(16, -16))
            e.eng.copy(wp[i][:, 0, :, :], wT[i][:]).then_inc(sem("wp1"), 1)

    def parts_w(e, r):
        i = r.par
        if e.kind == "pool":
            wait(e.eng, sem("wp1"), r.lin(1, 1))
            split_rest(e.eng, wp[i][:, 0, :, :], wT[i][:], rest[:], wp[i][:, 1, :, :], wp[i][:, 2, :, :],
                       sem("ws"), r.lin(3))
            wait(e.eng, u.s_pv, r.lin(UPR, -UPR))
            e.eng.tensor_copy(vl[i][:, :, :, 0:HD], w[i][:].rearrange("p n (h d) -> p n h d", d=HD))\
                .then_inc(sem("vl"), 1)
            xr = p.xres[:, bass.ds(r.lin(NT), NT), :]
            e.eng.tensor_tensor(xr, xr, out_b[:], ALU.add).then_inc(sem("xb"), 1)
        if e.kind == "sp":
            wait(e.eng, sem("ws"), r.lin(3, 3))
            wait(e.eng, sem("stacks"), r.lin(192))
            e.eng.dma_start(w_scr[i].rearrange("c (k p) t -> p c k t", p=P), wp[i][:]).then_inc(sem("w_scr"), 16)
            wait(e.eng, sem("w_scr"), r.lin(16, 16))
            wait(e.eng, u.s_scores, r.lin(UPR, -UPR))
            load_stack(e.eng, qs[i], w_scr[i], Q_SLOTS, sem("stacks"))
            load_stack(e.eng, ks[i], w_scr[i], K_SLOTS, sem("stacks"))

    def compress(e, r):
        i = r.par

        def products(pe):
            taps = [(k, t) for k in range(DT) for t in range(CK)]
            for n, (k, t) in enumerate(taps):
                mm = pe.matmul(p.M[0:G, 0:D], wT[i][:, k, :].rearrange("p (g t) -> p t g", t=CK)[:, t, :],
                               conv_w[:, k, t, :], start=(n == 0), stop=(n == len(taps) - 1))
            return mm

        def add_bias(dve):
            wait(dve, st.written("turn_g"), r.lin(1))
            wait(dve, sem("vg"), r.lin(1))
            return dve.tensor_tensor(gn[:], p.M[0:G, 0:D], conv_b[:], ALU.add)
        st.run(e, "conv", r.lin(1), [(st.read("turn_w"), r.lin(1, 1))], products, "dve", add_bias)
        if e.kind == "pool":
            wait(e.eng, st.read("conv"), r.lin(1, 1))
            wait(e.eng, u.s_pv, r.lin(UPR, -UPR))
            e.eng.tensor_copy(vg[i][0:G, :, 0:HD], gn[:].rearrange("p (h d) -> p h d", d=HD))\
                .then_inc(sem("vg"), 1)

    def turn_g(e, r):
        i = r.par

        def turn(pe):
            for k in range(DT):
                mm = pe.transpose(p.M[:, k * G:(k + 1) * G], gn[:, k * P:(k + 1) * P],
                                  p.ident[0:G, 0:G])
            return mm

        def copy(act):
            wait(act, sem("gs"), r.lin(3))
            return act.copy(gT[:, :, 0:G], p.M[:, 0:DT * G].rearrange("p (k g) -> p k g", k=DT))
        st.run(e, "turn_g", r.lin(1), [(st.read("conv"), r.lin(1, 1))], turn, "act", copy)
        if e.kind == "act":
            wait(e.eng, st.read("turn_g"), r.lin(1, 1))
            wait(e.eng, sem("g_scr"), r.lin(16))
            e.eng.copy(gp[:, 0, :, :], gT[:]).then_inc(sem("gp1"), 1)

    def parts_g(e, r):
        i = r.par
        if e.kind == "pool":
            wait(e.eng, sem("gp1"), r.lin(1, 1))
            split_rest(e.eng, gp[:, 0, :, :], gT[:], grest[:], gp[:, 1, :, :], gp[:, 2, :, :],
                       sem("gs"), r.lin(3))
        if e.kind == "sp":
            wait(e.eng, sem("gs"), r.lin(3, 3))
            wait(e.eng, sem("g_stack"), r.lin(96))
            e.eng.dma_start(g_scr[i].rearrange("c (k p) t -> p c k t", p=P), gp[:]).then_inc(sem("g_scr"), 16)
            wait(e.eng, sem("g_scr"), r.lin(16, 16))
            load_stack(e.eng, gs[i], g_scr[i], K_SLOTS, sem("g_stack"))


    def unit(s):
        return s // 4, s // 2 % 2, s % 2

    def scores(e, r, s):
        n, kind, f = unit(s)
        i = r.par
        if e.kind == "pe":
            if s == 0:
                wait(e.eng, sem("stacks"), r.lin(192, 192))
            if s == 2:
                wait(e.eng, sem("g_stack"), r.lin(96, 96))
            q = lambda h: qs[i][:, f * HU + h, n * P:(n + 1) * P]
            k = (lambda h: gs[i][:, f * HU + h, :]) if kind else (lambda h: ks[i][:, f * HU + h, n * P:(n + 1) * P])
            u.scores(e.eng, r.lin(UPR, s), s % 2, q, k, P)
        if e.kind == "dve":
            u.maxima(e.eng, r.lin(UPR, s), s % 2, P)

    def values(e, r, s):
        n, kind, f = unit(s)
        i = r.par
        if s == 0:
            wait(e.eng, sem("vl"), r.lin(1, 1))
            wait(e.eng, sem("vg"), r.lin(1, 1))
        v = (lambda h: vg[i][:, f * HU + h, :]) if kind else (lambda h: vl[i][:, n, f * HU + h, :])
        u.values(e.eng, r.lin(UPR, s), s % 2, r.lin(UPR // 2, s // 2) if f == 0 else None, f, v, P)


    def turn_back(e, r, n, kind):
        o = r.lin(UPR // 2, 2 * n + kind)

        def turn(pe):
            for g in range(4):
                mm = pe.transpose(p.M[:, g * P:(g + 1) * P], u.outT[kind][:, g, :], p.ident[:])
            return mm

        def divide(dve):
            m = p.M[:].rearrange("p (h d) -> p h d", h=H)
            dve.reciprocal(rec[:], m[:, :, HD:HD + 1]).then_inc(sem("rec"), 1)
            wait(dve, sem("rec"), o + 1)
            if kind == 0:
                wait(dve, sem("mixed"), r.lin(NT, n - 1))
            return dve.tensor_tensor(att[n][kind][:].rearrange("p (h d) -> p h d", d=HD), m[:, :, 0:HD],
                                     rec[:].broadcast_to((P, H, HD)), ALU.mult)
        st.run(e, "back", o, [(u.s_out, o + 1)], turn, "dve", divide)

    def turn_att(e, r, n):
        t = r.lin(NT, n)

        def turn(pe):
            for kind in range(2):
                for k in range(DT):
                    c = (kind * DT + k) * P
                    mm = pe.transpose(p.M[:, c:c + P], att[n][kind][:, k * P:(k + 1) * P], p.ident[:])
            return mm

        def copy(act):
            return act.copy(attT[:], p.M[:].rearrange("p (k t) -> p k t", k=2 * DT))
        st.run(e, "att", t, [(st.read("back"), r.lin(UPR // 2, 2 * n + 2))], turn, "act", copy)

    def gate(e, r, n):
        t = r.lin(NT, n)

        def products(pe):
            for k in range(2 * DT):
                mm = pe.matmul(p.M[:, 0:D], attT[:, k, :], gate_w[:, k, :], start=(k == 0), stop=(k == 2 * DT - 1))
            return mm

        def add_bias(dve):
            wait(dve, sem("tanh"), t)
            return dve.tensor_tensor(z[:], p.M[:, 0:D], gate_b[:], ALU.add)
        st.run(e, "gate", t, [(st.read("att"), t + 1)], products, "dve", add_bias)
        if e.kind == "pool":
            wait(e.eng, st.read("back"), r.lin(UPR // 2, 2 * n + 2))
            wait(e.eng, sem("half"), t)
            e.eng.tensor_tensor(diff[:], att[n][0][:], att[n][1][:], ALU.subtract).then_inc(sem("df"), 1)

    def mix_tile(e, r, n):
        t = r.lin(NT, n)
        if e.kind == "act":
            wait(e.eng, st.read("gate"), t + 1)
            wait(e.eng, sem("half"), t)
            e.eng.activation(tanh[:], z[:], ACT.Tanh, scale=0.5).then_inc(sem("tanh"), 1)
        if e.kind == "dve":
            wait(e.eng, sem("tanh"), t + 1)
            wait(e.eng, sem("df"), t + 1)
            wait(e.eng, st.written("mixT"), t)
            e.eng.scalar_tensor_tensor(mix[:], tanh[:], 1.0, diff[:], ALU.add, ALU.mult).then_inc(sem("half"), 1)
            wait(e.eng, sem("half"), t + 1)
            e.eng.scalar_tensor_tensor(mix[:], mix[:], 0.5, att[n][1][:], ALU.mult, ALU.add)\
                .then_inc(sem("mixed"), 1)

    def turn_mix(e, r, n):
        t = r.lin(NT, n)

        def turn(pe):
            for k in range(DT):
                mm = pe.transpose(p.M[:, k * P:(k + 1) * P], mix[:, k * P:(k + 1) * P], p.ident[:])
            return mm

        def copy(act):
            return act.copy(mixT[:], p.M[:, 0:D].rearrange("p (k t) -> p k t", k=DT))
        st.run(e, "mixT", t, [(sem("mixed"), t + 1)], turn, "act", copy)

    def project(e, r, n):
        t = r.lin(NT, n)

        def products(pe):
            for k in range(DT):
                mm = pe.matmul(p.M[:, 0:D], mixT[:, k, :], out_w[:, k, :], start=(k == 0), stop=(k == DT - 1))
            return mm

        def residual(dve):
            wait(dve, sem("xb"), r.lin(1, 1))
            x = p.xres[:, bass.ds(t, 1), :]
            return dve.tensor_tensor(x, p.M[:, 0:D].unsqueeze(1), x, ALU.add)
        st.run(e, "proj", t, [(st.read("mixT"), t + 1)], products, "dve", residual)


    def prologue(e):
        consts(e)
        r0 = Row(None, 0)
        load_x(e, r0)
        load_x(e, r0.plus(1))
        normalise(e, r0)
        apply_norm(e, r0)
        turn_w(e, r0)
        parts_w(e, r0)
        compress(e, r0)
        turn_g(e, r0)
        parts_g(e, r0)
        scores(e, r0, 0)

    def slot(e, r, s, first, last, drain=False):
        U, nxt, prev = r.lin(UPR, s), r.plus(1), r.plus(-1)
        lag = lambda d: (r, s - d) if s >= d else (prev, s - d + UPR)
        exists = lambda d: s >= d or not first
        done = lambda f, *x: (lambda: None if first else f(e, prev, *x))
        this = lambda f, *x: (lambda: None if drain else f(e, r, *x))
        then = lambda f: (lambda: None if last or drain else f(e, nxt))
        stages = {
            0: [done(turn_back, 1, 0), done(gate, 0)],
            1: [then(turn_w)],
            2: [done(turn_mix, 0), done(turn_back, 1, 1), then(compress)],
            3: [done(project, 0), done(turn_att, 1)],
            4: [then(turn_g), this(turn_back, 0, 0)],
            5: [done(gate, 1)],
            6: [this(turn_back, 0, 1), done(turn_mix, 1)],
            7: [done(project, 1), this(turn_att, 0)],
        }[s] + [lambda: None] * 3
        more = not drain and not (last and s == UPR - 1)
        if s == 0 and not (last or drain):
            normalise(e, nxt)
        k = e.kind
        if k == "dve":
            stages[0]()
        if more:
            scores(e, *((r, s + 1) if s + 1 < UPR else (nxt, 0)))
        if k == "pe":
            stages[0]()
            if not drain:
                u.subtract_max(e.eng, U, s % 2, P)
            if exists(1) and not (drain and s >= 1):
                u.turn(e.eng, *at_unit(lag(1)), P)
            stages[1]()
            if exists(2) and not (drain and s >= 2):
                values(e, *lag(2))
            stages[2]()
            return
        if s == 0 and not (last or drain):
            apply_norm(e, nxt)
        if k != "dve":
            stages[0]()
        if k == "act" and not drain:
            u.exponentials(e.eng, U, s % 2, P)
        if k == "act" and s in (0, 5) and not first:
            mix_tile(e, prev, s // 5)
        if exists(1) and not (drain and s >= 1) and k in ("act", "dve"):
            u.evacuate(e.eng, 0 if k == "act" else 1, *at_unit(lag(1)), P)
        stages[1]()
        if k == "act" and s % 2 == 1 and exists(2) and not (drain and s >= 2):
            rr, ss = lag(2)
            u.out_copy(e.eng, rr.lin(UPR, ss), rr.lin(UPR // 2, ss // 2), ss // 2 % 2, st.written("back"))
        stages[2]()
        if k == "dve" and s in (1, 5) and not first:
            mix_tile(e, prev, s // 5)
        if s == 1 and not (last or drain):
            parts_w(e, nxt)
        if s == 5 and not (last or drain):
            parts_g(e, nxt)

    def at_unit(x):
        r, s = x
        return r.lin(UPR, s), s % 2

    def row(e, r, first, last):
        if e.kind == "sp":
            if not last:
                if not (r.reg is None and r.off >= NB - 2):
                    load_x(e, r.plus(2))
                parts_w(e, r.plus(1))
                parts_g(e, r.plus(1))
            return
        e.free = [(st.read("turn_g"), 1) if first else (st.read("att"), r.lin(NT, -1))]
        for s in range(UPR):
            slot(e, r, s, first, last)

    def epilogue(e, r):
        if e.kind == "sp":
            return
        e.free = [(st.read("att"), r.lin(NT, -1))]
        for s in range(UPR):
            slot(e, r, s, False, True, drain=True)

    on_engines(nc, lambda e: rows_of(e, NB, prologue, row, epilogue))



def cross_attention(p, ctx):
    nc, a = p.nc, p.a
    sb = lambda n, s, dt=F32: p.sb(n, s, dt, ctx)
    u = Units(p, ctx, "xa")
    st = Stages(p, "xa")
    sem = lambda n: p.sem("xa_" + n)
    UPR = DT * NT

    wt = {n: sb(n + "_sb", [P, DT, D]) for n in ("WqT", "WkT", "WvT", "WoT")}
    masked_score = sb("masked_score", [P, 1])
    xn = sb("xn", [P, NT, D])
    nT = sb("nT", [P, DT, S])
    ctx_n = [sb(f"ctx_n{i}", [KX, D]) for i in range(2)]
    cT = [sb(f"cT{i}", [P, DT, KX]) for i in range(2)]
    qT = sb("qT", [P, DT, S])
    qp = sb("qp", [P, 3, DT, S], BF16)
    kT = sb("kT", [P, DT, KX])
    kp = sb("kp", [P, 3, DT, KX], BF16)
    rest = sb("xrest", [P, DT, S])
    qs = [sb(f"xqs{i}", [KS, H, S], BF16) for i in range(2)]
    ks = [sb(f"xks{i}", [KS, H, KX], BF16) for i in range(2)]
    vx = [sb(f"vx{i}", [KX, H, 2 * HD]) for i in range(2)]
    mask = [sb(f"mask{i}", [P, NT, KX], I32) for i in range(2)]
    zero = [sb(f"zero{i}", [P, NT, KX], I32) for i in range(2)]
    stats = sb("xstats", [P, NT, 6])
    mv = sb("xmv", [P, NT, 2])
    rstd = sb("xrstd", [P, NT, 1])
    rec = sb("xrec", [P, H, 1])
    att = sb("xatt", [P, D])
    attT = sb("xattT", [P, DT, P])
    q_scr = [nc.dram_tensor(f"q_scr{i}", [3, D, S], BF16, kind="Internal").ap() for i in range(2)]
    k_scr = [nc.dram_tensor(f"k_scr{i}", [3, D, KX], BF16, kind="Internal").ap() for i in range(2)]
    ctx_t = a["ctx"].rearrange("b k d -> k b d")
    mask_t = a["mask"].rearrange("b (n p) k -> p (b n) k", p=P)
    w3_t = a["w3T"].rearrange("e (k p) h -> p (e k) h", p=P)
    w2_t = a["w2T"].rearrange("e (k p) d -> p (e k) d", p=P)

    def consts(e):
        N_CONST = 16 * 4
        if e.kind == "sp":
            for n in ("WqT", "WkT", "WvT", "WoT"):
                e.eng.dma_start(wt[n][:], a[n].rearrange("(k p) o -> p k o", p=P)).then_inc(sem("const"), 16)
            wait(e.eng, sem("set"), 3)
        if e.kind == "pool":
            e.eng.memset(masked_score[:], 1e-9 / SCALE).then_inc(sem("set"), 1)
            for i in range(2):
                e.eng.memset(vx[i][:], 1.0).then_inc(sem("set"), 1)
            wait(e.eng, sem("set"), 3)
        if e.kind in ("dve", "act"):
            wait(e.eng, sem("set"), 3)
        if e.kind == "pe":
            wait(e.eng, sem("const"), N_CONST)
            wait(e.eng, sem("set"), 3)

    def load(e, r):
        if e.kind == "sp":
            i = r.par
            wait(e.eng, sem("in"), r.lin(64))
            wait(e.eng, st.written("turn_c"), r.lin(1, -1))
            wait(e.eng, sem("zero"), r.lin(1, -1))
            e.eng.dma_start(ctx_n[i][:].unsqueeze(1), ctx_t[:, bass.ds(r.lin(1), 1), :]).then_inc(sem("in"), 16)
            e.eng.dma_start(mask[i][:], mask_t[:, bass.ds(r.lin(NT), NT), :]).then_inc(sem("in"), 16)
            e.eng.dma_start(p.w3s[:, bass.ds(r.lin(1), 1), :], w3_t[:, bass.ds(r.lin(1), 1), :])\
                .then_inc(sem("in"), 16)
            e.eng.dma_start(p.w2s[:, bass.ds(r.lin(2), 2), :], w2_t[:, bass.ds(r.lin(2), 2), :])\
                .then_inc(sem("in"), 16)

    def normalise(e, r):
        if e.kind == "dve":
            for n in range(NT):
                e.eng.bn_stats(stats[:, n, :], p.xres[:, bass.ds(r.lin(NT, n), 1), :]).then_inc(sem("stats"), 1)
            wait(e.eng, sem("stats"), r.lin(NT, NT), apart=True)
            for n in range(NT):
                e.eng.bn_aggr(mv[:, n, :], stats[:, n, :]).then_inc(sem("mv"), 1)
        if e.kind == "pool":
            wait(e.eng, sem("mv"), r.lin(NT, NT))
            wait(e.eng, sem("norm"), r.lin(NT))
            e.eng.tensor_scalar(rstd[:], mv[:, :, 1:2], EPS, None, ALU.add).then_inc(sem("rstd"), 1)
            wait(e.eng, sem("rstd"), r.lin(2, 1))
            e.eng.tensor_tensor(rstd[:], rstd[:], p.eps[:, 0:1].unsqueeze(1).broadcast_to((P, NT, 1)),
                                ALU.pow).then_inc(sem("rstd"), 1)

    def make_zero(e, r):
        if e.kind == "pool":
            wait(e.eng, sem("in"), r.lin(64, 64))
            wait(e.eng, u.s_masked, r.lin(UPR, -UPR))
            e.eng.tensor_scalar(zero[r.par][:], mask[r.par][:], 0.0, None, ALU.is_equal).then_inc(sem("zero"), 1)

    def apply_norm(e, r):
        if e.kind == "dve":
            wait(e.eng, sem("rstd"), r.lin(2, 2))
            wait(e.eng, st.written("turn_n"), r.lin(1))
            for n in range(NT):
                e.eng.tensor_scalar(xn[:, n, :].unsqueeze(1), p.xres[:, bass.ds(r.lin(NT, n), 1), :],
                                    mv[:, n, 0:1], rstd[:, n, :], ALU.subtract, ALU.mult)\
                    .then_inc(sem("norm"), 1)

    def turn_n(e, r):
        def turn(pe):
            for k in range(DT):
                for n in range(NT):
                    mm = pe.transpose(p.M[:, k * S + n * P:k * S + (n + 1) * P], xn[:, n, k * P:(k + 1) * P],
                                      p.ident[:])
            return mm

        def copy(act):
            return act.copy(nT[:], p.M[:].rearrange("p (k t) -> p k t", k=DT))
        st.run(e, "turn_n", r.lin(1), [(sem("norm"), r.lin(NT, NT))], turn, "act", copy)

    def turn_c(e, r):
        i = r.par

        def turn(pe):
            for k in range(DT):
                mm = pe.transpose(p.M[:, k * KX:(k + 1) * KX], ctx_n[i][:, k * P:(k + 1) * P],
                                  p.ident[0:KX, 0:KX])
            return mm

        def copy(act):
            return act.copy(cT[i][:], p.M[:, 0:DT * KX].rearrange("p (k t) -> p k t", k=DT))
        st.run(e, "turn_c", r.lin(1), [(sem("in"), r.lin(64, 64))], turn, "act", copy)

    def features(pe, weights, xT, n):
        for o in range(DT):
            for k in range(DT):
                mm = pe.matmul(p.M[:, o * n:(o + 1) * n], weights[:, k, o * P:(o + 1) * P], xT[:, k, :],
                               start=(k == 0), stop=(k == DT - 1))
        return mm

    def queries(e, r):
        def copy(act):
            wait(act, sem("qp"), r.lin(3))
            return act.copy(qT[:], p.M[:].rearrange("p (k t) -> p k t", k=DT))
        st.run(e, "q", r.lin(1), [(st.read("turn_n"), r.lin(1, 1))],
               lambda pe: features(pe, wt["WqT"], nT, S), "act", copy)
        if e.kind == "act":
            wait(e.eng, st.read("q"), r.lin(1, 1))
            wait(e.eng, sem("q_scr"), r.lin(16))
            e.eng.copy(qp[:, 0, :, :], qT[:]).then_inc(sem("qp1"), 1)

    def keys(e, r):
        i = r.par

        def copy(act):
            wait(act, sem("kp"), r.lin(3))
            return act.copy(kT[:], p.M[:, 0:DT * KX].rearrange("p (k t) -> p k t", k=DT))
        st.run(e, "k", r.lin(1), [(st.read("turn_c"), r.lin(1, 1))],
               lambda pe: features(pe, wt["WkT"], cT[i], KX), "act", copy)
        if e.kind == "act":
            wait(e.eng, st.read("k"), r.lin(1, 1))
            wait(e.eng, sem("k_scr"), r.lin(16))
            e.eng.copy(kp[:, 0, :, :], kT[:]).then_inc(sem("kp1"), 1)

    def parts(e, r):
        i = r.par
        if e.kind == "pool":
            wait(e.eng, sem("qp1"), r.lin(1, 1))
            wait(e.eng, sem("kp"), r.lin(3))
            split_rest(e.eng, qp[:, 0, :, :], qT[:], rest[:], qp[:, 1, :, :], qp[:, 2, :, :], sem("qp"), r.lin(3))
            wait(e.eng, sem("kp1"), r.lin(1, 1))
            wait(e.eng, sem("qp"), r.lin(3, 3))
            split_rest(e.eng, kp[:, 0, :, :], kT[:], rest[:, :, 0:KX], kp[:, 1, :, :], kp[:, 2, :, :],
                       sem("kp"), r.lin(3))
        if e.kind == "sp":
            wait(e.eng, sem("qp"), r.lin(3, 3))
            wait(e.eng, sem("stacks"), r.lin(192))
            e.eng.dma_start(q_scr[i].rearrange("c (k p) t -> p c k t", p=P), qp[:]).then_inc(sem("q_scr"), 16)
            wait(e.eng, sem("kp"), r.lin(3, 3))
            e.eng.dma_start(k_scr[i].rearrange("c (k p) t -> p c k t", p=P), kp[:]).then_inc(sem("k_scr"), 16)
            wait(e.eng, u.s_scores, r.lin(UPR, -UPR))
            wait(e.eng, sem("q_scr"), r.lin(16, 16))
            load_stack(e.eng, qs[i], q_scr[i], Q_SLOTS, sem("stacks"))
            wait(e.eng, sem("k_scr"), r.lin(16, 16))
            load_stack(e.eng, ks[i], k_scr[i], K_SLOTS, sem("stacks"))

    def make_values(e, r):
        i = r.par

        def products(pe):
            for k in range(DT):
                mm = pe.matmul(p.M[0:KX, 0:D], cT[i][:, k, :], wt["WvT"][:, k, :], start=(k == 0),
                               stop=(k == DT - 1))
            return mm

        def copy(act):
            wait(act, u.s_pv, r.lin(UPR, -UPR))
            return act.copy(vx[i][:, :, 0:HD], p.M[0:KX, 0:D].rearrange("p (h d) -> p h d", d=HD))
        st.run(e, "v", r.lin(1), [(st.read("turn_c"), r.lin(1, 1))], products, "act", copy)

    def scores(e, r, s):
        n, f = s // DT, s % DT
        i = r.par
        if e.kind == "pe":
            if s == 0:
                wait(e.eng, sem("stacks"), r.lin(192, 192))
            u.scores(e.eng, r.lin(UPR, s), s % 2, lambda h: qs[i][:, f * HU + h, n * P:(n + 1) * P],
                     lambda h: ks[i][:, f * HU + h, :], KX)
        if e.kind == "dve":
            if s == 0:
                wait(e.eng, sem("zero"), r.lin(1, 1), apart=True)
            u.maxima(e.eng, r.lin(UPR, s), s % 2, KX, (zero[i][:, n, :], masked_score[:]))

    def values(e, r, s):
        f = s % DT
        if s == 0:
            wait(e.eng, st.read("v"), r.lin(1, 1))
        u.values(e.eng, r.lin(UPR, s), s % 2, r.lin(UPR // 2, s // 2) if f == 0 else None, f,
                 lambda h: vx[r.par][:, f * HU + h, :], KX)

    def turn_back(e, r, n):
        t = r.lin(NT, n)

        def turn(pe):
            for g in range(4):
                mm = pe.transpose(p.M[:, g * P:(g + 1) * P], u.outT[n][:, g, :], p.ident[:])
            return mm

        def divide(dve):
            m = p.M[:].rearrange("p (h d) -> p h d", h=H)
            dve.reciprocal(rec[:], m[:, :, HD:HD + 1]).then_inc(sem("rec"), 1)
            wait(dve, sem("rec"), t + 1)
            wait(dve, st.written("att"), t)
            return dve.tensor_tensor(att[:].rearrange("p (h d) -> p h d", d=HD), m[:, :, 0:HD],
                                     rec[:].broadcast_to((P, H, HD)), ALU.mult)
        st.run(e, "back", t, [(u.s_out, t + 1)], turn, "dve", divide)

    def turn_att(e, r, n):
        t = r.lin(NT, n)

        def turn(pe):
            for k in range(DT):
                mm = pe.transpose(p.M[:, k * P:(k + 1) * P], att[:, k * P:(k + 1) * P], p.ident[:])
            return mm

        def copy(act):
            return act.copy(attT[:], p.M[:, 0:D].rearrange("p (k t) -> p k t", k=DT))
        st.run(e, "att", t, [(st.read("back"), t + 1)], turn, "act", copy)

    def project(e, r, n):
        t = r.lin(NT, n)

        def products(pe):
            for k in range(DT):
                mm = pe.matmul(p.M[:, 0:D], attT[:, k, :], wt["WoT"][:, k, :], start=(k == 0), stop=(k == DT - 1))
            return mm

        def residual(dve):
            x = p.xres[:, bass.ds(t, 1), :]
            return dve.tensor_tensor(x, p.M[:, 0:D].unsqueeze(1), x, ALU.add)
        st.run(e, "proj", t, [(st.read("att"), t + 1)], products, "dve", residual)

    def prepare(e, r):
        turn_n(e, r)
        turn_c(e, r)
        queries(e, r)
        keys(e, r)
        parts(e, r)
        make_zero(e, r)
        load(e, r.plus(1))
        normalise(e, r.plus(1))
        apply_norm(e, r.plus(1))

    def prologue(e):
        consts(e)
        load(e, Row(None, 0))
        normalise(e, Row(None, 0))
        apply_norm(e, Row(None, 0))
        prepare(e, Row(None, 0))
        make_values(e, Row(None, 0))
        prepare(e, Row(None, 1))
        scores(e, Row(None, 0), 0)

    def lag(r, s, d):
        return (r, s - d) if s >= d else (r.plus(-1), s - d + UPR)

    def at_unit(x):
        return x[0].lin(UPR, x[1]), x[1] % 2

    def slot(e, r, s, first, ahead, ahead3, last, drain=False):
        U, nxt, nxt2, prev = r.lin(UPR, s), r.plus(1), r.plus(2), r.plus(-1)
        exists = lambda d: s >= d or not first
        done = lambda f, *x: (lambda: None if first else f(e, prev, *x))
        then = lambda f, row, ok: (lambda: f(e, row) if ok else None)
        stages = {
            0: [done(turn_back, 0), then(turn_n, nxt2, ahead)],
            1: [done(turn_att, 0), then(queries, nxt2, ahead), then(turn_c, nxt2, ahead)],
            2: [done(project, 0), then(keys, nxt2, ahead), done(turn_back, 1)],
            3: [done(turn_att, 1), then(make_values, nxt, not (last or drain)), done(project, 1)],
        }[s] + [lambda: None]
        k = e.kind
        if s == 1 and ahead3:
            normalise(e, r.plus(3))
        if k == "dve":
            stages[0]()
        if not drain and not (last and s == UPR - 1):
            scores(e, *((r, s + 1) if s + 1 < UPR else (nxt, 0)))
        if s == 2 and ahead3:
            apply_norm(e, r.plus(3))
        if k != "dve":
            stages[0]()
        if k == "act" and not drain:
            u.exponentials(e.eng, U, s % 2, KX)
        if k == "pe" and not drain:
            u.subtract_max(e.eng, U, s % 2, KX)
        if exists(1) and not (drain and s >= 1):
            if k == "pe":
                u.turn(e.eng, *at_unit(lag(r, s, 1)), KX)
            if k in ("act", "dve"):
                u.evacuate(e.eng, 0 if k == "act" else 1, *at_unit(lag(r, s, 1)), KX)
        stages[1]()
        if exists(2) and not (drain and s >= 2):
            rr, ss = lag(r, s, 2)
            if k == "pe":
                values(e, rr, ss)
            if k == "act" and s % 2 == 1:
                u.out_copy(e.eng, rr.lin(UPR, ss), rr.lin(UPR // 2, ss // 2), ss // 2 % 2, st.written("back"))
        stages[2]()
        if s == 1 and ahead:
            parts(e, nxt2)
        if s == 2 and ahead:
            make_zero(e, nxt2)

    def row(e, r, first, last):
        ahead = not (r.reg is None and r.off >= NB - 2)
        ahead3 = not (r.reg is None and r.off >= NB - 3)
        if e.kind == "sp":
            if ahead3:
                load(e, r.plus(3))
            if ahead:
                parts(e, r.plus(2))
            return
        if not first:
            e.free = [(st.read("v"), r.lin(1, 1)), (st.read("proj"), r.lin(NT, -NT))]
        for s in range(UPR):
            slot(e, r, s, first, ahead, ahead3, last)

    def epilogue(e, r):
        if e.kind != "sp":
            for s in range(UPR):
                slot(e, r, s, False, False, False, True, drain=True)

    on_engines(nc, lambda e: rows_of(e, NB, prologue, row, epilogue))



GROUP = 16
SPARE = TOKENS + 1


def experts(p, ctx):
    nc = p.nc
    slot_row = p.sb("slot_row", [P, N_ST], I32, ctx)
    slot_share = p.sb("slot_share", [P, N_ST], ctx=ctx)
    tile_expert = p.sb("tile_expert", [1, N_ST], I32, ctx)
    xn_dram = nc.dram_tensor("xn_rows", [TOKENS + P, D], F32, kind="Internal").ap()
    sum_dram = nc.dram_tensor("sum_rows", [TOKENS + P, D], F32, kind="Internal").ap()
    with ExitStack() as c:
        route(p, c, xn_dram, sum_dram, slot_row, slot_share, tile_expert)
    with ExitStack() as c:
        expert_tiles(p, c, xn_dram, sum_dram, slot_row, slot_share, tile_expert)
    with nc.Block() as block:
        @block.sync
        def _(sp):
            out = p.a["out"].rearrange("b s d -> (b s) d").rearrange("(q n) d -> q (n d)", q=P)
            sums = sum_dram[0:TOKENS, :].rearrange("(q n) d -> q (n d)", q=P)
            sp.dma_start(out, sums).then_inc(p.sem("out"), 16)
            sp.wait_ge(p.sem("out"), 16)


def route(p, ctx, xn_dram, sum_dram, slot_row, slot_share, tile_expert):
    nc, a = p.nc, p.a
    sb = lambda n, s, dt=F32: p.sb(n, s, dt, ctx)
    sem = lambda n: p.sem("rt_" + n)
    xb = [sb(f"xb{i}", [P, NT, D]) for i in range(2)]
    nT = [sb(f"rnT{i}", [P, DT, S]) for i in range(2)]
    routerT = sb("routerT_sb", [P, DT, E])
    before = sb("before_sb", [P, P])
    ones = sb("ones", [P, P])
    zeros = sb("zeros", [P, D])
    iota_e = sb("iota_e_sb", [P, E])
    iota_t = sb("iota_t_sb", [P, N_ST])
    iota_p = sb("iota_p_sb", [P, P])
    token1 = sb("token1_sb", [P, TILES])
    spare = sb("spare_sb", [P, 1])
    stats = [sb(f"rstats{i}", [P, NT, 6]) for i in range(2)]
    mv = [sb(f"rmv{i}", [P, NT, 2]) for i in range(2)]
    rstd = [sb(f"rrstd{i}", [P, NT, 1]) for i in range(2)]
    t8 = lambda n, dt=F32: sb(n, [P, TILES, E], dt)
    prob, top, sel, posn, tmp = (t8(n) for n in ("prob", "top", "sel", "posn", "tmp"))
    hot = [t8("hot0"), t8("hot1")]
    scan = [t8("scan0"), t8("scan1")]
    top_id = t8("top_id", U32)
    tile1 = sb("tile1", [P, TILES, 1])
    idf = sb("idf", [P, TILES, TOP])
    share = sb("share", [P, TOP, TILES])
    slotf = sb("slotf", [P, TOP, TILES, 1])
    slot_i, part_i = (sb(n, [P, TOP, TILES], I32) for n in ("slot_i", "part_i"))
    slot_tile, slot_lane = (sb(n, [P, TOP, TILES]) for n in ("slot_tile", "slot_lane"))
    count_i = sb("count_i", [P, E], I32)
    tiles_i = sb("tiles_i", [P, E], I32)
    tiles_e, starts = sb("tiles_e", [P, E]), sb("starts", [P, E])
    cum = [sb("cum0", [P, E]), sb("cum1", [P, E])]
    passed = sb("passed", [1, N_ST, E])
    expert_f = sb("expert_f", [1, N_ST, 1])
    lane_hot = [sb(f"lane_hot{i}", [P, GROUP, P]) for i in range(2)]
    tile_hot = [sb(f"tile_hot{i}", [P, GROUP, N_ST]) for i in range(2)]
    entry = [sb(f"entry{i}", [P, GROUP, 2, N_ST]) for i in range(2)]
    empty = sb("empty", [P, N_ST])
    xn_t = xn_dram[0:TOKENS, :].rearrange("(t p) d -> p t d", p=P)
    sum_t = sum_dram[0:TOKENS, :].rearrange("(t p) d -> p t d", p=P)

    def walk(e):
        if e.kind == "sp":
            wide = lambda n: a[n].unsqueeze(0).broadcast_to((P, a[n].shape[0]))
            for dst, src in ((routerT[:], a["routerT"].rearrange("(k p) e -> p k e", p=P)),
                             (before[:], a["before"]), (iota_e[:], wide("iota_e")), (iota_t[:], wide("iota_t")),
                             (iota_p[:], wide("iota_p")), (token1[:], a["token1"]), (spare[:], a["spare"])):
                e.eng.dma_start(dst, src).then_inc(sem("const"), 16)
        if e.kind == "pool":
            e.eng.memset(zeros[:], 0.0).then_inc(sem("set"), 1)
            e.eng.memset(ones[:], 1.0).then_inc(sem("set"), 1)
        if e.kind in ("pe", "dve"):
            wait(e.eng, sem("const"), 7 * 16)
            wait(e.eng, sem("set"), 2)
        statistics(e, Row(None, 0))
        for n in range(FIRST):
            row(e, Row(None, n))
        with e.eng.Fori(FIRST, NB - 2, 2) as r:
            row(e, Row(r, 0, FIRST % 2))
            row(e, Row(r, 1, 1 - FIRST % 2))
        row(e, Row(None, NB - 1), last=True)
        assign(e)
        if e.kind == "sp":
            wait(e.eng, sem("set"), 2)
            e.eng.dma_start(sum_t, p.xres[:]).then_inc(sem("sums"), 16)
            e.eng.dma_start(sum_dram[TOKENS:, :], zeros[:]).then_inc(sem("sums"), 16)
            e.eng.dma_start(xn_dram[TOKENS:, :], zeros[:]).then_inc(sem("sums"), 16)
            for i in range(2):
                wait(e.eng, sem(f"stored{i}"), 16 * NB // 2)
            wait(e.eng, sem("sums"), 48)

    def statistics(e, r):
        i = r.par
        if e.kind == "dve":
            wait(e.eng, sem("norm"), r.lin(NT, -NT))
            for n in range(NT):
                e.eng.bn_stats(stats[i][:, n, :], p.xres[:, bass.ds(r.lin(NT, n), 1), :]).then_inc(sem("stats"), 1)
            wait(e.eng, sem("stats"), r.lin(NT, NT), apart=True)
            for n in range(NT):
                e.eng.bn_aggr(mv[i][:, n, :], stats[i][:, n, :]).then_inc(sem("mv"), 1)
        if e.kind == "pool":
            wait(e.eng, sem("mv"), r.lin(NT, NT))
            wait(e.eng, sem("norm"), r.lin(NT, -NT))
            e.eng.tensor_scalar(rstd[i][:], mv[i][:, :, 1:2], EPS, None, ALU.add).then_inc(sem("rstd"), 1)
            wait(e.eng, sem("rstd"), r.lin(2, 1))
            e.eng.tensor_tensor(rstd[i][:], rstd[i][:], p.eps[:, 0:1].unsqueeze(1).broadcast_to((P, NT, 1)),
                                ALU.pow).then_inc(sem("rstd"), 1)

    def row(e, r, last=False):
        i = r.par
        if not last:
            statistics(e, r.plus(1))
        if e.kind == "dve":
            wait(e.eng, sem("rstd"), r.lin(2, 2))
            wait(e.eng, sem("turn"), r.lin(1, -1))
            wait(e.eng, sem(f"stored{i}"), r.lin(8, -8 * i))
            for n in range(NT):
                e.eng.tensor_scalar(xb[i][:, n:n + 1, :], p.xres[:, bass.ds(r.lin(NT, n), 1), :], mv[i][:, n, 0:1],
                                    rstd[i][:, n, :], ALU.subtract, ALU.mult).then_inc(sem("norm"), 1)
        if e.kind == "sp":
            wait(e.eng, sem("norm"), r.lin(NT, NT))
            wait(e.eng, sem(f"stored{i}"), r.lin(8, -8 * i))
            e.eng.dma_start(xn_t[:, bass.ds(r.lin(NT), NT), :], xb[i][:]).then_inc(sem(f"stored{i}"), 16)
        if e.kind == "pe":
            wait(e.eng, sem("norm"), r.lin(NT, NT))
            wait(e.eng, sem("nT"), r.lin(1, -1))
            for k in range(DT):
                for n in range(NT):
                    mm = e.eng.transpose(p.T[i][:, k * NT + n, :], xb[i][:, n, k * P:(k + 1) * P], p.ident[:])
            mm.then_inc(sem("turn"), 1)
            wait(e.eng, sem("nT"), r.lin(1, 1))
            out = p.O[:].rearrange("p a b -> p (a b)")
            for n in range(NT):
                for k in range(DT):
                    mm = e.eng.matmul(out[:, bass.ds(r.lin(NT * E, n * E), E)], nT[i][:, k, n * P:(n + 1) * P],
                                      routerT[:, k, :], start=(k == 0), stop=(k == DT - 1), skip_group_check=True)
            mm.then_inc(sem("logits"), 1)
        if e.kind == "act":
            wait(e.eng, sem("turn"), r.lin(1, 1))
            wait(e.eng, sem("logits"), r.lin(1, -1))
            e.eng.copy(nT[i][:], p.T[i][:].rearrange("p (k n) t -> p k (n t)", k=DT)).then_inc(sem("nT"), 1)

    def assign(e):
        flat = lambda x: x[:].rearrange("p t e -> p (t e)")
        wide = lambda x: x.unsqueeze(1).broadcast_to((P, TILES, E))
        counts = lambda x: x[:, 0:TILES * E].rearrange("p (t e) -> p t e", e=E)
        bank = lambda x: x[:].rearrange("p a b -> p (a b)")
        v = e.eng
        steps = 0

        def step(ins):
            nonlocal steps
            steps += 1
            ins.then_inc(sem("step"), 1)
            wait(v, sem("step"), steps)

        if e.kind == "dve":
            wait(v, sem("logits"), NB)
            logits = counts(bank(p.O))
            step(v.tensor_reduce(tile1[:], logits, AX_X, ALU.max))
            step(v.tensor_tensor(tmp[:], logits, tile1[:].broadcast_to((P, TILES, E)), ALU.subtract))
        if e.kind == "act":
            wait(e.eng, sem("step"), 2)
            e.eng.activation(prob[:], tmp[:], ACT.Exp).then_inc(sem("exp"), 1)
        if e.kind == "dve":
            wait(v, sem("exp"), 1)
            step(v.tensor_reduce(tile1[:], prob[:], AX_X, ALU.add))
            step(v.reciprocal(tile1[:], tile1[:]))
            step(v.tensor_tensor(prob[:], prob[:], tile1[:].broadcast_to((P, TILES, E)), ALU.mult))
            for t in range(TILES):
                ins = v.max(top[:, t, :], prob[:, t, :])
            step(ins)
            for t in range(TILES):
                ins = v.max_index(top_id[:, t, :], top[:, t, :], prob[:, t, :])
            step(ins)
            step(v.tensor_tensor(tile1[:], top[:, :, 0:1], top[:, :, 1:2], ALU.add))
            step(v.reciprocal(tile1[:], tile1[:]))
            for j in range(TOP):
                step(v.tensor_tensor(share[:, j, :].unsqueeze(2), top[:, :, j:j + 1], tile1[:], ALU.mult))
            step(v.tensor_copy(idf[:], top_id[:, :, 0:TOP]))
            for j in range(TOP):
                step(v.tensor_tensor(hot[j][:], wide(iota_e[:]), idf[:, :, j:j + 1].broadcast_to((P, TILES, E)),
                                     ALU.is_equal))
            v.tensor_tensor(sel[:], hot[0][:], hot[1][:], ALU.add).then_inc(sem("sel"), 1)
        if e.kind == "pe":
            wait(e.eng, sem("sel"), 1)
            e.eng.matmul(p.M[:, 0:TILES * E], before[:], flat(sel), start=True, stop=True)
            e.eng.matmul(bank(p.T[0])[:, 0:TILES * E], ones[:], flat(sel), start=True,
                         stop=True).then_inc(sem("count"), 1)
        if e.kind == "dve":
            total, prefix = counts(bank(p.T[0])), counts(p.M)
            wait(v, sem("count"), 1)
            step(v.tensor_copy(scan[0][:], total))
            cur, d = 0, 1
            while d < TILES:
                step(v.tensor_copy(scan[1 - cur][:, 0:d, :], scan[cur][:, 0:d, :]))
                step(v.tensor_tensor(scan[1 - cur][:, d:, :], scan[cur][:, d:, :], scan[cur][:, 0:TILES - d, :],
                                     ALU.add))
                cur, d = 1 - cur, 2 * d
            step(v.tensor_scalar(count_i[:], scan[cur][:, TILES - 1, :], float(P - 1), None, ALU.add))
            step(v.tensor_scalar(tiles_i[:], count_i[:], P.bit_length() - 1, None, ALU.logical_shift_right))
            step(v.tensor_copy(tiles_e[:], tiles_i[:]))
            step(v.tensor_copy(cum[0][:], tiles_e[:]))
            c, d = 0, 1
            while d < E:
                step(v.tensor_copy(cum[1 - c][:, 0:d], cum[c][:, 0:d]))
                step(v.tensor_tensor(cum[1 - c][:, d:], cum[c][:, d:], cum[c][:, 0:E - d], ALU.add))
                c, d = 1 - c, 2 * d
            step(v.tensor_tensor(starts[:], cum[c][:], tiles_e[:], ALU.subtract))
            step(v.tensor_scalar(starts[:], starts[:], float(P), None, ALU.mult))
            step(v.tensor_tensor(posn[:], scan[cur][:], total, ALU.subtract))
            step(v.tensor_tensor(posn[:], posn[:], prefix, ALU.add))
            step(v.tensor_tensor(posn[:], posn[:], wide(starts[:]), ALU.add))
            for j in range(TOP):
                step(v.tensor_tensor(tmp[:], posn[:], hot[j][:], ALU.mult))
                step(v.tensor_reduce(slotf[:, j, :, :], tmp[:], AX_X, ALU.add))
            step(v.tensor_copy(slot_i[:], slotf[:].rearrange("p j t o -> p j (t o)")))
            step(v.tensor_scalar(part_i[:], slot_i[:], P.bit_length() - 1, None, ALU.logical_shift_right))
            step(v.tensor_copy(slot_tile[:], part_i[:]))
            step(v.scalar_tensor_tensor(slot_lane[:], slot_tile[:], -float(P), slotf[:].rearrange("p j t o -> p j (t o)"),
                                        ALU.mult, ALU.add))
            step(v.tensor_tensor(passed[:], iota_t[0:1, :].unsqueeze(2).broadcast_to((1, N_ST, E)),
                                 cum[c][0:1, :].unsqueeze(1).broadcast_to((1, N_ST, E)), ALU.is_ge))
            step(v.tensor_reduce(expert_f[:], passed[:], AX_X, ALU.add))
            step(v.tensor_scalar(tile_expert[:].unsqueeze(2), expert_f[:], float(E - 1), None, ALU.min))
        flat2 = lambda x: x[:].rearrange("p j t -> p (j t)")
        tokens_ps = bank(p.T[1])[:, 0:2 * N_ST]
        n_groups = TOP * TILES // GROUP
        for g in range(n_groups):
            b, c0 = g % 2, g * GROUP
            t0 = c0 % TILES
            if e.kind == "dve":
                spread = lambda x, c, n: x[:, c:c + GROUP].unsqueeze(2).broadcast_to((P, GROUP, n))
                same = lambda x, n: x[:].unsqueeze(1).broadcast_to((P, GROUP, n))
                wait(v, sem("placed"), g - 1)
                v.tensor_tensor(lane_hot[b][:], same(iota_p, P), spread(flat2(slot_lane), c0, P), ALU.is_equal)\
                    .then_inc(sem("hot"), 1)
                v.tensor_tensor(tile_hot[b][:], same(iota_t, N_ST), spread(flat2(slot_tile), c0, N_ST),
                                ALU.is_equal).then_inc(sem("hot"), 1)
                wait(v, sem("hot"), 4 * g + 2)
                v.tensor_tensor(entry[b][:, :, 0, :], tile_hot[b][:], spread(token1, t0, N_ST), ALU.mult)\
                    .then_inc(sem("hot"), 1)
                v.tensor_tensor(entry[b][:, :, 1, :], tile_hot[b][:], spread(flat2(share), c0, N_ST), ALU.mult)\
                    .then_inc(sem("hot"), 1)
            if e.kind == "pe":
                wait(e.eng, sem("hot"), 4 * g + 4)
                for c in range(GROUP):
                    mm = e.eng.matmul(tokens_ps, lane_hot[b][:, c, :], entry[b][:, c, :, :],
                                      start=(g == 0 and c == 0), stop=(g == n_groups - 1 and c == GROUP - 1))
                mm.then_inc(sem("placed"), 1)
        if e.kind == "dve":
            wait(v, sem("placed"), n_groups)
            numbers = tokens_ps[:, 0:N_ST]
            step(v.tensor_copy(slot_share[:], tokens_ps[:, N_ST:2 * N_ST]))
            step(v.tensor_scalar(empty[:], numbers, 0.0, None, ALU.is_equal))
            step(v.scalar_tensor_tensor(empty[:], empty[:], spare[:, 0:1], numbers, ALU.mult, ALU.add))
            step(v.tensor_scalar(slot_row[:], empty[:], -1.0, None, ALU.add))

    on_engines(nc, walk)




def expert_tiles(p, ctx, xn_dram, sum_dram, slot_row, slot_share, tile_expert):
    nc = p.nc
    sb = lambda n, s, dt=F32: p.sb(n, s, dt, ctx)
    sem = lambda n: p.sem("et_" + n)
    xg = [sb(f"xg{i}", [P, D]) for i in range(2)]
    xgT = [sb(f"xgT{i}", [P, DT, P]) for i in range(2)]
    silu = [sb(f"silu{i}", [P, HID]) for i in range(2)]
    gate = [sb(f"gate{i}", [P, HID]) for i in range(2)]
    gT = [sb(f"ggT{i}", [P, HT, P]) for i in range(2)]
    y = [sb(f"y{i}", [P, D]) for i in range(2)]
    h_ps = [p.S[i][:].rearrange("p (w a) b -> p w (a b)", w=2) for i in range(2)]
    x_ps, g_ps = p.T[0], p.T[1]
    y_ps = p.O[:].rearrange("p a b -> p (a b)")[:, 0:D]
    from_row = [sb(f"from_row{i}", [P, 1], I32) for i in range(2)]
    to_row = [sb(f"to_row{i}", [P, 1], I32) for i in range(2)]
    share = [sb(f"tile_share{i}", [P, 1]) for i in range(2)]

    def load(e, r):
        i = r.par
        if e.kind == "pool":
            wait(e.eng, sem("x_in"), r.lin(16))
            e.eng.tensor_copy(from_row[i][:], slot_row[:, bass.ds(r.lin(1), 1)]).then_inc(sem("from"), 1)
            wait(e.eng, sem("from"), r.lin(1, 1))
            wait(e.eng, sem("x_turn"), r.lin(1, -1))
            e.eng.indirect_dma_start(xg[i][:], None, xn_dram, bass.IndirectOffsetOnAxis(ap=from_row[i][:], axis=0))\
                .then_inc(sem("x_in"), 16)

    def turn_x(e, r):
        if e.kind == "pe":
            wait(e.eng, sem("x_in"), r.lin(16, 16))
            wait(e.eng, sem("xT"), r.lin(1))
            for k in range(DT):
                mm = e.eng.transpose(x_ps[:, k, :], xg[r.par][:, k * P:(k + 1) * P], p.ident[:])
            mm.then_inc(sem("x_turn"), 1)
        if e.kind == "act":
            wait(e.eng, sem("x_turn"), r.lin(1, 1))
            wait(e.eng, sem("h"), r.lin(1, -1))
            e.eng.copy(xgT[r.par][:], x_ps[:, 0:DT, :]).then_inc(sem("xT"), 1)

    def expert_of(e, r):
        return e.eng.value_load(tile_expert[0:1, bass.ds(r.lin(1), 1)], min_val=0, max_val=E - 1)

    def hidden(e, r):
        i = r.par
        if e.kind == "pe":
            expert = expert_of(e, r)
            wait(e.eng, sem("xT"), r.lin(1, 1))
            wait(e.eng, sem("gate"), r.lin(1, -1))
            for j, w in enumerate((p.w1s, p.w3s)):
                for k in range(DT):
                    mm = e.eng.matmul(h_ps[i][:, j:j + 1, :], xgT[i][:, k, :], w[:, bass.ds(expert * DT + k, 1), :],
                                      start=(k == 0), stop=(k == DT - 1))
            mm.then_inc(sem("h"), 1)
        if e.kind == "act":
            wait(e.eng, sem("h"), r.lin(1, 1))
            wait(e.eng, sem("gate"), r.lin(1, -1))
            e.eng.activation(silu[i][:], h_ps[i][:, 0, :], ACT.Silu).then_inc(sem("silu"), 1)
        if e.kind == "dve":
            wait(e.eng, sem("silu"), r.lin(1, 1))
            wait(e.eng, sem("g_turn"), r.lin(1, -1))
            e.eng.tensor_tensor(gate[i][:], h_ps[i][:, 1, :], silu[i][:], ALU.mult).then_inc(sem("gate"), 1)

    def turn_gate(e, r):
        i = r.par
        if e.kind == "pe":
            wait(e.eng, sem("gate"), r.lin(1, 1))
            wait(e.eng, sem("gT"), r.lin(1))
            for k in range(HT):
                mm = e.eng.transpose(g_ps[:, k, :], gate[i][:, k * P:(k + 1) * P], p.ident[:])
            mm.then_inc(sem("g_turn"), 1)
        if e.kind == "act":
            wait(e.eng, sem("g_turn"), r.lin(1, 1))
            wait(e.eng, sem("y"), r.lin(1, -1))
            e.eng.copy(gT[i][:], g_ps[:]).then_inc(sem("gT"), 1)

    def outputs(e, r):
        i = r.par
        if e.kind == "pe":
            expert = expert_of(e, r)
            wait(e.eng, sem("gT"), r.lin(1, 1))
            wait(e.eng, sem("y_sb"), r.lin(1))
            for k in range(HT):
                mm = e.eng.matmul(y_ps.unsqueeze(1), gT[i][:, k, :], p.w2s[:, bass.ds(expert * HT + k, 1), :],
                                  start=(k == 0), stop=(k == HT - 1))
            mm.then_inc(sem("y"), 1)
        if e.kind == "pool":
            wait(e.eng, sem("y_out"), r.lin(16, -16))
            wait(e.eng, sem("y_sb"), r.lin(1, -1))
            e.eng.tensor_copy(to_row[i][:], slot_row[:, bass.ds(r.lin(1), 1)]).then_inc(sem("to"), 1)
            e.eng.tensor_copy(share[i][:], slot_share[:, bass.ds(r.lin(1), 1)]).then_inc(sem("share"), 1)
            wait(e.eng, sem("to"), r.lin(1, 1))
            wait(e.eng, sem("y_sb"), r.lin(1, 1))
            wait(e.eng, sem("y_out"), r.lin(16))
            e.eng.indirect_dma_start(sum_dram, bass.IndirectOffsetOnAxis(ap=to_row[i][:], axis=0), y[i][:], None,
                                     compute_op=ALU.add).then_inc(sem("y_out"), 16)
        if e.kind == "dve":
            wait(e.eng, sem("y"), r.lin(1, 1))
            wait(e.eng, sem("share"), r.lin(1, 1))
            wait(e.eng, sem("y_out"), r.lin(16, -16))
            e.eng.tensor_scalar(y[i][:], y_ps, share[i][:], None, ALU.mult).then_inc(sem("y_sb"), 1)

    def tile(e, r):
        n = r.off if r.reg is None else None
        has = lambda d: n is None or 0 <= n + d < N_ST
        if has(2):
            load(e, r.plus(2))
        if has(0):
            hidden(e, r)
        if has(-1):
            turn_gate(e, r.plus(-1))
        if has(1):
            turn_x(e, r.plus(1))
        if has(-2):
            outputs(e, r.plus(-2))

    def walk(e):
        load(e, Row(None, 0))
        load(e, Row(None, 1))
        turn_x(e, Row(None, 0))
        for n in range(4):
            tile(e, Row(None, n))
        with e.eng.Fori(4, N_ST - 3, 2) as r:
            tile(e, Row(r, 0, 0))
            tile(e, Row(r, 1, 1))
        for n in range(N_ST - 2, N_ST + 2):
            tile(e, Row(None, n))
        if e.kind == "pool":
            wait(e.eng, sem("y_out"), 16 * N_ST)

    on_engines(nc, walk)


def layout(x, ctx_1024, mask_Bx1xSxS2_ik1, L0_attn_pos_emb, L0_attn_global_memory, L0_attn_conv_w,
           L0_attn_conv_b, L0_attn_gate_w, L0_attn_gate_b, L0_attn_out_w, L0_attn_out_b,
           L0_xattn_Wq, L0_xattn_Wk, L0_xattn_Wv, L0_xattn_Wo, L0_ffn_router_w, L0_ffn_w1,
           L0_ffn_w2, L0_ffn_w3):
    c = np.ascontiguousarray
    return {
        "x": c(x), "ctx": c(ctx_1024), "mask": c(np.reshape(mask_Bx1xSxS2_ik1, (NB, S, KX))),
        "pos_emb": c(L0_attn_pos_emb), "global_memory": c(L0_attn_global_memory),
        "conv_w": c(np.transpose(L0_attn_conv_w, (1, 2, 0))), "conv_b": c(L0_attn_conv_b),
        "gate_w": c(L0_attn_gate_w), "gate_b": c(L0_attn_gate_b),
        "out_w": c(L0_attn_out_w), "out_b": c(L0_attn_out_b),
        "WqT": c(np.transpose(L0_xattn_Wq)), "WkT": c(np.transpose(L0_xattn_Wk)),
        "WvT": c(np.transpose(L0_xattn_Wv)), "WoT": c(np.transpose(L0_xattn_Wo)),
        "routerT": c(np.transpose(L0_ffn_router_w)),
        "w1T": c(np.transpose(L0_ffn_w1, (0, 2, 1))), "w3T": c(np.transpose(L0_ffn_w3, (0, 2, 1))),
        "w2T": c(np.transpose(L0_ffn_w2, (0, 2, 1))),
        "ident": np.eye(P, dtype=np.float32), "before": np.triu(np.ones((P, P), np.float32), 1),
        "iota_e": np.arange(E, dtype=np.float32), "iota_t": np.arange(N_ST, dtype=np.float32),
        "iota_p": np.arange(P, dtype=np.float32), "spare": np.arange(P, dtype=np.float32)[:, None] + SPARE,
        "token1": np.ascontiguousarray(np.arange(1, TOKENS + 1, dtype=np.float32).reshape(TILES, P).T),
    }


def kernel(**inputs):
    import concourse.bacc as bacc
    from concourse.bass_utils import run_bass_kernel_spmd

    nc = bacc.Bacc("TRN2", target_bir_lowering=False, num_devices=1)
    arrays = {f"in_{name}": array for name, array in layout(**inputs).items()}
    aps = {name[3:]: nc.dram_tensor(name, array.shape, mybir.dt.from_np(array.dtype), kind="ExternalInput").ap()
           for name, array in arrays.items()}
    aps["out"] = nc.dram_tensor("out", (NB, S, D), F32, kind="ExternalOutput").ap()
    build(nc, aps)
    return run_bass_kernel_spmd(nc, [arrays], core_ids=[0]).results[0]["out"]
```

```python
from contextlib import ExitStack

import numpy as np

import concourse.bass as bass
from concourse import mybir

F32 = mybir.dt.float32
BF16 = mybir.dt.bfloat16
I32 = mybir.dt.int32
U32 = mybir.dt.uint32
ALU = mybir.AluOpType
ACT = mybir.ActivationFunctionType
AX_X = mybir.AxisListType.X

P = 128
D = 256
DT = D // P
H = 16
HD = D // H
HU = H // DT
NB = 16
S = 256
NT = S // P
TILES = NB * NT
G = 64
CK = 4
KX = 120
E = 8
HID = 512
HT = HID // P
TOKENS = NB * S
TOP = 2
N_ST = (TOP * TOKENS + E * (P - 1)) // P
EPS = 1e-5
SCALE = 1.0 / float(np.sqrt(HD))
Q_SLOTS = ((0, 3, 0), (1, 2, 0), (2, 1, 0))
K_SLOTS = ((0, 3, 1), (0, 2, 1), (0, 1, 0))
SLOTS = 6
KS = SLOTS * HD




class Row:

    def __init__(self, reg, off, par=None):
        self.reg, self.off = reg, off
        self.par = off % 2 if reg is None else par

    def plus(self, n):
        return Row(self.reg, self.off + n, (self.par + n) % 2)

    def lin(self, k, c=0):
        if self.reg is None:
            return k * self.off + c
        return self.reg * k + (k * self.off + c)


class Started:
    sem = None


def wait(eng, sem, value, apart=False):
    if isinstance(value, int):
        if value > 0:
            eng.wait_ge(sem, value)
        return
    if apart or eng.engine in (mybir.EngineType.Pool, mybir.EngineType.SP):
        value = eng.to_reg(value)
        eng.wait_ge(Started.sem, 1)
    eng.wait_ge(sem, value)


def build(nc, a):
    with ExitStack() as ctx:
        Program(nc, a, ctx).emit()


class Program:
    def __init__(self, nc, a, ctx):
        self.nc, self.a, self.ctx = nc, a, ctx
        self.sems = {}

    def sem(self, name):
        if name not in self.sems:
            self.sems[name] = self.ctx.enter_context(self.nc.semaphore(name))
        return self.sems[name]

    def sb(self, name, shape, dt=F32, ctx=None):
        return (ctx or self.ctx).enter_context(self.nc.sbuf_tensor(name, shape, dt))

    def emit(self):
        nc, a, ctx = self.nc, self.a, self.ctx
        self.xres = self.sb("xres", [P, TILES, D])
        self.w1s = self.sb("w1s", [P, E * DT, HID])
        self.ident = self.sb("ident", [P, P])
        self.neg_ident = self.sb("neg_ident", [P, P], BF16)
        self.ones = self.sb("ones16", [P, P], BF16)
        self.eps = self.sb("eps", [P, 4])
        Started.sem = self.sem("started")
        self.S = [ctx.enter_context(nc.psum_tensor(f"ps_scores{i}", [P, HU, P], F32)) for i in range(2)]
        turned = ctx.enter_context(nc.psum_tensor("ps_turn", [P, HU, P], F32))
        self.T2 = turned[:]
        self.T = [turned[:, 4 * g:4 * g + 4, :] for g in range(2)]
        self.O = ctx.enter_context(nc.psum_tensor("ps_out", [P, 4, P], F32))
        self.M = ctx.enter_context(nc.psum_tensor("ps_misc", [P, 512], F32))
        self.banks = [self.M[:], self.T[0].rearrange("p a b -> p (a b)")]
        with ExitStack() as c1:
            self_attention(self, c1)
        self.w3s = self.sb("w3s", [P, E * DT, HID])
        self.w2s = self.sb("w2s", [P, E * HT, D])
        with ExitStack() as c2:
            cross_attention(self, c2)
        with ExitStack() as c3:
            experts(self, c3)


class Units:

    def __init__(self, p, ctx, tag):
        self.p, self.nc = p, p.nc
        sem = lambda n: p.sem(f"{tag}_{n}")
        self.s_scores = sem("scores")
        self.s_masked = sem("masked")
        self.s_max = sem("max")
        self.s_negm = sem("negm")
        self.s_exp = sem("exp")
        self.s_turn = sem("turn")
        self.s_ev = [sem("ev0"), sem("ev1")]
        self.s_pv = sem("pv")
        self.s_out = sem("oev")
        self.probs = [p.sb(f"{tag}_probs{i}", [P, HU, P], ctx=ctx) for i in range(2)]
        self.probsT = [p.sb(f"{tag}_probsT{i}", [P, HU, P], ctx=ctx) for i in range(2)]
        self.rowmax = [p.sb(f"{tag}_rowmax{i}", [P, HU], BF16, ctx=ctx) for i in range(2)]
        self.outT = [p.sb(f"{tag}_outT{i}", [P, 4, P], ctx=ctx) for i in range(2)]

    def scores(self, pe, U, up, q, k, nk):
        wait(pe, self.s_exp, U - 1)
        for h in range(HU):
            mm = pe.matmul(self.p.S[up][:, h, 0:nk], q(h), k(h), start=(h % 4 == 0), stop=False,
                           skip_group_check=True)
        mm.then_inc(self.s_scores, 1)

    def maxima(self, dve, U, up, nk, masked=None):
        sc = self.p.S[up][:, :, 0:nk]
        wait(dve, self.s_scores, U + 1, apart=masked is not None)
        if masked is not None:
            mask, value = masked
            dve.copy_predicated(sc, mask.unsqueeze(1).broadcast_to((P, HU, nk)),
                                value.unsqueeze(2).broadcast_to((P, HU, nk))).then_inc(self.s_masked, 1)
            wait(dve, self.s_masked, U + 1)
        dve.tensor_reduce(self.rowmax[up][:], sc, AX_X, ALU.max).then_inc(self.s_max, 1)

    def subtract_max(self, pe, U, up, nk):
        wait(pe, self.s_max, U + 1)
        for g in range(2):
            mm = pe.matmul(self.p.S[up][:, 4 * g:4 * g + 4, 0:nk], self.p.neg_ident[:],
                           self.rowmax[up][:, 4 * g:4 * g + 4].unsqueeze(2).broadcast_to((P, 4, nk)),
                           start=False, stop=True, skip_group_check=True)
        mm.then_inc(self.s_negm, 1)

    def exponentials(self, act, U, up, nk):
        wait(act, self.s_negm, U + 1)
        wait(act, self.s_turn, 2 * (U - 1))
        act.activation(self.probs[up][:, :, 0:nk], self.p.S[up][:, :, 0:nk], ACT.Exp,
                       scale=SCALE).then_inc(self.s_exp, 1)

    def turn(self, pe, U, up, nk):
        wait(pe, self.s_exp, U + 1)
        for g in range(2):
            wait(pe, self.s_ev[g], U)
            for h in range(4):
                mm = pe.transpose(self.p.T[g][0:nk, h, :], self.probs[up][:, 4 * g + h, 0:nk], self.p.ident[:])
            mm.then_inc(self.s_turn, 1)

    def evacuate(self, eng, g, U, up, nk):
        wait(eng, self.s_turn, 2 * U + 1 + g)
        wait(eng, self.s_pv, U - 1)
        dst, src = self.probsT[up][0:nk, 4 * g:4 * g + 4, :], self.p.T[g][0:nk, :, :]
        ins = eng.copy(dst, src) if g == 0 else eng.tensor_copy(dst, src)
        ins.then_inc(self.s_ev[g], 1)

    def values(self, pe, U, up, Oi, ft, v, nk):
        wait(pe, self.s_ev[0], U + 1)
        wait(pe, self.s_ev[1], U + 1)
        if Oi is not None:
            wait(pe, self.s_out, Oi)
        for h in range(HU):
            j = h % 4
            mm = pe.matmul(self.p.O[32 * j:32 * j + 32, 2 * ft + h // 4, :], v(h),
                           self.probsT[up][0:nk, h, :], start=True, stop=True,
                           tile_position=(0, 32 * j), skip_group_check=True)
        mm.then_inc(self.s_pv, 1)

    def out_copy(self, act, U, Oi, op, s_back):
        wait(act, self.s_pv, U + 1)
        wait(act, s_back, Oi - 1)
        act.copy(self.outT[op][:], self.p.O[:]).then_inc(self.s_out, 1)


class TurnedUnits:

    def __init__(self, p, ctx, tag):
        self.p, self.nc = p, p.nc
        sem = lambda n: p.sem(f"{tag}_{n}")
        self.s_scores = sem("scores")
        self.s_max = sem("max")
        self.s_diag = sem("diag")
        self.s_negm = sem("negm")
        self.s_exp = sem("exp")
        self.s_pv = sem("pv")
        self.s_out = sem("oev")
        self.probs = [p.sb(f"{tag}_probs{i}", [P, HU, P], ctx=ctx) for i in range(2)]
        self.rowmax = [p.sb(f"{tag}_rowmax{i}", [P, HU], BF16, ctx=ctx) for i in range(2)]
        self.diag = [p.sb(f"{tag}_diag{i}", [P, HU, P], BF16, ctx=ctx) for i in range(2)]
        self.outT = [p.sb(f"{tag}_outT{i}", [P, 4, P], ctx=ctx) for i in range(2)]

    def scores(self, pe, U, up, q, k, symmetric):
        wait(pe, self.s_exp, U - 1)
        for h in range(HU):
            mm = pe.matmul(self.p.S[up][:, h, :], k(h), q(h), start=(h % 4 == 0), stop=False,
                           skip_group_check=True)
        if not symmetric:
            wait(pe, self.s_max, U)
            for h in range(HU):
                mm = pe.matmul(self.p.T2[:, h, :], q(h), k(h), start=(h % 4 == 0), stop=(h % 4 == 3),
                               skip_group_check=True)
        mm.then_inc(self.s_scores, 1)

    def maxima(self, dve, U, up, symmetric):
        wait(dve, self.s_scores, U + 1)
        wait(dve, self.s_diag, U - 1)
        dve.tensor_reduce(self.rowmax[up][:], self.p.S[up][:] if symmetric else self.p.T2, AX_X, ALU.max)\
            .then_inc(self.s_max, 1)

    def diagonals(self, dve, U, up):
        wait(dve, self.s_max, U + 1)
        wait(dve, self.s_negm, U - 1)
        dve.tensor_tensor(self.diag[up][:], self.p.neg_ident[:].unsqueeze(1).broadcast_to((P, HU, P)),
                          self.rowmax[up][:].unsqueeze(2).broadcast_to((P, HU, P)), ALU.mult)\
            .then_inc(self.s_diag, 1)

    def subtract_max(self, pe, U, up):
        wait(pe, self.s_diag, U + 1)
        for g in range(2):
            mm = pe.matmul(self.p.S[up][:, 4 * g:4 * g + 4, :], self.p.ones[:],
                           self.diag[up][:, 4 * g:4 * g + 4, :], start=False, stop=True, skip_group_check=True)
        mm.then_inc(self.s_negm, 1)

    def exponentials(self, act, U, up):
        wait(act, self.s_negm, U + 1)
        wait(act, self.s_pv, U - 1)
        act.activation(self.probs[up][:], self.p.S[up][:], ACT.Exp, scale=SCALE).then_inc(self.s_exp, 1)

    def values(self, pe, U, up, Oi, ft, v):
        wait(pe, self.s_exp, U + 1)
        if Oi is not None:
            wait(pe, self.s_out, Oi)
        for h in range(HU):
            j = h % 4
            mm = pe.matmul(self.p.O[32 * j:32 * j + 32, 2 * ft + h // 4, :], v(h), self.probs[up][:, h, :],
                           start=True, stop=True, tile_position=(0, 32 * j), skip_group_check=True)
        mm.then_inc(self.s_pv, 1)

    def out_copy(self, act, U, Oi, op, s_back):
        wait(act, self.s_pv, U + 1)
        wait(act, s_back, Oi - 1)
        act.copy(self.outT[op][:], self.p.O[:]).then_inc(self.s_out, 1)


FIRST = 3
LAST = 3


def rows_of(e, n_rows, prologue, row, epilogue):
    prologue(e)
    for n in range(FIRST):
        row(e, Row(None, n), n == 0, False)
    with e.eng.Fori(FIRST, n_rows - LAST - 1, 2) as r:
        row(e, Row(r, 0, FIRST % 2), False, False)
        row(e, Row(r, 1, 1 - FIRST % 2), False, False)
    for n in range(n_rows - LAST, n_rows):
        row(e, Row(None, n), False, n == n_rows - 1)
    epilogue(e, Row(None, n_rows))


class Walker:

    def __init__(self, kind, eng):
        self.kind, self.eng, self.free = kind, eng, [[], []]


class Stages:

    def __init__(self, p, tag):
        self.p, self.tag = p, tag

    def written(self, name):
        return self.p.sem(f"{self.tag}_{name}_mm")

    def read(self, name):
        return self.p.sem(f"{self.tag}_{name}_rd")

    def run(self, e, name, index, needs, produce, reader, consume, bank=0):
        if e.kind == "pe":
            for sem, value in e.free[bank]:
                wait(e.eng, sem, value, apart=True)
            for sem, value in needs:
                wait(e.eng, sem, value, apart=True)
            produce(e.eng).then_inc(self.written(name), 1)
        if e.kind == reader:
            wait(e.eng, self.written(name), index + 1)
            consume(e.eng).then_inc(self.read(name), 1)
        e.free[bank] = [(self.read(name), index + 1)]


def on_engines(nc, walk, before=None):
    with nc.Block() as block:
        @block.tensor
        def _(eng):
            walk(Walker("pe", eng))

        @block.scalar
        def _(eng):
            walk(Walker("act", eng))

        @block.vector
        def _(eng):
            walk(Walker("dve", eng))

        @block.gpsimd
        def _(eng):
            walk(Walker("pool", eng))

        @block.sync
        def _(eng):
            walk(Walker("sp", eng))


def split_rest(pool, first, whole, rest, second, third, sem, count):
    pool.tensor_tensor(rest, whole, first, ALU.subtract).then_inc(sem, 1)
    wait(pool, sem, count + 1)
    pool.tensor_copy(second, rest).then_inc(sem, 1)
    wait(pool, sem, count + 2)
    pool.tensor_tensor(third, rest, second, ALU.subtract).then_inc(sem, 1)


def load_stack(sp, stack, scratch, slots, sem):
    row = 0
    for part, n, step in slots:
        n_rows = n * HD
        for s in range(n):
            src = scratch[part + s * step].rearrange("(h d) t -> d h t", d=HD)
            sp.dma_start(stack[row + s * HD:row + (s + 1) * HD, :, :], src).then_inc(sem, 16)
        row += n_rows


def self_attention(p, ctx):
    nc, a = p.nc, p.a
    sb = lambda n, s, dt=F32: p.sb(n, s, dt, ctx)
    u = TurnedUnits(p, ctx, "sa")
    st = Stages(p, "sa")
    sem = p.sem
    UPR = 2 * DT * NT

    pos = sb("pos", [P, NT, D])
    conv_w = sb("conv_w", [P, DT, CK, D])
    conv_b = sb("conv_b", [G, D])
    gate_w = sb("gate_w", [P, 2 * DT, D])
    gate_b = sb("gate_b", [P, D])
    out_w = sb("out_w", [P, DT, D])
    out_b = sb("out_b", [P, NT, D])
    memory = sb("memory", [P, D])
    w = [sb(f"w{i}", [P, NT, D]) for i in range(2)]
    wT = [sb(f"wT{i}", [P, DT, S]) for i in range(2)]
    wp = [sb(f"wp{i}", [P, 3, DT, S], BF16) for i in range(2)]
    rest = sb("rest", [P, DT, S])
    gT = sb("gT", [P, DT, P])
    gp = sb("gp", [P, 3, DT, P], BF16)
    grest = sb("grest", [P, DT, P])
    qs = [sb(f"qs{i}", [KS, H, S], BF16) for i in range(2)]
    ks = [sb(f"ks{i}", [KS, H, S], BF16) for i in range(2)]
    gs = [sb(f"gs{i}", [KS, H, P], BF16) for i in range(2)]
    gn = sb("gn", [G, D])
    vl = [sb(f"vl{i}", [P, NT, H, 2 * HD]) for i in range(2)]
    vg = [sb(f"vg{i}", [P, H, 2 * HD]) for i in range(2)]
    stats = sb("stats", [P, NT, 6])
    mv = sb("mv", [P, NT, 2])
    rstd = sb("rstd", [P, NT, 1])
    rec = sb("rec", [P, H, 1])
    att = [[sb(f"att{i}{j}", [P, D]) for j in range(2)] for i in range(NT)]
    attT = sb("attT", [P, 2 * DT, P])
    z = sb("z", [P, D])
    tanh = sb("tanh", [P, D])
    diff = sb("diff", [P, D])
    mix = sb("mix", [P, D])
    mixT = sb("mixT", [P, DT, P])
    w_scr = [nc.dram_tensor(f"w_scr{i}", [3, D, S], BF16, kind="Internal").ap() for i in range(2)]
    g_scr = [nc.dram_tensor(f"g_scr{i}", [3, D, P], BF16, kind="Internal").ap() for i in range(2)]
    x_t = a["x"].rearrange("b (n p) d -> p (b n) d", p=P)
    w1_t = a["w1T"].rearrange("e (k p) h -> p (e k) h", p=P)

    def consts(e, early):
        first = [(p.ident[:], a["ident"]), (pos[:], a["pos_emb"][0:S].rearrange("(n p) d -> p n d", p=P))]
        others = [(conv_w[:], a["conv_w"].rearrange("(k p) t o -> p k t o", p=P)),
                  (conv_b[:], a["conv_b"].unsqueeze(0).broadcast_to((G, D))),
                  (memory[G:P, :], a["global_memory"][0]),
                  (gate_w[:], a["gate_w"].rearrange("(k p) o -> p k o", p=P)),
                  (gate_b[:], a["gate_b"].unsqueeze(0).broadcast_to((P, D))),
                  (out_w[:], a["out_w"].rearrange("(k p) o -> p k o", p=P)),
                  (out_b[:, 0, :], a["out_b"].unsqueeze(0).broadcast_to((P, D))),
                  (out_b[:, 1, :], a["out_b"].unsqueeze(0).broadcast_to((P, D)))]
        loads, name = (first, "first") if early else (others, "const")
        if e.kind == "sp":
            for dst, src in loads:
                e.eng.dma_start(dst, src).then_inc(sem(name), 16)
        if early:
            if e.kind == "pool":
                e.eng.memset(p.eps[:, 1:2], 0.0).then_inc(Started.sem, 1)
                e.eng.memset(p.eps[:, 0:1], -0.5).then_inc(sem("set"), 1)
                e.eng.memset(p.ones[:], 1.0).then_inc(sem("set"), 1)
                e.eng.memset(memory[0:G, :], 0.0).then_inc(sem("set"), 1)
                for i in range(2):
                    e.eng.memset(vl[i][:], 1.0).then_inc(sem("set"), 1)
                    e.eng.memset(vg[i][:], 1.0).then_inc(sem("set"), 1)
                wait(e.eng, sem("set"), 7)
            if e.kind == "dve":
                wait(e.eng, sem("first"), 16 * len(first))
                e.eng.tensor_scalar(p.neg_ident[:], p.ident[:], -1.0, None, ALU.mult).then_inc(sem("set_dve"), 1)
            if e.kind in ("pe", "pool"):
                wait(e.eng, sem("first"), 16 * len(first))
            if e.kind == "pe":
                wait(e.eng, sem("set_dve"), 1)
            return
        if e.kind != "sp":
            wait(e.eng, sem("const"), 16 * len(others))
        if e.kind == "pool":
            wait(e.eng, sem("w"), 1)
            for i in range(2):
                e.eng.tensor_copy(vg[i][G:P, :, 0:HD], memory[G:P, :].rearrange("p (h d) -> p h d", d=HD))\
                    .then_inc(sem("set"), 1)
        if e.kind in ("act", "pe", "pool"):
            wait(e.eng, sem("set"), 9)


        def turn(pe):
            for k in range(DT):
                mm = pe.transpose(p.M[:, k * P:(k + 1) * P], memory[:, k * P:(k + 1) * P], p.ident[:])
            return mm

        def copy(act):
            return act.copy(gT[:, :, G:P], p.M[:, 0:DT * P].rearrange("p (k g) -> p k g", k=DT)[:, :, G:P])
        st.run(e, "mem", 0, [], turn, "act", copy)


    def load_x(e, r):
        if e.kind == "sp":
            t = r.lin(NT)
            wait(e.eng, sem("x"), r.lin(32))
            e.eng.dma_start(p.xres[:, bass.ds(t, NT), :], x_t[:, bass.ds(t, NT), :]).then_inc(sem("x"), 16)
            e.eng.dma_start(p.w1s[:, bass.ds(r.lin(1), 1), :], w1_t[:, bass.ds(r.lin(1), 1), :])\
                .then_inc(sem("x"), 16)

    def normalise(e, r):
        if e.kind == "dve":
            wait(e.eng, sem("x"), r.lin(32, 32))
            for n in range(NT):
                e.eng.bn_stats(stats[:, n, :], p.xres[:, bass.ds(r.lin(NT, n), 1), :]).then_inc(sem("stats"), 1)
            wait(e.eng, sem("stats"), r.lin(NT, NT), apart=True)
            for n in range(NT):
                e.eng.bn_aggr(mv[:, n, :], stats[:, n, :]).then_inc(sem("mv"), 1)

    def apply_norm(e, r):
        i = r.par
        if e.kind == "dve":
            wait(e.eng, sem("rstd"), r.lin(2, 2))
            wait(e.eng, sem("wp1"), r.lin(1, -1))
            wait(e.eng, sem("vl"), r.lin(1, -1))
            for n in range(NT):
                e.eng.tensor_scalar(w[i][:, n, :].unsqueeze(1), p.xres[:, bass.ds(r.lin(NT, n), 1), :],
                                    mv[:, n, 0:1], rstd[:, n, :], ALU.subtract, ALU.mult)\
                    .then_inc(sem("norm"), 1)
        if e.kind == "pool":
            wait(e.eng, sem("mv"), r.lin(NT, NT))
            wait(e.eng, sem("norm"), r.lin(NT))
            e.eng.tensor_scalar(rstd[:], mv[:, :, 1:2], EPS, None, ALU.add).then_inc(sem("rstd"), 1)
            wait(e.eng, sem("rstd"), r.lin(2, 1))
            e.eng.tensor_tensor(rstd[:], rstd[:], p.eps[:, 0:1].unsqueeze(1).broadcast_to((P, NT, 1)),
                                ALU.pow).then_inc(sem("rstd"), 1)
            wait(e.eng, sem("norm"), r.lin(NT, NT))
            e.eng.tensor_tensor(w[i][:], w[i][:], pos[:], ALU.add).then_inc(sem("w"), 1)

    def turn_w(e, r):
        i = r.par

        def turn(pe):
            for k in range(DT):
                for n in range(NT):
                    mm = pe.transpose(p.M[:, k * S + n * P:k * S + (n + 1) * P], w[i][:, n, k * P:(k + 1) * P],
                                      p.ident[:])
            return mm

        def copy(act):
            wait(act, sem("ws"), r.lin(3, -3))
            return act.copy(wT[i][:], p.M[:].rearrange("p (k t) -> p k t", k=DT))
        st.run(e, "turn_w", r.lin(1), [(sem("w"), r.lin(1, 1))], turn, "act", copy)

    def first_part_w(e, r):
        i = r.par
        if e.kind == "act":
            wait(e.eng, st.read("turn_w"), r.lin(1, 1))
            wait(e.eng, sem("w_scr"), r.lin(16, -16))
            e.eng.copy(wp[i][:, 0, :, :], wT[i][:]).then_inc(sem("wp1"), 1)

    def parts_w(e, r):
        i = r.par
        if e.kind == "pool":
            wait(e.eng, sem("wp1"), r.lin(1, 1))
            split_rest(e.eng, wp[i][:, 0, :, :], wT[i][:], rest[:], wp[i][:, 1, :, :], wp[i][:, 2, :, :],
                       sem("ws"), r.lin(3))
            wait(e.eng, u.s_pv, r.lin(UPR, -UPR))
            e.eng.tensor_copy(vl[i][:, :, :, 0:HD], w[i][:].rearrange("p n (h d) -> p n h d", d=HD))\
                .then_inc(sem("vl"), 1)
            xr = p.xres[:, bass.ds(r.lin(NT), NT), :]
            e.eng.tensor_tensor(xr, xr, out_b[:], ALU.add).then_inc(sem("xb"), 1)
        if e.kind == "sp":
            wait(e.eng, sem("ws"), r.lin(3, 3))
            wait(e.eng, sem("stacks"), r.lin(192))
            e.eng.dma_start(w_scr[i].rearrange("c (k p) t -> p c k t", p=P), wp[i][:]).then_inc(sem("w_scr"), 16)
            wait(e.eng, sem("w_scr"), r.lin(16, 16))
            wait(e.eng, u.s_scores, r.lin(UPR, -UPR))
            load_stack(e.eng, qs[i], w_scr[i], Q_SLOTS, sem("stacks"))
            load_stack(e.eng, ks[i], w_scr[i], K_SLOTS, sem("stacks"))

    def compress(e, r):
        i = r.par

        def products(pe):
            taps = [(k, t) for k in range(DT) for t in range(CK)]
            for n, (k, t) in enumerate(taps):
                mm = pe.matmul(p.M[0:G, 0:D], wT[i][:, k, :].rearrange("p (g t) -> p t g", t=CK)[:, t, :],
                               conv_w[:, k, t, :], start=(n == 0), stop=(n == len(taps) - 1))
            return mm

        def add_bias(dve):
            wait(dve, st.written("turn_g"), r.lin(1))
            wait(dve, sem("vg"), r.lin(1))
            return dve.tensor_tensor(gn[:], p.M[0:G, 0:D], conv_b[:], ALU.add)
        st.run(e, "conv", r.lin(1), [(st.read("turn_w"), r.lin(1, 1))], products, "dve", add_bias)
        if e.kind == "pool":
            wait(e.eng, st.read("conv"), r.lin(1, 1))
            wait(e.eng, u.s_pv, r.lin(UPR, -UPR))
            e.eng.tensor_copy(vg[i][0:G, :, 0:HD], gn[:].rearrange("p (h d) -> p h d", d=HD))\
                .then_inc(sem("vg"), 1)

    def turn_g(e, r):
        i = r.par

        def turn(pe):
            for k in range(DT):
                mm = pe.transpose(p.M[:, k * G:(k + 1) * G], gn[:, k * P:(k + 1) * P],
                                  p.ident[0:G, 0:G])
            return mm

        def copy(act):
            wait(act, sem("gs"), r.lin(3))
            return act.copy(gT[:, :, 0:G], p.M[:, 0:DT * G].rearrange("p (k g) -> p k g", k=DT))
        st.run(e, "turn_g", r.lin(1), [(st.read("conv"), r.lin(1, 1))], turn, "act", copy)
        if e.kind == "act":
            wait(e.eng, st.read("turn_g"), r.lin(1, 1))
            wait(e.eng, sem("g_scr"), r.lin(16))
            e.eng.copy(gp[:, 0, :, :], gT[:]).then_inc(sem("gp1"), 1)

    def parts_g(e, r):
        i = r.par
        if e.kind == "pool":
            wait(e.eng, sem("gp1"), r.lin(1, 1))
            split_rest(e.eng, gp[:, 0, :, :], gT[:], grest[:], gp[:, 1, :, :], gp[:, 2, :, :],
                       sem("gs"), r.lin(3))
        if e.kind == "sp":
            wait(e.eng, sem("gs"), r.lin(3, 3))
            wait(e.eng, sem("g_stack"), r.lin(96))
            e.eng.dma_start(g_scr[i].rearrange("c (k p) t -> p c k t", p=P), gp[:]).then_inc(sem("g_scr"), 16)
            wait(e.eng, sem("g_scr"), r.lin(16, 16))
            load_stack(e.eng, gs[i], g_scr[i], K_SLOTS, sem("g_stack"))


    def unit(s):
        return s // 4, s // 2 % 2, s % 2

    def scores(e, r, s):
        n, kind, f = unit(s)
        i = r.par
        if e.kind == "pe":
            if s == 0:
                wait(e.eng, sem("stacks"), r.lin(192, 192))
            if s == 2:
                wait(e.eng, sem("g_stack"), r.lin(96, 96))
            if kind:
                for s_free, value in e.free[1]:
                    wait(e.eng, s_free, value, apart=True)
            q = lambda h: qs[i][:, f * HU + h, n * P:(n + 1) * P]
            k = (lambda h: gs[i][:, f * HU + h, :]) if kind else (lambda h: ks[i][:, f * HU + h, n * P:(n + 1) * P])
            u.scores(e.eng, r.lin(UPR, s), s % 2, q, k, symmetric=kind == 0)
        if e.kind == "dve":
            u.maxima(e.eng, r.lin(UPR, s), s % 2, symmetric=kind == 0)

    def diagonals(e, r, s):
        if e.kind == "dve":
            u.diagonals(e.eng, r.lin(UPR, s), s % 2)

    def values(e, r, s):
        n, kind, f = unit(s)
        i = r.par
        if s == 0:
            wait(e.eng, sem("vl"), r.lin(1, 1))
            wait(e.eng, sem("vg"), r.lin(1, 1))
        v = (lambda h: vg[i][:, f * HU + h, :]) if kind else (lambda h: vl[i][:, n, f * HU + h, :])
        u.values(e.eng, r.lin(UPR, s), s % 2, r.lin(UPR // 2, s // 2) if f == 0 else None, f, v)



    def turn_back(e, r, n, kind, bank=0, taken=()):
        o = r.lin(UPR // 2, 2 * n + kind)
        m = p.banks[bank]

        def turn(pe):
            for g in range(4):
                mm = pe.transpose(m[:, g * P:(g + 1) * P], u.outT[kind][:, g, :], p.ident[:])
            return mm

        def divide(dve):
            m3 = m.rearrange("p (h d) -> p h d", h=H)
            dve.reciprocal(rec[:], m3[:, :, HD:HD + 1]).then_inc(sem("rec"), 1)
            wait(dve, sem("rec"), o + 1)
            if kind == 0:
                wait(dve, sem("mixed"), r.lin(NT, n - 1))
            return dve.tensor_tensor(att[n][kind][:].rearrange("p (h d) -> p h d", d=HD), m3[:, :, 0:HD],
                                     rec[:].broadcast_to((P, H, HD)), ALU.mult)
        st.run(e, "back", o, [(u.s_out, o + 1), *taken], turn, "dve", divide, bank)

    def turn_att(e, r, n, bank=0, taken=()):
        t = r.lin(NT, n)
        m = p.banks[bank]

        def turn(pe):
            for kind in range(2):
                for k in range(DT):
                    c = (kind * DT + k) * P
                    mm = pe.transpose(m[:, c:c + P], att[n][kind][:, k * P:(k + 1) * P], p.ident[:])
            return mm

        def copy(act):
            return act.copy(attT[:], m.rearrange("p (k t) -> p k t", k=2 * DT))
        st.run(e, "att", t, [(st.read("back"), r.lin(UPR // 2, 2 * n + 2)), *taken], turn, "act", copy,
               bank)

    def gate(e, r, n, bank=0, taken=()):
        t = r.lin(NT, n)
        m = p.banks[bank]

        def products(pe):
            for k in range(2 * DT):
                mm = pe.matmul(m[:, 0:D], attT[:, k, :], gate_w[:, k, :], start=(k == 0), stop=(k == 2 * DT - 1))
            return mm

        def add_bias(dve):
            wait(dve, sem("tanh"), t)
            return dve.tensor_tensor(z[:], m[:, 0:D], gate_b[:], ALU.add)
        st.run(e, "gate", t, [(st.read("att"), t + 1), *taken], products, "dve", add_bias, bank)
        if e.kind == "pool":
            wait(e.eng, st.read("back"), r.lin(UPR // 2, 2 * n + 2))
            wait(e.eng, sem("half"), t)
            e.eng.tensor_tensor(diff[:], att[n][0][:], att[n][1][:], ALU.subtract).then_inc(sem("df"), 1)

    def mix_tile(e, r, n):
        t = r.lin(NT, n)
        if e.kind == "act":
            wait(e.eng, st.read("gate"), t + 1)
            wait(e.eng, sem("half"), t)
            e.eng.activation(tanh[:], z[:], ACT.Tanh, scale=0.5).then_inc(sem("tanh"), 1)
        if e.kind == "dve":
            wait(e.eng, sem("tanh"), t + 1)
            wait(e.eng, sem("df"), t + 1)
            wait(e.eng, st.written("mixT"), t)
            e.eng.scalar_tensor_tensor(mix[:], tanh[:], 1.0, diff[:], ALU.add, ALU.mult).then_inc(sem("half"), 1)
            wait(e.eng, sem("half"), t + 1)
            e.eng.scalar_tensor_tensor(mix[:], mix[:], 0.5, att[n][1][:], ALU.mult, ALU.add)\
                .then_inc(sem("mixed"), 1)

    def turn_mix(e, r, n):
        t = r.lin(NT, n)

        def turn(pe):
            for k in range(DT):
                mm = pe.transpose(p.M[:, k * P:(k + 1) * P], mix[:, k * P:(k + 1) * P], p.ident[:])
            return mm

        def copy(act):
            return act.copy(mixT[:], p.M[:, 0:D].rearrange("p (k t) -> p k t", k=DT))
        st.run(e, "mixT", t, [(sem("mixed"), t + 1)], turn, "act", copy)

    def project(e, r, n):
        t = r.lin(NT, n)

        def products(pe):
            for k in range(DT):
                mm = pe.matmul(p.M[:, 0:D], mixT[:, k, :], out_w[:, k, :], start=(k == 0), stop=(k == DT - 1))
            return mm

        def residual(dve):
            wait(dve, sem("xb"), r.lin(1, 1))
            x = p.xres[:, bass.ds(t, 1), :]
            return dve.tensor_tensor(x, p.M[:, 0:D].unsqueeze(1), x, ALU.add)
        st.run(e, "proj", t, [(st.read("mixT"), t + 1)], products, "dve", residual)


    def prologue(e):
        r0 = Row(None, 0)
        load_x(e, r0)
        consts(e, early=True)
        if e.kind == "sp":
            consts(e, early=False)
            load_x(e, r0.plus(1))
        normalise(e, r0)
        apply_norm(e, r0)
        turn_w(e, r0)
        first_part_w(e, r0)
        if e.kind != "sp":
            consts(e, early=False)
        parts_w(e, r0)
        compress(e, r0)
        turn_g(e, r0)
        parts_g(e, r0)
        scores(e, r0, 0)
        diagonals(e, r0, 0)

    def slot(e, r, s, first, last, drain=False):
        U, nxt, prev = r.lin(UPR, s), r.plus(1), r.plus(-1)
        lag = lambda d: (r, s - d) if s >= d else (prev, s - d + UPR)
        exists = lambda d: s >= d or not first
        done = lambda f, *x: (lambda: None if first else f(e, prev, *x))
        this = lambda f, *x: (lambda: None if drain else f(e, r, *x))
        then = lambda f: (lambda: None if last or drain else f(e, nxt))
        nothing = lambda: None
        maxima = lambda n: [(u.s_max, r.lin(UPR, 0 if drain else n))]
        stages = {
            0: [done(turn_back, 1, 0), done(gate, 0, 1, maxima(0))],
            1: [then(turn_w)],
            2: [done(turn_back, 1, 1), done(turn_mix, 0), then(compress)],
            3: [nothing, done(turn_att, 1, 1, maxima(4)), done(project, 0)],
            4: [then(turn_g), this(turn_back, 0, 0, 1, maxima(4))],
            5: [nothing, done(gate, 1)],
            6: [this(turn_back, 0, 1), nothing, done(turn_mix, 1)],
            7: [done(project, 1), this(turn_att, 0, 1, maxima(8))],
        }[s] + [nothing] * 3
        more = not drain and not (last and s == UPR - 1)
        if s == 0 and not (last or drain):
            normalise(e, nxt)
        k = e.kind
        if k == "dve":
            stages[0]()
        if more:
            scores(e, *((r, s + 1) if s + 1 < UPR else (nxt, 0)))
        if k == "pe":
            stages[0]()
            if not drain:
                u.subtract_max(e.eng, U, s % 2)
            stages[1]()
            if exists(1) and not (drain and s >= 1):
                values(e, *lag(1))
            stages[2]()
            return
        if s == 0 and not (last or drain):
            apply_norm(e, nxt)
        if k != "dve":
            stages[0]()
        if k == "act" and not drain:
            u.exponentials(e.eng, U, s % 2)
        if s == 1 and not (last or drain):
            first_part_w(e, nxt)
        if k == "act" and s in (0, 5) and not first:
            mix_tile(e, prev, s // 5)
        stages[1]()
        if more:
            diagonals(e, *((r, s + 1) if s + 1 < UPR else (nxt, 0)))
        if k == "act" and s % 2 == 0 and exists(1) and not (drain and s >= 1):
            rr, ss = lag(1)
            u.out_copy(e.eng, rr.lin(UPR, ss), rr.lin(UPR // 2, ss // 2), ss // 2 % 2, st.written("back"))
        stages[2]()
        if k == "dve" and s in (1, 5) and not first:
            mix_tile(e, prev, s // 5)
        if s == 1 and not (last or drain):
            parts_w(e, nxt)
        if s == 5 and not (last or drain):
            parts_g(e, nxt)

    def row(e, r, first, last):
        if e.kind == "sp":
            if not last:
                if not (r.reg is None and r.off >= NB - 2):
                    load_x(e, r.plus(2))
                parts_w(e, r.plus(1))
                parts_g(e, r.plus(1))
            return
        if not first:
            if r.reg is None and r.off == 1:
                e.free[0] = [(st.read("back"), 2)]
            else:
                e.free[0] = [(st.read("proj"), r.lin(NT, -NT))]
            e.free[1] = [(st.read("att"), r.lin(NT, -1))]
        for s in range(UPR):
            slot(e, r, s, first, last)

    def epilogue(e, r):
        if e.kind == "sp":
            return
        e.free = [[(st.read("proj"), r.lin(NT, -NT))], [(st.read("att"), r.lin(NT, -1))]]
        for s in range(UPR):
            slot(e, r, s, False, True, drain=True)

    on_engines(nc, lambda e: rows_of(e, NB, prologue, row, epilogue))



def cross_attention(p, ctx):
    nc, a = p.nc, p.a
    sb = lambda n, s, dt=F32: p.sb(n, s, dt, ctx)
    u = Units(p, ctx, "xa")
    st = Stages(p, "xa")
    sem = lambda n: p.sem("xa_" + n)
    UPR = DT * NT

    wt = {n: sb(n + "_sb", [P, DT, D]) for n in ("WqT", "WkT", "WvT", "WoT")}
    masked_score = sb("masked_score", [P, 1])
    xn = sb("xn", [P, NT, D])
    nT = sb("nT", [P, DT, S])
    ctx_n = [sb(f"ctx_n{i}", [KX, D]) for i in range(2)]
    cT = [sb(f"cT{i}", [P, DT, KX]) for i in range(2)]
    qT = sb("qT", [P, DT, S])
    qp = sb("qp", [P, 3, DT, S], BF16)
    kT = sb("kT", [P, DT, KX])
    kp = sb("kp", [P, 3, DT, KX], BF16)
    rest = sb("xrest", [P, DT, S])
    qs = [sb(f"xqs{i}", [KS, H, S], BF16) for i in range(2)]
    ks = [sb(f"xks{i}", [KS, H, KX], BF16) for i in range(2)]
    vx = [sb(f"vx{i}", [KX, H, 2 * HD]) for i in range(2)]
    mask = [sb(f"mask{i}", [P, NT, KX], I32) for i in range(2)]
    zero = [sb(f"zero{i}", [P, NT, KX], I32) for i in range(2)]
    stats = sb("xstats", [P, NT, 6])
    mv = sb("xmv", [P, NT, 2])
    rstd = sb("xrstd", [P, NT, 1])
    rec = sb("xrec", [P, H, 1])
    att = sb("xatt", [P, D])
    attT = sb("xattT", [P, DT, P])
    q_scr = [nc.dram_tensor(f"q_scr{i}", [3, D, S], BF16, kind="Internal").ap() for i in range(2)]
    k_scr = [nc.dram_tensor(f"k_scr{i}", [3, D, KX], BF16, kind="Internal").ap() for i in range(2)]
    ctx_t = a["ctx"].rearrange("b k d -> k b d")
    mask_t = a["mask"].rearrange("b (n p) k -> p (b n) k", p=P)
    w3_t = a["w3T"].rearrange("e (k p) h -> p (e k) h", p=P)
    w2_t = a["w2T"].rearrange("e (k p) d -> p (e k) d", p=P)

    def consts(e):
        N_CONST = 16 * 4
        if e.kind == "sp":
            for n in ("WqT", "WkT", "WvT", "WoT"):
                e.eng.dma_start(wt[n][:], a[n].rearrange("(k p) o -> p k o", p=P)).then_inc(sem("const"), 16)
            wait(e.eng, sem("set"), 3)
        if e.kind == "pool":
            e.eng.memset(masked_score[:], 1e-9 / SCALE).then_inc(sem("set"), 1)
            for i in range(2):
                e.eng.memset(vx[i][:], 1.0).then_inc(sem("set"), 1)
            wait(e.eng, sem("set"), 3)
        if e.kind in ("dve", "act"):
            wait(e.eng, sem("set"), 3)
        if e.kind == "pe":
            wait(e.eng, sem("const"), N_CONST)
            wait(e.eng, sem("set"), 3)

    def load(e, r):
        if e.kind == "sp":
            i = r.par
            wait(e.eng, sem("in"), r.lin(64))
            wait(e.eng, st.written("turn_c"), r.lin(1, -1))
            wait(e.eng, sem("zero"), r.lin(1, -1))
            e.eng.dma_start(ctx_n[i][:].unsqueeze(1), ctx_t[:, bass.ds(r.lin(1), 1), :]).then_inc(sem("in"), 16)
            e.eng.dma_start(mask[i][:], mask_t[:, bass.ds(r.lin(NT), NT), :]).then_inc(sem("in"), 16)
            e.eng.dma_start(p.w3s[:, bass.ds(r.lin(1), 1), :], w3_t[:, bass.ds(r.lin(1), 1), :])\
                .then_inc(sem("in"), 16)
            e.eng.dma_start(p.w2s[:, bass.ds(r.lin(2), 2), :], w2_t[:, bass.ds(r.lin(2), 2), :])\
                .then_inc(sem("in"), 16)

    def normalise(e, r):
        if e.kind == "dve":
            for n in range(NT):
                e.eng.bn_stats(stats[:, n, :], p.xres[:, bass.ds(r.lin(NT, n), 1), :]).then_inc(sem("stats"), 1)
            wait(e.eng, sem("stats"), r.lin(NT, NT), apart=True)
            for n in range(NT):
                e.eng.bn_aggr(mv[:, n, :], stats[:, n, :]).then_inc(sem("mv"), 1)
        if e.kind == "pool":
            wait(e.eng, sem("mv"), r.lin(NT, NT))
            wait(e.eng, sem("norm"), r.lin(NT))
            e.eng.tensor_scalar(rstd[:], mv[:, :, 1:2], EPS, None, ALU.add).then_inc(sem("rstd"), 1)
            wait(e.eng, sem("rstd"), r.lin(2, 1))
            e.eng.tensor_tensor(rstd[:], rstd[:], p.eps[:, 0:1].unsqueeze(1).broadcast_to((P, NT, 1)),
                                ALU.pow).then_inc(sem("rstd"), 1)

    def make_zero(e, r):
        if e.kind == "pool":
            wait(e.eng, sem("in"), r.lin(64, 64))
            wait(e.eng, u.s_masked, r.lin(UPR, -UPR))
            e.eng.tensor_scalar(zero[r.par][:], mask[r.par][:], 0.0, None, ALU.is_equal).then_inc(sem("zero"), 1)

    def apply_norm(e, r):
        if e.kind == "dve":
            wait(e.eng, sem("rstd"), r.lin(2, 2))
            wait(e.eng, st.written("turn_n"), r.lin(1))
            for n in range(NT):
                e.eng.tensor_scalar(xn[:, n, :].unsqueeze(1), p.xres[:, bass.ds(r.lin(NT, n), 1), :],
                                    mv[:, n, 0:1], rstd[:, n, :], ALU.subtract, ALU.mult)\
                    .then_inc(sem("norm"), 1)

    def turn_n(e, r):
        def turn(pe):
            for k in range(DT):
                for n in range(NT):
                    mm = pe.transpose(p.M[:, k * S + n * P:k * S + (n + 1) * P], xn[:, n, k * P:(k + 1) * P],
                                      p.ident[:])
            return mm

        def copy(act):
            return act.copy(nT[:], p.M[:].rearrange("p (k t) -> p k t", k=DT))
        st.run(e, "turn_n", r.lin(1), [(sem("norm"), r.lin(NT, NT))], turn, "act", copy)

    def turn_c(e, r):
        i = r.par

        def turn(pe):
            for k in range(DT):
                mm = pe.transpose(p.M[:, k * KX:(k + 1) * KX], ctx_n[i][:, k * P:(k + 1) * P],
                                  p.ident[0:KX, 0:KX])
            return mm

        def copy(act):
            return act.copy(cT[i][:], p.M[:, 0:DT * KX].rearrange("p (k t) -> p k t", k=DT))
        st.run(e, "turn_c", r.lin(1), [(sem("in"), r.lin(64, 64))], turn, "act", copy)

    def features(pe, weights, xT, n):
        for o in range(DT):
            for k in range(DT):
                mm = pe.matmul(p.M[:, o * n:(o + 1) * n], weights[:, k, o * P:(o + 1) * P], xT[:, k, :],
                               start=(k == 0), stop=(k == DT - 1))
        return mm

    def queries(e, r):
        def copy(act):
            wait(act, sem("qp"), r.lin(3))
            return act.copy(qT[:], p.M[:].rearrange("p (k t) -> p k t", k=DT))
        st.run(e, "q", r.lin(1), [(st.read("turn_n"), r.lin(1, 1))],
               lambda pe: features(pe, wt["WqT"], nT, S), "act", copy)

    def first_part_q(e, r):
        if e.kind == "act":
            wait(e.eng, st.read("q"), r.lin(1, 1))
            wait(e.eng, sem("q_scr"), r.lin(16))
            e.eng.copy(qp[:, 0, :, :], qT[:]).then_inc(sem("qp1"), 1)

    def keys(e, r):
        i = r.par

        def copy(act):
            wait(act, sem("kp"), r.lin(3))
            return act.copy(kT[:], p.M[:, 0:DT * KX].rearrange("p (k t) -> p k t", k=DT))
        st.run(e, "k", r.lin(1), [(st.read("turn_c"), r.lin(1, 1))],
               lambda pe: features(pe, wt["WkT"], cT[i], KX), "act", copy)
        if e.kind == "act":
            wait(e.eng, st.read("k"), r.lin(1, 1))
            wait(e.eng, sem("k_scr"), r.lin(16))
            e.eng.copy(kp[:, 0, :, :], kT[:]).then_inc(sem("kp1"), 1)

    def parts(e, r):
        i = r.par
        if e.kind == "pool":
            wait(e.eng, sem("qp1"), r.lin(1, 1))
            wait(e.eng, sem("kp"), r.lin(3))
            split_rest(e.eng, qp[:, 0, :, :], qT[:], rest[:], qp[:, 1, :, :], qp[:, 2, :, :], sem("qp"), r.lin(3))
            wait(e.eng, sem("kp1"), r.lin(1, 1))
            wait(e.eng, sem("qp"), r.lin(3, 3))
            split_rest(e.eng, kp[:, 0, :, :], kT[:], rest[:, :, 0:KX], kp[:, 1, :, :], kp[:, 2, :, :],
                       sem("kp"), r.lin(3))
        if e.kind == "sp":
            wait(e.eng, sem("qp"), r.lin(3, 3))
            wait(e.eng, sem("stacks"), r.lin(192))
            e.eng.dma_start(q_scr[i].rearrange("c (k p) t -> p c k t", p=P), qp[:]).then_inc(sem("q_scr"), 16)
            wait(e.eng, sem("kp"), r.lin(3, 3))
            e.eng.dma_start(k_scr[i].rearrange("c (k p) t -> p c k t", p=P), kp[:]).then_inc(sem("k_scr"), 16)
            wait(e.eng, u.s_scores, r.lin(UPR, -UPR))
            wait(e.eng, sem("q_scr"), r.lin(16, 16))
            load_stack(e.eng, qs[i], q_scr[i], Q_SLOTS, sem("stacks"))
            wait(e.eng, sem("k_scr"), r.lin(16, 16))
            load_stack(e.eng, ks[i], k_scr[i], K_SLOTS, sem("stacks"))

    def make_values(e, r):
        i = r.par

        def products(pe):
            for k in range(DT):
                mm = pe.matmul(p.M[0:KX, 0:D], cT[i][:, k, :], wt["WvT"][:, k, :], start=(k == 0),
                               stop=(k == DT - 1))
            return mm

        def copy(act):
            wait(act, u.s_pv, r.lin(UPR, -UPR))
            return act.copy(vx[i][:, :, 0:HD], p.M[0:KX, 0:D].rearrange("p (h d) -> p h d", d=HD))
        st.run(e, "v", r.lin(1), [(st.read("turn_c"), r.lin(1, 1))], products, "act", copy)

    def scores(e, r, s):
        n, f = s // DT, s % DT
        i = r.par
        if e.kind == "pe":
            if s == 0:
                wait(e.eng, sem("stacks"), r.lin(192, 192))
            u.scores(e.eng, r.lin(UPR, s), s % 2, lambda h: qs[i][:, f * HU + h, n * P:(n + 1) * P],
                     lambda h: ks[i][:, f * HU + h, :], KX)
        if e.kind == "dve":
            if s == 0:
                wait(e.eng, sem("zero"), r.lin(1, 1), apart=True)
            u.maxima(e.eng, r.lin(UPR, s), s % 2, KX, (zero[i][:, n, :], masked_score[:]))

    def values(e, r, s):
        f = s % DT
        if s == 0:
            wait(e.eng, st.read("v"), r.lin(1, 1))
        u.values(e.eng, r.lin(UPR, s), s % 2, r.lin(UPR // 2, s // 2) if f == 0 else None, f,
                 lambda h: vx[r.par][:, f * HU + h, :], KX)

    def turn_back(e, r, n):
        t = r.lin(NT, n)

        def turn(pe):
            for g in range(4):
                mm = pe.transpose(p.M[:, g * P:(g + 1) * P], u.outT[n][:, g, :], p.ident[:])
            return mm

        def divide(dve):
            m = p.M[:].rearrange("p (h d) -> p h d", h=H)
            dve.reciprocal(rec[:], m[:, :, HD:HD + 1]).then_inc(sem("rec"), 1)
            wait(dve, sem("rec"), t + 1)
            wait(dve, st.written("att"), t)
            return dve.tensor_tensor(att[:].rearrange("p (h d) -> p h d", d=HD), m[:, :, 0:HD],
                                     rec[:].broadcast_to((P, H, HD)), ALU.mult)
        st.run(e, "back", t, [(u.s_out, t + 1)], turn, "dve", divide)

    def turn_att(e, r, n):
        t = r.lin(NT, n)

        def turn(pe):
            for k in range(DT):
                mm = pe.transpose(p.M[:, k * P:(k + 1) * P], att[:, k * P:(k + 1) * P], p.ident[:])
            return mm

        def copy(act):
            return act.copy(attT[:], p.M[:, 0:D].rearrange("p (k t) -> p k t", k=DT))
        st.run(e, "att", t, [(st.read("back"), t + 1)], turn, "act", copy)

    def project(e, r, n):
        t = r.lin(NT, n)

        def products(pe):
            for k in range(DT):
                mm = pe.matmul(p.M[:, 0:D], attT[:, k, :], wt["WoT"][:, k, :], start=(k == 0), stop=(k == DT - 1))
            return mm

        def residual(dve):
            x = p.xres[:, bass.ds(t, 1), :]
            return dve.tensor_tensor(x, p.M[:, 0:D].unsqueeze(1), x, ALU.add)
        st.run(e, "proj", t, [(st.read("att"), t + 1)], products, "dve", residual)

    def prologue(e):
        r0, r1, r2 = (Row(None, n) for n in range(3))
        consts(e)
        load(e, r0)
        load(e, r1)
        normalise(e, r0)
        apply_norm(e, r0)
        turn_n(e, r0)
        turn_c(e, r0)
        normalise(e, r1)
        apply_norm(e, r1)
        queries(e, r0)
        first_part_q(e, r0)
        keys(e, r0)
        parts(e, r0)
        make_zero(e, r0)
        make_values(e, r0)
        turn_n(e, r1)
        turn_c(e, r1)
        load(e, r2)
        normalise(e, r2)
        queries(e, r1)
        first_part_q(e, r1)
        keys(e, r1)
        parts(e, r1)
        make_zero(e, r1)
        apply_norm(e, r2)
        scores(e, r0, 0)

    def lag(r, s, d):
        return (r, s - d) if s >= d else (r.plus(-1), s - d + UPR)

    def at_unit(x):
        return x[0].lin(UPR, x[1]), x[1] % 2

    def slot(e, r, s, first, ahead, ahead3, last, drain=False):
        U, nxt, nxt2, prev = r.lin(UPR, s), r.plus(1), r.plus(2), r.plus(-1)
        exists = lambda d: s >= d or not first
        done = lambda f, *x: (lambda: None if first else f(e, prev, *x))
        then = lambda f, row, ok: (lambda: f(e, row) if ok else None)
        stages = {
            0: [done(turn_back, 0), then(turn_n, nxt2, ahead)],
            1: [done(turn_att, 0), then(queries, nxt2, ahead), then(turn_c, nxt2, ahead)],
            2: [done(project, 0), then(keys, nxt2, ahead), done(turn_back, 1)],
            3: [done(turn_att, 1), then(make_values, nxt, not (last or drain)), done(project, 1)],
        }[s] + [lambda: None]
        k = e.kind
        if s == 1 and ahead3:
            normalise(e, r.plus(3))
        if k == "dve":
            stages[0]()
        if not drain and not (last and s == UPR - 1):
            scores(e, *((r, s + 1) if s + 1 < UPR else (nxt, 0)))
        if k != "dve":
            stages[0]()
        if k == "act" and not drain:
            u.exponentials(e.eng, U, s % 2, KX)
        if k == "pe" and not drain:
            u.subtract_max(e.eng, U, s % 2, KX)
        if exists(1) and not (drain and s >= 1):
            if k == "pe":
                u.turn(e.eng, *at_unit(lag(r, s, 1)), KX)
            if k in ("act", "dve"):
                u.evacuate(e.eng, 0 if k == "act" else 1, *at_unit(lag(r, s, 1)), KX)
        stages[1]()
        if exists(2) and not (drain and s >= 2):
            rr, ss = lag(r, s, 2)
            if k == "pe":
                values(e, rr, ss)
            if k == "act" and s % 2 == 1:
                u.out_copy(e.eng, rr.lin(UPR, ss), rr.lin(UPR // 2, ss // 2), ss // 2 % 2, st.written("back"))
        stages[2]()
        if s == 2 and ahead3:
            apply_norm(e, r.plus(3))
        if s == 1 and ahead:
            first_part_q(e, nxt2)
            parts(e, nxt2)
        if s == 2 and ahead:
            make_zero(e, nxt2)

    def row(e, r, first, last):
        ahead = not (r.reg is None and r.off >= NB - 2)
        ahead3 = not (r.reg is None and r.off >= NB - 3)
        if e.kind == "sp":
            if ahead3:
                load(e, r.plus(3))
            if ahead:
                parts(e, r.plus(2))
            return
        if not first:
            e.free[0] = [(st.read("v"), r.lin(1, 1)), (st.read("proj"), r.lin(NT, -NT))]
        for s in range(UPR):
            slot(e, r, s, first, ahead, ahead3, last)

    def epilogue(e, r):
        if e.kind != "sp":
            for s in range(UPR):
                slot(e, r, s, False, False, False, True, drain=True)

    on_engines(nc, lambda e: rows_of(e, NB, prologue, row, epilogue))



GROUP = 16
SPARE = TOKENS + 1


def experts(p, ctx):
    nc = p.nc
    slot_row = p.sb("slot_row", [P, N_ST], I32, ctx)
    slot_share = p.sb("slot_share", [P, N_ST], ctx=ctx)
    tile_expert = p.sb("tile_expert", [1, N_ST], I32, ctx)
    xn_dram = nc.dram_tensor("xn_rows", [TOKENS + P, D], F32, kind="Internal").ap()
    sum_dram = nc.dram_tensor("sum_rows", [TOKENS + P, D], F32, kind="Internal").ap()
    with ExitStack() as c:
        route(p, c, xn_dram, sum_dram, slot_row, slot_share, tile_expert)
    with ExitStack() as c:
        expert_tiles(p, c, xn_dram, sum_dram, slot_row, slot_share, tile_expert)
    with nc.Block() as block:
        @block.sync
        def _(sp):
            out = p.a["out"].rearrange("b s d -> (b s) d").rearrange("(q n) d -> q (n d)", q=P)
            sums = sum_dram[0:TOKENS, :].rearrange("(q n) d -> q (n d)", q=P)
            sp.dma_start(out, sums).then_inc(p.sem("out"), 16)
            sp.wait_ge(p.sem("out"), 16)


def route(p, ctx, xn_dram, sum_dram, slot_row, slot_share, tile_expert):
    nc, a = p.nc, p.a
    sb = lambda n, s, dt=F32: p.sb(n, s, dt, ctx)
    sem = lambda n: p.sem("rt_" + n)
    xb = [sb(f"xb{i}", [P, NT, D]) for i in range(2)]
    nT = [sb(f"rnT{i}", [P, DT, S]) for i in range(2)]
    routerT = sb("routerT_sb", [P, DT, E])
    before = sb("before_sb", [P, P])
    ones = sb("ones", [P, P])
    zeros = sb("zeros", [P, D])
    iota_e = sb("iota_e_sb", [P, E])
    iota_t = sb("iota_t_sb", [P, N_ST])
    iota_p = sb("iota_p_sb", [P, P])
    token1 = sb("token1_sb", [P, TILES])
    spare = sb("spare_sb", [P, 1])
    stats = [sb(f"rstats{i}", [P, NT, 6]) for i in range(2)]
    mv = [sb(f"rmv{i}", [P, NT, 2]) for i in range(2)]
    rstd = [sb(f"rrstd{i}", [P, NT, 1]) for i in range(2)]
    t8 = lambda n, dt=F32: sb(n, [P, TILES, E], dt)
    prob, top, sel, posn, tmp = (t8(n) for n in ("prob", "top", "sel", "posn", "tmp"))
    hot = [t8("hot0"), t8("hot1")]
    scan = [t8("scan0"), t8("scan1")]
    top_id = t8("top_id", U32)
    tile1 = sb("tile1", [P, TILES, 1])
    idf = sb("idf", [P, TILES, TOP])
    share = sb("share", [P, TOP, TILES])
    slotf = sb("slotf", [P, TOP, TILES, 1])
    slot_i, part_i = (sb(n, [P, TOP, TILES], I32) for n in ("slot_i", "part_i"))
    slot_tile, slot_lane = (sb(n, [P, TOP, TILES]) for n in ("slot_tile", "slot_lane"))
    count_i = sb("count_i", [P, E], I32)
    tiles_i = sb("tiles_i", [P, E], I32)
    tiles_e, starts = sb("tiles_e", [P, E]), sb("starts", [P, E])
    cum = [sb("cum0", [P, E]), sb("cum1", [P, E])]
    passed = sb("passed", [1, N_ST, E])
    expert_f = sb("expert_f", [1, N_ST, 1])
    lane_hot = [sb(f"lane_hot{i}", [P, GROUP, P]) for i in range(2)]
    tile_hot = [sb(f"tile_hot{i}", [P, GROUP, N_ST]) for i in range(2)]
    entry = [sb(f"entry{i}", [P, GROUP, 2, N_ST]) for i in range(2)]
    empty = sb("empty", [P, N_ST])
    xn_t = xn_dram[0:TOKENS, :].rearrange("(t p) d -> p t d", p=P)
    sum_t = sum_dram[0:TOKENS, :].rearrange("(t p) d -> p t d", p=P)

    def walk(e):
        if e.kind == "sp":
            wide = lambda n: a[n].unsqueeze(0).broadcast_to((P, a[n].shape[0]))
            for dst, src in ((routerT[:], a["routerT"].rearrange("(k p) e -> p k e", p=P)),
                             (before[:], a["before"]), (iota_e[:], wide("iota_e")), (iota_t[:], wide("iota_t")),
                             (iota_p[:], wide("iota_p")), (token1[:], a["token1"]), (spare[:], a["spare"])):
                e.eng.dma_start(dst, src).then_inc(sem("const"), 16)
        if e.kind == "pool":
            e.eng.memset(zeros[:], 0.0).then_inc(sem("set"), 1)
            e.eng.memset(ones[:], 1.0).then_inc(sem("set"), 1)
        if e.kind in ("pe", "dve"):
            wait(e.eng, sem("const"), 7 * 16)
            wait(e.eng, sem("set"), 2)
        statistics(e, Row(None, 0))
        for n in range(FIRST):
            row(e, Row(None, n), first=n == 0)
        with e.eng.Fori(FIRST, NB - 2, 2) as r:
            row(e, Row(r, 0, FIRST % 2))
            row(e, Row(r, 1, 1 - FIRST % 2))
        row(e, Row(None, NB - 1), last=True)
        router(e, Row(None, NB - 1))
        assign(e)
        if e.kind == "sp":
            wait(e.eng, sem("set"), 2)
            e.eng.dma_start(sum_t, p.xres[:]).then_inc(sem("sums"), 16)
            e.eng.dma_start(sum_dram[TOKENS:, :], zeros[:]).then_inc(sem("sums"), 16)
            e.eng.dma_start(xn_dram[TOKENS:, :], zeros[:]).then_inc(sem("sums"), 16)
            for i in range(2):
                wait(e.eng, sem(f"stored{i}"), 16 * NB // 2)
            wait(e.eng, sem("sums"), 48)

    def statistics(e, r):
        i = r.par
        if e.kind == "dve":
            wait(e.eng, sem("norm"), r.lin(NT, -NT))
            for n in range(NT):
                e.eng.bn_stats(stats[i][:, n, :], p.xres[:, bass.ds(r.lin(NT, n), 1), :]).then_inc(sem("stats"), 1)
            wait(e.eng, sem("stats"), r.lin(NT, NT), apart=True)
            for n in range(NT):
                e.eng.bn_aggr(mv[i][:, n, :], stats[i][:, n, :]).then_inc(sem("mv"), 1)
        if e.kind == "pool":
            wait(e.eng, sem("mv"), r.lin(NT, NT))
            wait(e.eng, sem("norm"), r.lin(NT, -NT))
            e.eng.tensor_scalar(rstd[i][:], mv[i][:, :, 1:2], EPS, None, ALU.add).then_inc(sem("rstd"), 1)
            wait(e.eng, sem("rstd"), r.lin(2, 1))
            e.eng.tensor_tensor(rstd[i][:], rstd[i][:], p.eps[:, 0:1].unsqueeze(1).broadcast_to((P, NT, 1)),
                                ALU.pow).then_inc(sem("rstd"), 1)

    def row(e, r, first=False, last=False):
        i = r.par
        if not last:
            statistics(e, r.plus(1))
        if e.kind == "dve":
            wait(e.eng, sem("rstd"), r.lin(2, 2))
            wait(e.eng, sem("turn"), r.lin(1, -1))
            wait(e.eng, sem(f"stored{i}"), r.lin(8, -8 * i))
            for n in range(NT):
                e.eng.tensor_scalar(xb[i][:, n:n + 1, :], p.xres[:, bass.ds(r.lin(NT, n), 1), :], mv[i][:, n, 0:1],
                                    rstd[i][:, n, :], ALU.subtract, ALU.mult).then_inc(sem("norm"), 1)
        if e.kind == "sp":
            wait(e.eng, sem("norm"), r.lin(NT, NT))
            wait(e.eng, sem(f"stored{i}"), r.lin(8, -8 * i))
            e.eng.dma_start(xn_t[:, bass.ds(r.lin(NT), NT), :], xb[i][:]).then_inc(sem(f"stored{i}"), 16)
        if e.kind == "pe":
            wait(e.eng, sem("norm"), r.lin(NT, NT))
            wait(e.eng, sem("nT"), r.lin(1, -1))
            for k in range(DT):
                for n in range(NT):
                    mm = e.eng.transpose(p.T[i][:, k * NT + n, :], xb[i][:, n, k * P:(k + 1) * P], p.ident[:])
            mm.then_inc(sem("turn"), 1)
        if e.kind == "act":
            wait(e.eng, sem("turn"), r.lin(1, 1))
            wait(e.eng, sem("logits"), r.lin(1, -1))
            e.eng.copy(nT[i][:], p.T[i][:].rearrange("p (k n) t -> p k (n t)", k=DT)).then_inc(sem("nT"), 1)
        if not first:
            router(e, r.plus(-1))

    def router(e, r):
        i = r.par
        if e.kind == "pe":
            wait(e.eng, sem("nT"), r.lin(1, 1))
            out = p.O[:].rearrange("p a b -> p (a b)")
            for n in range(NT):
                for k in range(DT):
                    mm = e.eng.matmul(out[:, bass.ds(r.lin(NT * E, n * E), E)], nT[i][:, k, n * P:(n + 1) * P],
                                      routerT[:, k, :], start=(k == 0), stop=(k == DT - 1), skip_group_check=True)
            mm.then_inc(sem("logits"), 1)

    def assign(e):
        flat = lambda x: x[:].rearrange("p t e -> p (t e)")
        wide = lambda x: x.unsqueeze(1).broadcast_to((P, TILES, E))
        counts = lambda x: x[:, 0:TILES * E].rearrange("p (t e) -> p t e", e=E)
        bank = lambda x: x[:].rearrange("p a b -> p (a b)")
        v = e.eng
        steps = 0

        def step(ins):
            nonlocal steps
            steps += 1
            ins.then_inc(sem("step"), 1)
            wait(v, sem("step"), steps)

        if e.kind == "dve":
            wait(v, sem("logits"), NB)
            logits = counts(bank(p.O))
            step(v.tensor_reduce(tile1[:], logits, AX_X, ALU.max))
            step(v.tensor_tensor(tmp[:], logits, tile1[:].broadcast_to((P, TILES, E)), ALU.subtract))
        if e.kind == "act":
            wait(e.eng, sem("step"), 2)
            e.eng.activation(prob[:], tmp[:], ACT.Exp).then_inc(sem("exp"), 1)
        if e.kind == "dve":
            wait(v, sem("exp"), 1)
            step(v.tensor_reduce(tile1[:], prob[:], AX_X, ALU.add))
            step(v.reciprocal(tile1[:], tile1[:]))
            step(v.tensor_tensor(prob[:], prob[:], tile1[:].broadcast_to((P, TILES, E)), ALU.mult))
            for t in range(TILES):
                ins = v.max(top[:, t, :], prob[:, t, :])
            step(ins)
            for t in range(TILES):
                ins = v.max_index(top_id[:, t, :], top[:, t, :], prob[:, t, :])
            step(ins)
            step(v.tensor_tensor(tile1[:], top[:, :, 0:1], top[:, :, 1:2], ALU.add))
            step(v.reciprocal(tile1[:], tile1[:]))
            for j in range(TOP):
                step(v.tensor_tensor(share[:, j, :].unsqueeze(2), top[:, :, j:j + 1], tile1[:], ALU.mult))
            step(v.tensor_copy(idf[:], top_id[:, :, 0:TOP]))
            for j in range(TOP):
                step(v.tensor_tensor(hot[j][:], wide(iota_e[:]), idf[:, :, j:j + 1].broadcast_to((P, TILES, E)),
                                     ALU.is_equal))
            v.tensor_tensor(sel[:], hot[0][:], hot[1][:], ALU.add).then_inc(sem("sel"), 1)
        if e.kind == "pe":
            wait(e.eng, sem("sel"), 1)
            e.eng.matmul(p.M[:, 0:TILES * E], before[:], flat(sel), start=True, stop=True)
            e.eng.matmul(bank(p.T[0])[:, 0:TILES * E], ones[:], flat(sel), start=True,
                         stop=True).then_inc(sem("count"), 1)
        if e.kind == "dve":
            total, prefix = counts(bank(p.T[0])), counts(p.M)
            wait(v, sem("count"), 1)
            step(v.tensor_copy(scan[0][:], total))
            cur, d = 0, 1
            while d < TILES:
                step(v.tensor_copy(scan[1 - cur][:, 0:d, :], scan[cur][:, 0:d, :]))
                step(v.tensor_tensor(scan[1 - cur][:, d:, :], scan[cur][:, d:, :], scan[cur][:, 0:TILES - d, :],
                                     ALU.add))
                cur, d = 1 - cur, 2 * d
            step(v.tensor_scalar(count_i[:], scan[cur][:, TILES - 1, :], float(P - 1), None, ALU.add))
            step(v.tensor_scalar(tiles_i[:], count_i[:], P.bit_length() - 1, None, ALU.logical_shift_right))
            step(v.tensor_copy(tiles_e[:], tiles_i[:]))
            step(v.tensor_copy(cum[0][:], tiles_e[:]))
            c, d = 0, 1
            while d < E:
                step(v.tensor_copy(cum[1 - c][:, 0:d], cum[c][:, 0:d]))
                step(v.tensor_tensor(cum[1 - c][:, d:], cum[c][:, d:], cum[c][:, 0:E - d], ALU.add))
                c, d = 1 - c, 2 * d
            step(v.tensor_tensor(starts[:], cum[c][:], tiles_e[:], ALU.subtract))
            step(v.tensor_scalar(starts[:], starts[:], float(P), None, ALU.mult))
            step(v.tensor_tensor(posn[:], scan[cur][:], total, ALU.subtract))
            step(v.tensor_tensor(posn[:], posn[:], prefix, ALU.add))
            step(v.tensor_tensor(posn[:], posn[:], wide(starts[:]), ALU.add))
            for j in range(TOP):
                step(v.tensor_tensor(tmp[:], posn[:], hot[j][:], ALU.mult))
                step(v.tensor_reduce(slotf[:, j, :, :], tmp[:], AX_X, ALU.add))
            step(v.tensor_copy(slot_i[:], slotf[:].rearrange("p j t o -> p j (t o)")))
            step(v.tensor_scalar(part_i[:], slot_i[:], P.bit_length() - 1, None, ALU.logical_shift_right))
            step(v.tensor_copy(slot_tile[:], part_i[:]))
            step(v.scalar_tensor_tensor(slot_lane[:], slot_tile[:], -float(P), slotf[:].rearrange("p j t o -> p j (t o)"),
                                        ALU.mult, ALU.add))
        flat2 = lambda x: x[:].rearrange("p j t -> p (j t)")
        tokens_ps = bank(p.T[1])[:, 0:2 * N_ST]
        n_groups = TOP * TILES // GROUP
        for g in range(n_groups):
            b, c0 = g % 2, g * GROUP
            t0 = c0 % TILES
            spread = lambda x, c, n: x[:, c:c + GROUP].unsqueeze(2).broadcast_to((P, GROUP, n))
            same = lambda x, n: x[:].unsqueeze(1).broadcast_to((P, GROUP, n))
            if e.kind == "dve":
                wait(v, sem("placed"), g - 1)
                wait(v, sem("shares"), g - 1)
                v.tensor_tensor(tile_hot[b][:], same(iota_t, N_ST), spread(flat2(slot_tile), c0, N_ST),
                                ALU.is_equal).then_inc(sem("hot"), 1)
                v.tensor_tensor(lane_hot[b][:], same(iota_p, P), spread(flat2(slot_lane), c0, P), ALU.is_equal)\
                    .then_inc(sem("hot"), 1)
                wait(v, sem("hot"), 3 * g + 2)
                v.tensor_tensor(entry[b][:, :, 0, :], tile_hot[b][:], spread(token1, t0, N_ST), ALU.mult)\
                    .then_inc(sem("hot"), 1)
            if e.kind == "pool":
                wait(v, sem("placed"), g - 1)
                wait(v, sem("hot"), 3 * g + 1)
                v.tensor_tensor(entry[b][:, :, 1, :], tile_hot[b][:], spread(flat2(share), c0, N_ST), ALU.mult)\
                    .then_inc(sem("shares"), 1)
            if e.kind == "pe":
                wait(e.eng, sem("hot"), 3 * g + 3)
                wait(e.eng, sem("shares"), g + 1)
                for c in range(GROUP):
                    mm = e.eng.matmul(tokens_ps, lane_hot[b][:, c, :], entry[b][:, c, :, :],
                                      start=(g == 0 and c == 0), stop=(g == n_groups - 1 and c == GROUP - 1))
                mm.then_inc(sem("placed"), 1)
        if e.kind == "dve":
            step(v.tensor_tensor(passed[:], iota_t[0:1, :].unsqueeze(2).broadcast_to((1, N_ST, E)),
                                 cum[c][0:1, :].unsqueeze(1).broadcast_to((1, N_ST, E)), ALU.is_ge))
            step(v.tensor_reduce(expert_f[:], passed[:], AX_X, ALU.add))
            step(v.tensor_scalar(tile_expert[:].unsqueeze(2), expert_f[:], float(E - 1), None, ALU.min))
            wait(v, sem("placed"), n_groups)
            numbers = tokens_ps[:, 0:N_ST]
            step(v.tensor_copy(slot_share[:], tokens_ps[:, N_ST:2 * N_ST]))
            step(v.tensor_scalar(empty[:], numbers, 0.0, None, ALU.is_equal))
            step(v.scalar_tensor_tensor(empty[:], empty[:], spare[:, 0:1], numbers, ALU.mult, ALU.add))
            step(v.tensor_scalar(slot_row[:], empty[:], -1.0, None, ALU.add))

    on_engines(nc, walk)




def expert_tiles(p, ctx, xn_dram, sum_dram, slot_row, slot_share, tile_expert):
    nc = p.nc
    sb = lambda n, s, dt=F32: p.sb(n, s, dt, ctx)
    sem = lambda n: p.sem("et_" + n)
    xg = [sb(f"xg{i}", [P, D]) for i in range(2)]
    xgT = [sb(f"xgT{i}", [P, DT, P]) for i in range(2)]
    silu = [sb(f"silu{i}", [P, HID]) for i in range(2)]
    gate = [sb(f"gate{i}", [P, HID]) for i in range(2)]
    gT = [sb(f"ggT{i}", [P, HT, P]) for i in range(2)]
    y = [sb(f"y{i}", [P, D]) for i in range(2)]
    h_ps = [p.S[i][:].rearrange("p (w a) b -> p w (a b)", w=2) for i in range(2)]
    x_ps, g_ps = p.T[0], p.T[1]
    y_ps = p.O[:].rearrange("p a b -> p (a b)")[:, 0:D]
    from_row = [sb(f"from_row{i}", [P, 1], I32) for i in range(2)]
    to_row = [sb(f"to_row{i}", [P, 1], I32) for i in range(2)]
    share = [sb(f"tile_share{i}", [P, 1]) for i in range(2)]

    def load(e, r):
        i = r.par
        if e.kind == "pool":
            wait(e.eng, sem("x_in"), r.lin(16))
            e.eng.tensor_copy(from_row[i][:], slot_row[:, bass.ds(r.lin(1), 1)]).then_inc(sem("from"), 1)
            wait(e.eng, sem("from"), r.lin(1, 1))
            wait(e.eng, sem("x_turn"), r.lin(1, -1))
            e.eng.indirect_dma_start(xg[i][:], None, xn_dram, bass.IndirectOffsetOnAxis(ap=from_row[i][:], axis=0))\
                .then_inc(sem("x_in"), 16)

    def turn_x(e, r):
        if e.kind == "pe":
            wait(e.eng, sem("x_in"), r.lin(16, 16))
            wait(e.eng, sem("xT"), r.lin(1))
            for k in range(DT):
                mm = e.eng.transpose(x_ps[:, k, :], xg[r.par][:, k * P:(k + 1) * P], p.ident[:])
            mm.then_inc(sem("x_turn"), 1)
        if e.kind == "act":
            wait(e.eng, sem("x_turn"), r.lin(1, 1))
            wait(e.eng, sem("h"), r.lin(1, -1))
            e.eng.copy(xgT[r.par][:], x_ps[:, 0:DT, :]).then_inc(sem("xT"), 1)

    def expert_of(e, r):
        return e.eng.value_load(tile_expert[0:1, bass.ds(r.lin(1), 1)], min_val=0, max_val=E - 1)

    def hidden(e, r):
        i = r.par
        if e.kind == "pe":
            expert = expert_of(e, r)
            wait(e.eng, sem("xT"), r.lin(1, 1))
            wait(e.eng, sem("gate"), r.lin(1, -1))
            for j, w in enumerate((p.w1s, p.w3s)):
                for k in range(DT):
                    mm = e.eng.matmul(h_ps[i][:, j:j + 1, :], xgT[i][:, k, :], w[:, bass.ds(expert * DT + k, 1), :],
                                      start=(k == 0), stop=(k == DT - 1))
            mm.then_inc(sem("h"), 1)
        if e.kind == "act":
            wait(e.eng, sem("h"), r.lin(1, 1))
            wait(e.eng, sem("gate"), r.lin(1, -1))
            e.eng.activation(silu[i][:], h_ps[i][:, 0, :], ACT.Silu).then_inc(sem("silu"), 1)
        if e.kind == "dve":
            wait(e.eng, sem("silu"), r.lin(1, 1))
            wait(e.eng, sem("g_turn"), r.lin(1, -1))
            e.eng.tensor_tensor(gate[i][:], h_ps[i][:, 1, :], silu[i][:], ALU.mult).then_inc(sem("gate"), 1)

    def turn_gate(e, r):
        i = r.par
        if e.kind == "pe":
            wait(e.eng, sem("gate"), r.lin(1, 1))
            wait(e.eng, sem("gT"), r.lin(1))
            for k in range(HT):
                mm = e.eng.transpose(g_ps[:, k, :], gate[i][:, k * P:(k + 1) * P], p.ident[:])
            mm.then_inc(sem("g_turn"), 1)
        if e.kind == "act":
            wait(e.eng, sem("g_turn"), r.lin(1, 1))
            wait(e.eng, sem("y"), r.lin(1, -1))
            e.eng.copy(gT[i][:], g_ps[:]).then_inc(sem("gT"), 1)

    def outputs(e, r):
        i = r.par
        if e.kind == "pe":
            expert = expert_of(e, r)
            wait(e.eng, sem("gT"), r.lin(1, 1))
            wait(e.eng, sem("y_sb"), r.lin(1))
            for k in range(HT):
                mm = e.eng.matmul(y_ps.unsqueeze(1), gT[i][:, k, :], p.w2s[:, bass.ds(expert * HT + k, 1), :],
                                  start=(k == 0), stop=(k == HT - 1))
            mm.then_inc(sem("y"), 1)
        if e.kind == "pool":
            wait(e.eng, sem("y_out"), r.lin(16, -16))
            wait(e.eng, sem("y_sb"), r.lin(1, -1))
            e.eng.tensor_copy(to_row[i][:], slot_row[:, bass.ds(r.lin(1), 1)]).then_inc(sem("to"), 1)
            e.eng.tensor_copy(share[i][:], slot_share[:, bass.ds(r.lin(1), 1)]).then_inc(sem("share"), 1)
            wait(e.eng, sem("to"), r.lin(1, 1))
            wait(e.eng, sem("y_sb"), r.lin(1, 1))
            wait(e.eng, sem("y_out"), r.lin(16))
            e.eng.indirect_dma_start(sum_dram, bass.IndirectOffsetOnAxis(ap=to_row[i][:], axis=0), y[i][:], None,
                                     compute_op=ALU.add).then_inc(sem("y_out"), 16)
        if e.kind == "dve":
            wait(e.eng, sem("y"), r.lin(1, 1))
            wait(e.eng, sem("share"), r.lin(1, 1))
            wait(e.eng, sem("y_out"), r.lin(16, -16))
            e.eng.tensor_scalar(y[i][:], y_ps, share[i][:], None, ALU.mult).then_inc(sem("y_sb"), 1)

    def tile(e, r):
        n = r.off if r.reg is None else None
        has = lambda d: n is None or 0 <= n + d < N_ST
        if has(2):
            load(e, r.plus(2))
        if has(0):
            hidden(e, r)
        if has(-1):
            turn_gate(e, r.plus(-1))
        if has(1):
            turn_x(e, r.plus(1))
        if has(-2):
            outputs(e, r.plus(-2))

    def walk(e):
        load(e, Row(None, 0))
        load(e, Row(None, 1))
        turn_x(e, Row(None, 0))
        for n in range(4):
            tile(e, Row(None, n))
        end = N_ST - 2 - N_ST % 2
        with e.eng.Fori(4, end - 1, 2) as r:
            tile(e, Row(r, 0, 0))
            tile(e, Row(r, 1, 1))
        for n in range(end, N_ST + 2):
            tile(e, Row(None, n))
        if e.kind == "pool":
            wait(e.eng, sem("y_out"), 16 * N_ST)

    on_engines(nc, walk)


def layout(x, ctx_1024, mask_Bx1xSxS2_ik1, L0_attn_pos_emb, L0_attn_global_memory, L0_attn_conv_w,
           L0_attn_conv_b, L0_attn_gate_w, L0_attn_gate_b, L0_attn_out_w, L0_attn_out_b,
           L0_xattn_Wq, L0_xattn_Wk, L0_xattn_Wv, L0_xattn_Wo, L0_ffn_router_w, L0_ffn_w1,
           L0_ffn_w2, L0_ffn_w3):
    c = np.ascontiguousarray
    return {
        "x": c(x), "ctx": c(ctx_1024), "mask": c(np.reshape(mask_Bx1xSxS2_ik1, (NB, S, KX))),
        "pos_emb": c(L0_attn_pos_emb), "global_memory": c(L0_attn_global_memory),
        "conv_w": c(np.transpose(L0_attn_conv_w, (1, 2, 0))), "conv_b": c(L0_attn_conv_b),
        "gate_w": c(L0_attn_gate_w), "gate_b": c(L0_attn_gate_b),
        "out_w": c(L0_attn_out_w), "out_b": c(L0_attn_out_b),
        "WqT": c(np.transpose(L0_xattn_Wq)), "WkT": c(np.transpose(L0_xattn_Wk)),
        "WvT": c(np.transpose(L0_xattn_Wv)), "WoT": c(np.transpose(L0_xattn_Wo)),
        "routerT": c(np.transpose(L0_ffn_router_w)),
        "w1T": c(np.transpose(L0_ffn_w1, (0, 2, 1))), "w3T": c(np.transpose(L0_ffn_w3, (0, 2, 1))),
        "w2T": c(np.transpose(L0_ffn_w2, (0, 2, 1))),
        "ident": np.eye(P, dtype=np.float32), "before": np.triu(np.ones((P, P), np.float32), 1),
        "iota_e": np.arange(E, dtype=np.float32), "iota_t": np.arange(N_ST, dtype=np.float32),
        "iota_p": np.arange(P, dtype=np.float32), "spare": np.arange(P, dtype=np.float32)[:, None] + SPARE,
        "token1": np.ascontiguousarray(np.arange(1, TOKENS + 1, dtype=np.float32).reshape(TILES, P).T),
    }


def kernel(**inputs):
    import concourse.bacc as bacc
    from concourse.bass_utils import run_bass_kernel_spmd

    nc = bacc.Bacc("TRN2", target_bir_lowering=False, num_devices=1)
    arrays = {f"in_{name}": array for name, array in layout(**inputs).items()}
    aps = {name[3:]: nc.dram_tensor(name, array.shape, mybir.dt.from_np(array.dtype), kind="ExternalInput").ap()
           for name, array in arrays.items()}
    aps["out"] = nc.dram_tensor("out", (NB, S, D), F32, kind="ExternalOutput").ap()
    build(nc, aps)
    return run_bass_kernel_spmd(nc, [arrays], core_ids=[0]).results[0]["out"]
```
